# Optimizing a Trainium2 kernel written in Bass

```python
import numpy as np
import jax
import jax.numpy as jnp

def _softmax(x, axis=-1):
    return jax.nn.softmax(x, axis=axis)

def _gelu(x):
    return jax.nn.gelu(x, approximate=True)

def _silu(x):
    return jax.nn.silu(x)

def _sigmoid(x):
    return jax.nn.sigmoid(x)

def _layernorm(x, axis=-1, eps=1e-05):
    m = jnp.mean(x, axis=axis, keepdims=True)
    v = jnp.var(x, axis=axis, keepdims=True)
    return (x - m) / jnp.sqrt(v + eps)

def _scatter_add(tgt, idx, src, axis=0):
    return tgt.at[idx].add(src)

def _segment_sum(src, seg, n):
    return jax.ops.segment_sum(src, seg, n)
kernel_name = 'mk_gnn_resnorm_d4_gnn_r8_b9cd20'

def setup_inputs(seed: int=0):
    np.random.seed(seed)
    _w = jnp.asarray

    def _rec_inputs():
        import jax
        import jax.numpy as jnp
        _gk = jax.random.key(seed)
        x = -0.0001006 + 1 * jax.random.normal(jax.random.fold_in(_gk, 1), (6250, 96), jnp.float32)
        _s = jax.random.randint(jax.random.fold_in(_gk, 2), (50000,), 0, 6250, jnp.int32)
        _d = jax.random.randint(jax.random.fold_in(_gk, 3), (50000,), 0, 6250, jnp.int32)
        _loop = jnp.arange(6250, dtype=jnp.int32)
        src = jnp.concatenate([_s, _d, _loop])
        dst = jnp.concatenate([_d, _s, _loop])
        _o = jnp.argsort(dst, stable=True)
        src = src[_o]
        dst = dst[_o]
        edge_attr_4 = 0.000714719 + 1.00021 * jax.random.normal(jax.random.fold_in(_gk, 12), (106250, 4), jnp.float32)
        edge_weight = jax.random.uniform(jax.random.fold_in(_gk, 14), (106250,), jnp.float32, 0.0, 1)
        return (x, src, dst, edge_attr_4, edge_weight)
    x, src, dst, edge_attr_4, edge_weight = _rec_inputs()

    def _L0_gnn_setup():
        import jax, jax.numpy as jnp
        import numpy as np
        N_NODES = 6250
        N_EDGES = 100000
        IN_DIM = 96
        HID = 96

        def _gcn_conv(x, src, dst, norm, W, b, n_nodes):
            xw = x @ W
            msg = xw[src] * norm[:, None]
            agg = jax.ops.segment_sum(msg, dst, num_segments=n_nodes)
            return agg + b
        key = jax.random.key(seed)
        k1, k2, k3, k4 = jax.random.split(key, 4)
        x = jax.random.normal(k1, (N_NODES, IN_DIM), dtype=jnp.float32)
        edge_index = jax.random.randint(k2, (2, N_EDGES), 0, N_NODES, dtype=jnp.int64)
        s1 = 1.0 / np.sqrt(IN_DIM)
        s2 = 1.0 / np.sqrt(HID)
        W1 = jax.random.normal(k3, (IN_DIM, HID), dtype=jnp.float32) * s1
        b1 = jnp.zeros((HID,), dtype=jnp.float32)
        W2 = jax.random.normal(k4, (HID, HID), dtype=jnp.float32) * s2
        b2 = jnp.zeros((HID,), dtype=jnp.float32)
        return {'x': x, 'edge_index': edge_index, 'W1': W1, 'b1': b1, 'W2': W2, 'b2': b2}
    _L0_gnn_all = _L0_gnn_setup()
    _L0_gnn_in = {k: v for k, v in _L0_gnn_all.items() if k in ('W1', 'b1', 'W2', 'b2')}
    del _L0_gnn_all

    def _L1_gnn_setup():
        import jax, jax.numpy as jnp
        import numpy as np
        N = 6250
        E = 100000
        D = 96

        def _mean_aggr(h, src, dst, num_nodes):
            msgs = h[src]
            summed = jax.ops.segment_sum(msgs, dst, num_segments=num_nodes)
            deg = jax.ops.segment_sum(jnp.ones((src.shape[0],), h.dtype), dst, num_segments=num_nodes)
            return summed / jnp.maximum(deg, 1.0)[:, None]

        def _sage_conv(h, src, dst, Wl, bl, Wr, num_nodes):
            agg = _mean_aggr(h, src, dst, num_nodes)
            return agg @ Wl.T + bl + h @ Wr.T
        key = jax.random.key(seed)
        ks = jax.random.split(key, 8)
        s = 1.0 / np.sqrt(D)
        return {'x': jax.random.normal(ks[0], (N, D), dtype=jnp.float32), 'edge_index': jax.random.randint(ks[1], (2, E), 0, N, dtype=jnp.int64), 'Wl1': jax.random.normal(ks[2], (D, D), dtype=jnp.float32) * s, 'bl1': jnp.zeros((D,), dtype=jnp.float32), 'Wr1': jax.random.normal(ks[3], (D, D), dtype=jnp.float32) * s, 'Wl2': jax.random.normal(ks[4], (D, D), dtype=jnp.float32) * s, 'bl2': jnp.zeros((D,), dtype=jnp.float32), 'Wr2': jax.random.normal(ks[5], (D, D), dtype=jnp.float32) * s}
    _L1_gnn_all = _L1_gnn_setup()
    _L1_gnn_in = {k: v for k, v in _L1_gnn_all.items() if k in ('Wl1', 'bl1', 'Wr1', 'Wl2', 'bl2', 'Wr2')}
    del _L1_gnn_all

    def _L2_gnn_setup():
        import jax, jax.numpy as jnp
        import numpy as np
        N_NODES = 6250
        N_EDGES = 100000
        D_FEAT = 96
        D_OUT = 96
        key = jax.random.key(seed)
        ks = jax.random.split(key, 6)
        feat = jax.random.normal(ks[0], (N_NODES, D_FEAT), dtype=jnp.float32)
        affine = jax.random.uniform(ks[1], (N_EDGES,), dtype=jnp.float32)
        mlp_w = jax.random.normal(ks[2], (D_OUT, 2 * D_FEAT), dtype=jnp.float32) * (1.0 / np.sqrt(2 * D_FEAT))
        mlp_b = jax.random.normal(ks[3], (D_OUT,), dtype=jnp.float32) * 0.01
        src_idx = jax.random.randint(ks[4], (N_EDGES,), 0, N_NODES, dtype=jnp.int64)
        dst_idx = jax.random.randint(ks[5], (N_EDGES,), 0, N_NODES, dtype=jnp.int64)
        return {'feat': feat, 'affine': affine, 'mlp_w': mlp_w, 'mlp_b': mlp_b, 'src_idx': src_idx, 'dst_idx': dst_idx}
    _L2_gnn_all = _L2_gnn_setup()
    _L2_gnn_in = {k: v for k, v in _L2_gnn_all.items() if k in ('mlp_w', 'mlp_b')}
    del _L2_gnn_all

    def _L3_gnn_setup():
        import jax, jax.numpy as jnp
        import numpy as np
        EPS = 1e-05

        def _mlp(h, W, b, gamma, beta):
            h = jax.nn.relu(h @ W + b)
            mu = jnp.mean(h, axis=0)
            var = jnp.mean(jnp.square(h - mu), axis=0)
            return gamma * (h - mu) * jax.lax.rsqrt(var + EPS) + beta
        key = jax.random.key(seed)
        ks = jax.random.split(key, 10)
        N, E, C_in, C_out, E_dim = (6250, 100000, 96, 96, 4)
        x = jax.random.normal(ks[0], (N, C_in), dtype=jnp.float32)
        edge_index = jax.random.randint(ks[1], (2, E), 0, N, dtype=jnp.int64)
        edge_attr = jax.random.normal(ks[2], (E, E_dim), dtype=jnp.float32)
        s = lambda fan_in: 1.0 / np.sqrt(fan_in)
        W_node = jax.random.uniform(ks[3], (C_in, C_out), jnp.float32, -s(C_in), s(C_in))
        b_node = jnp.zeros((C_out,), jnp.float32)
        g_node = jnp.ones((C_out,), jnp.float32)
        beta_node = jnp.zeros((C_out,), jnp.float32)
        W_edge = jax.random.uniform(ks[4], (E_dim, C_out), jnp.float32, -s(E_dim), s(E_dim))
        b_edge = jnp.zeros((C_out,), jnp.float32)
        g_edge = jnp.ones((C_out,), jnp.float32)
        beta_edge = jnp.zeros((C_out,), jnp.float32)
        M_in = 2 * C_in + C_out
        W_msg = jax.random.uniform(ks[5], (M_in, C_out), jnp.float32, -s(M_in), s(M_in))
        b_msg = jnp.zeros((C_out,), jnp.float32)
        g_msg = jnp.ones((C_out,), jnp.float32)
        beta_msg = jnp.zeros((C_out,), jnp.float32)
        return dict(x=x, edge_index=edge_index, edge_attr=edge_attr, W_node=W_node, b_node=b_node, g_node=g_node, beta_node=beta_node, W_edge=W_edge, b_edge=b_edge, g_edge=g_edge, beta_edge=beta_edge, W_msg=W_msg, b_msg=b_msg, g_msg=g_msg, beta_msg=beta_msg)
    _L3_gnn_all = _L3_gnn_setup()
    _L3_gnn_in = {k: v for k, v in _L3_gnn_all.items() if k in ('W_node', 'b_node', 'g_node', 'beta_node', 'W_edge', 'b_edge', 'g_edge', 'beta_edge', 'W_msg', 'b_msg', 'g_msg', 'beta_msg')}
    del _L3_gnn_all
    return {'x': x, 'src': src, 'dst': dst, 'edge_attr_4': edge_attr_4, 'edge_weight': edge_weight, 'L0_gnn_W1': _L0_gnn_in['W1'], 'L0_gnn_b1': _L0_gnn_in['b1'], 'L0_gnn_W2': _L0_gnn_in['W2'], 'L0_gnn_b2': _L0_gnn_in['b2'], 'L1_gnn_Wl1': _L1_gnn_in['Wl1'], 'L1_gnn_bl1': _L1_gnn_in['bl1'], 'L1_gnn_Wr1': _L1_gnn_in['Wr1'], 'L1_gnn_Wl2': _L1_gnn_in['Wl2'], 'L1_gnn_bl2': _L1_gnn_in['bl2'], 'L1_gnn_Wr2': _L1_gnn_in['Wr2'], 'L2_gnn_mlp_w': _L2_gnn_in['mlp_w'], 'L2_gnn_mlp_b': _L2_gnn_in['mlp_b'], 'L3_gnn_W_node': _L3_gnn_in['W_node'], 'L3_gnn_b_node': _L3_gnn_in['b_node'], 'L3_gnn_g_node': _L3_gnn_in['g_node'], 'L3_gnn_beta_node': _L3_gnn_in['beta_node'], 'L3_gnn_W_edge': _L3_gnn_in['W_edge'], 'L3_gnn_b_edge': _L3_gnn_in['b_edge'], 'L3_gnn_g_edge': _L3_gnn_in['g_edge'], 'L3_gnn_beta_edge': _L3_gnn_in['beta_edge'], 'L3_gnn_W_msg': _L3_gnn_in['W_msg'], 'L3_gnn_b_msg': _L3_gnn_in['b_msg'], 'L3_gnn_g_msg': _L3_gnn_in['g_msg'], 'L3_gnn_beta_msg': _L3_gnn_in['beta_msg']}

def reference(x, src, dst, edge_attr_4, edge_weight, L0_gnn_W1, L0_gnn_b1, L0_gnn_W2, L0_gnn_b2, L1_gnn_Wl1, L1_gnn_bl1, L1_gnn_Wr1, L1_gnn_Wl2, L1_gnn_bl2, L1_gnn_Wr2, L2_gnn_mlp_w, L2_gnn_mlp_b, L3_gnn_W_node, L3_gnn_b_node, L3_gnn_g_node, L3_gnn_beta_node, L3_gnn_W_edge, L3_gnn_b_edge, L3_gnn_g_edge, L3_gnn_beta_edge, L3_gnn_W_msg, L3_gnn_b_msg, L3_gnn_g_msg, L3_gnn_beta_msg):
    import jax
    import jax.numpy as jnp

    def _L0_gnn_ref(x, edge_index, W1, b1, W2, b2):
        import jax, jax.numpy as jnp
        import numpy as np
        N_NODES = 6250
        N_EDGES = 100000
        IN_DIM = 96
        HID = 96

        def _gcn_conv(x, src, dst, norm, W, b, n_nodes):
            xw = x @ W
            msg = xw[src] * norm[:, None]
            agg = jax.ops.segment_sum(msg, dst, num_segments=n_nodes)
            return agg + b
        n_nodes = x.shape[0]
        loops = jnp.arange(n_nodes, dtype=edge_index.dtype)
        src = jnp.concatenate([edge_index[0], loops])
        dst = jnp.concatenate([edge_index[1], loops])
        deg = jax.ops.segment_sum(jnp.ones(dst.shape, dtype=x.dtype), dst, num_segments=n_nodes)
        dinv = jnp.where(deg > 0, jax.lax.rsqrt(deg), 0.0)
        norm = dinv[src] * dinv[dst]
        h = jax.nn.relu(_gcn_conv(x, src, dst, norm, W1, b1, n_nodes))
        h = jax.nn.relu(_gcn_conv(h, src, dst, norm, W2, b2, n_nodes))
        return h

    def _L1_gnn_ref(x, edge_index, Wl1, bl1, Wr1, Wl2, bl2, Wr2):
        import jax, jax.numpy as jnp
        import numpy as np
        N = 6250
        E = 100000
        D = 96

        def _mean_aggr(h, src, dst, num_nodes):
            msgs = h[src]
            summed = jax.ops.segment_sum(msgs, dst, num_segments=num_nodes)
            deg = jax.ops.segment_sum(jnp.ones((src.shape[0],), h.dtype), dst, num_segments=num_nodes)
            return summed / jnp.maximum(deg, 1.0)[:, None]

        def _sage_conv(h, src, dst, Wl, bl, Wr, num_nodes):
            agg = _mean_aggr(h, src, dst, num_nodes)
            return agg @ Wl.T + bl + h @ Wr.T
        src, dst = (edge_index[0], edge_index[1])
        n = x.shape[0]
        h = _sage_conv(x, src, dst, Wl1, bl1, Wr1, n)
        h = jax.nn.relu(h)
        h = _sage_conv(h, src, dst, Wl2, bl2, Wr2, n)
        return h

    def _L2_gnn_ref(feat, affine, mlp_w, mlp_b, src_idx, dst_idx):
        import jax, jax.numpy as jnp
        import numpy as np
        N_NODES = 6250
        N_EDGES = 100000
        D_FEAT = 96
        D_OUT = 96
        msgs = feat[src_idx] * affine[:, None]
        agg = jax.ops.segment_sum(msgs, dst_idx, num_segments=feat.shape[0])
        gcn_feat = jnp.concatenate([feat, agg], axis=-1)
        out = gcn_feat @ mlp_w.T + mlp_b
        return out

    def _L3_gnn_ref(x, edge_index, edge_attr, W_node, b_node, g_node, beta_node, W_edge, b_edge, g_edge, beta_edge, W_msg, b_msg, g_msg, beta_msg):
        import jax, jax.numpy as jnp
        import numpy as np
        EPS = 1e-05

        def _mlp(h, W, b, gamma, beta):
            h = jax.nn.relu(h @ W + b)
            mu = jnp.mean(h, axis=0)
            var = jnp.mean(jnp.square(h - mu), axis=0)
            return gamma * (h - mu) * jax.lax.rsqrt(var + EPS) + beta
        node_feat = _mlp(x, W_node, b_node, g_node, beta_node)
        edge_feat = _mlp(edge_attr, W_edge, b_edge, g_edge, beta_edge)
        row, col = (edge_index[0], edge_index[1])
        message = jnp.concatenate([x[row], x[col], edge_feat], axis=1)
        message = _mlp(message, W_msg, b_msg, g_msg, beta_msg)
        agg = jax.ops.segment_sum(message, col, num_segments=node_feat.shape[0])
        return agg + node_feat
    edge_index = jnp.stack([src, dst])
    x = _layernorm(x + _L0_gnn_ref(x, edge_index, L0_gnn_W1, L0_gnn_b1, L0_gnn_W2, L0_gnn_b2), axis=-1)
    x = _layernorm(x + _L1_gnn_ref(x, edge_index, L1_gnn_Wl1, L1_gnn_bl1, L1_gnn_Wr1, L1_gnn_Wl2, L1_gnn_bl2, L1_gnn_Wr2), axis=-1)
    x = _layernorm(x + _L2_gnn_ref(x, edge_weight, L2_gnn_mlp_w, L2_gnn_mlp_b, src, dst), axis=-1)
    x = _layernorm(x + _L3_gnn_ref(x, edge_index, edge_attr_4, L3_gnn_W_node, L3_gnn_b_node, L3_gnn_g_node, L3_gnn_beta_node, L3_gnn_W_edge, L3_gnn_b_edge, L3_gnn_g_edge, L3_gnn_beta_edge, L3_gnn_W_msg, L3_gnn_b_msg, L3_gnn_g_msg, L3_gnn_beta_msg), axis=-1)
    return x

_drawn_inputs = setup_inputs


def setup_inputs(seed=0):
    import zlib

    import numpy as np

    out = dict(_drawn_inputs(seed))
    spreads = {'L0_gnn_b1': (0.0, 0.1),
     'L0_gnn_b2': (0.0, 0.1),
     'L1_gnn_bl1': (0.0, 0.1),
     'L1_gnn_bl2': (0.0, 0.1),
     'L3_gnn_b_node': (0.0, 0.309),
     'L3_gnn_g_node': (1.0, 0.6),
     'L3_gnn_beta_node': (0.0, 0.632),
     'L3_gnn_b_edge': (0.0, 0.1),
     'L3_gnn_g_edge': (1.0, 0.2),
     'L3_gnn_beta_edge': (0.0, 0.271),
     'L3_gnn_b_msg': (0.0, 0.1),
     'L3_gnn_g_msg': (1.0, 0.2),
     'L3_gnn_beta_msg': (0.0, 0.1)}
    factors = {'L2_gnn_mlp_b': 31.099}
    for name, (base, spread) in spreads.items():
        noise = np.random.default_rng([zlib.crc32(name.encode()), seed]).standard_normal(out[name].shape)
        drawn = base * np.exp(spread * noise) if base else spread * noise
        out[name] = jnp.asarray(drawn.astype(out[name].dtype))
    for name, factor in factors.items():
        out[name] = (out[name] * factor).astype(out[name].dtype)
    return out
```

```python
import concourse.bass as bass
from concourse import mybir
from contextlib import ExitStack


def build(nc, x, src, dst, ea, ew, mats_dram, rows_dram, bias_rows, cols, w_edge, out, N, E, F, FE):
    mats = list(mats_dram)
    fp32, bf16, i32 = mybir.dt.float32, mybir.dt.bfloat16, mybir.dt.int32
    ALU, ACT, AX = mybir.AluOpType, mybir.ActivationFunctionType, mybir.AxisListType
    P, U = 128, 8
    GE = P * U
    NG = -(-E // GE)
    NG += NG % 2
    FULL = E // GE
    REST = E - FULL * GE
    NPAD_E = NG * GE - E
    NB = -(-N // P)
    CB = 7
    assert NB % CB == 0 and F % 32 == 0 and F < P
    NCH = NB // CB
    CW = CB * P
    NP = NB * P
    AW = NP + P
    MAXK = -(-N // P) + 1
    EPS = 1e-5
    FAR = 1.0e6

    ctx = ExitStack()
    with ctx:
        def sb(name, shape, dt=fp32):
            return ctx.enter_context(nc.sbuf_tensor(name, shape, dt))

        def pb(name, shape, dt=fp32):
            return ctx.enter_context(nc.psum_tensor(name, shape, dt))

        def sem(name):
            return ctx.enter_context(nc.semaphore(name))

        table = nc.dram_tensor("table", (NP, F), fp32, kind="Internal").ap()
        qtable = nc.dram_tensor("qtable", (AW, F), fp32, kind="Internal").ap()
        degrow = nc.dram_tensor("degrow", (1, NP), fp32, kind="Internal").ap()

        idx_all = sb("idx_all", [P, NG, U], i32)
        dstrel = sb("dstrel", [P, NG, U])
        w_all = sb("w_all", [P, NG, U])
        ea_all = sb("ea_all", [P, NG, U * FE])
        X = sb("X", [P, NB, F])
        TAB = sb("TAB", [P, NB, F])
        aggT = sb("aggT", [F, AW])
        degT = sb("degT", [F, AW])
        rT = sb("rT", [F, NP])
        M = sb("M", [F, len(mats), F])
        brow = sb("brow", [1, len(bias_rows), F])
        col = sb("col", [F, len(cols)])
        wblk = sb("wblk", [U * FE, U, F])
        ident = sb("ident", [P, P])
        identb = sb("identb", [P, P], bf16)
        iota_i = sb("iota_i", [P, P], i32)
        iota0 = sb("iota0", [P, P])
        iotak = sb("iotak", [P, P])
        ones_row = sb("ones_row", [1, P])
        ones_bf = sb("ones_bf", [P, F], bf16)
        eps_col = sb("eps_col", [P, 1])
        one_col = sb("one_col", [P, 1])
        base_row = sb("base_row", [1, NG])
        base_run = sb("base_run", [1, NG])
        basek_i = sb("basek_i", [1, NG], i32)
        kcnt = sb("kcnt", [1, 1], i32)
        dinv = sb("dinv", [P, NB])
        rdeg = sb("rdeg", [P, NB])
        est = sb("est", [F, 2])
        msq = sb("msq", [F, 1])
        crow = sb("crow", [1, F])
        idx_st = [sb(f"idx_st{i}", [P, U], i32) for i in range(2)]
        rows = [sb(f"rows{i}", [P, U, F]) for i in range(2)]
        oh = [sb(f"oh{i}", [P, U, P]) for i in range(2)]
        work = [sb(f"work{i}", [P, CB * P]) for i in range(4)]
        big = sb("big", [P, GE])
        big2 = sb("big2", [P, GE])
        big3 = sb("big3", [P, GE])
        ohb = sb("ohb", [P, U, P], bf16)
        ea_st = [sb(f"ea_st{i}", [P, U * FE]) for i in range(2)]
        eaT = [sb(f"eaT{i}", [U * FE, P]) for i in range(2)]
        erst = [sb(f"erst{i}", [F, 2]) for i in range(2)]
        small = sb("small", [P, 64])
        valid = [sb(f"valid{i}", [P, U]) for i in range(2)]
        vtmp = sb("vtmp", [P, U])
        qwin = [sb(f"qwin{i}", [P, F]) for i in range(2)]

        ps01 = pb("ps01", [P, 8, P])
        ps23 = pb("ps23", [P, 8, P])
        ps45 = pb("ps45", [P, 8, P])
        ps6 = pb("ps6", [P, 512])
        ps7 = pb("ps7", [P, 512])

        def mat(name):
            return M[:, mats.index(name), :]

        def bias(name):
            return brow[0:1, bias_rows.index(name), :]

        def cvec(name):
            return col[:, cols.index(name):cols.index(name) + 1]

        class Chain:

            def __init__(self, eng, semaphore, base, length):
                self.eng, self.sem, self.base, self.length, self.n = eng, semaphore, base, length, 0

            def __call__(self, ins):
                self.n += 1
                ins.then_inc(self.sem, 1)
                self.eng.wait_ge(self.sem, self.base + self.n)

            def done(self):
                assert self.n == self.length, (self.n, self.length)

        act_gate, pool_gate, dve_gate = sem("act_gate"), sem("pool_gate"), sem("dve_gate")

        s_pad, s_load, s_w, s_const, s_min = sem("s_pad"), sem("s_load"), sem("s_w"), sem("s_const"), sem("s_min")
        s_pe0, s_dv0 = sem("s_pe0"), sem("s_dv0")
        idx_staged, oh_ready, summed, acc_done = sem("idx_staged"), sem("oh_ready"), sem("summed"), sem("acc_done")
        gathered = [sem("gathered0"), sem("gathered1")]
        k_link, oh_cmp = sem("k_link"), sem("oh_cmp")
        ea_ready, eaT_ps, eaT_sb, er_ps = sem("ea_ready"), sem("eaT_ps"), sem("eaT_sb"), sem("er_ps")
        er_stat, est_done = sem("er_stat"), sem("est_done")
        dst_i = TAB[:, :, :].rearrange("p b f -> p (b f)").bitcast(i32)[:, 0:NG * U].rearrange("p (g u) -> p g u", u=U)
        gmm = work[0]
        FP, FR = REST // U, REST % U

        def edge_dmas(eng, d3, s1, width, s_done):
            n = 0
            if FULL:
                eng.dma_start(d3[:, 0:FULL, :], s1[0:FULL * GE * width].rearrange("(g p u) -> p g u", p=P, u=U * width)).then_inc(s_done, 16)
                n += 16
            if FP:
                o = FULL * GE * width
                eng.dma_start(d3[0:FP, FULL, :], s1[o:o + FP * U * width].rearrange("(p u) -> p u", p=FP)).then_inc(s_done, 16)
                n += 16
            if FR:
                o = (FULL * GE + FP * U) * width
                eng.dma_start(d3[FP:FP + 1, FULL, 0:FR * width], s1[o:o + FR * width].rearrange("(p u) -> p u", p=1)).then_inc(s_done, 16)
                n += 16
            return n

        with nc.Block() as block:
            @block.gpsimd
            def _(eng):
                eng.memset(idx_all[:, FULL:NG, :], 0).then_inc(s_pad, 1)
                eng.memset(dst_i[:, FULL:NG, :], int(FAR)).then_inc(s_pad, 1)
                eng.memset(w_all[:, FULL:NG, :], 0.0).then_inc(s_pad, 1)
                eng.memset(ea_all[:, FULL:NG, :], 0.0).then_inc(s_pad, 1)
                eng.memset(X[:, NB - 1:NB, :], 0.0).then_inc(s_pad, 1)
                eng.memset(wblk[:, :, :], 0.0).then_inc(s_pad, 1)
                eng.memset(ident[:, :], 0.0).then_inc(s_const, 1)
                eng.memset(ones_row[:, :], 1.0).then_inc(s_const, 1)
                eng.memset(ones_bf[:, :], 1.0).then_inc(s_const, 1)
                eng.memset(eps_col[:, :], EPS).then_inc(s_const, 1)
                eng.memset(one_col[:, :], 1.0).then_inc(s_const, 1)
                eng.iota(iota_i[:, :], pattern=[[1, P]], base=0, channel_multiplier=0).then_inc(s_const, 1)
                eng.wait_ge(s_const, 6)
                eng.affine_select(out=ident[:, :], in_=ident[:, :], compare_op=ALU.not_equal, fill=1.0,
                                  base=0, pattern=[[-1, P]], channel_multiplier=1).then_inc(s_const, 1)

            @block.sync
            def _(eng):
                eng.wait_ge(s_pad, 6)
                n = edge_dmas(eng, dst_i, dst, 1, s_load)
                n += edge_dmas(eng, idx_all, src, 1, s_load)
                eng.dma_start(X[:, 0:NB - 1, :], x[0:(NB - 1) * P, :].rearrange("(b p) f -> p b f", p=P)).then_inc(s_w, 16)
                eng.dma_start(X[0:N - (NB - 1) * P, NB - 1, :], x[(NB - 1) * P:N, :]).then_inc(s_w, 16)
                m = edge_dmas(eng, w_all, ew, 1, s_w) + 32
                m += edge_dmas(eng, ea_all, ea.rearrange("e c -> (e c)"), FE, s_w)
                for i, name in enumerate(mats):
                    eng.dma_start(M[:, i, :], mats_dram[name]).then_inc(s_w, 16)
                for i, name in enumerate(bias_rows):
                    eng.dma_start(brow[0:1, i, :], rows_dram[name].rearrange("(a f) -> a f", a=1)).then_inc(s_w, 16)
                for i, name in enumerate(cols):
                    eng.dma_start(col[:, i:i + 1], rows_dram[name].rearrange("(f a) -> f a", a=1)).then_inc(s_w, 16)
                for u in range(U):
                    eng.dma_start(wblk[u * FE:(u + 1) * FE, u, :], w_edge).then_inc(s_w, 16)
                m += 16 * (len(mats) + len(bias_rows) + len(cols) + U)
                eng.wait_ge(s_load, n)
                eng.wait_ge(s_w, m)
                eng.sem_inc(s_min, 1)

            @block.vector
            def _(eng):
                eng.sem_inc(acc_done, 2)
                eng.sem_inc(est_done, 2)
                eng.wait_ge(s_min, 1)
                eng.wait_ge(s_const, 7)
                link = Chain(eng, s_dv0, 0, 15)
                link(nc.vector.tensor_copy(iota0[:, :], iota_i[:, :]))
                link(nc.vector.tensor_copy(identb[:, :], ident[:, :]))
                link(nc.vector.tensor_copy(dstrel[:, :, :], dst_i[:, :, :]))
                link(nc.vector.tensor_reduce(gmm[:, 0:NG], dstrel[:, :, :], AX.X, ALU.min))
                m3 = work[1][:, 0:NG * U].rearrange("p (g u) -> p g u", u=U)
                link(nc.vector.scalar_tensor_tensor(out=m3, in0=dstrel[:, :, :], scalar=FAR, in1=dstrel[:, :, :],
                                                    op0=ALU.is_lt, op1=ALU.mult))
                link(nc.vector.tensor_reduce(gmm[:, NG:2 * NG], m3, AX.X, ALU.max))
                eng.wait_ge(s_pe0, 1)
                link(nc.vector.tensor_reduce(small[0:NG, 0:1], ps01[0:NG, 0, 0:P], AX.X, ALU.min))
                link(nc.vector.tensor_reduce(small[0:NG, 1:2], ps01[0:NG, 4, 0:P], AX.X, ALU.max))
                eng.wait_ge(s_pe0, 2)
                link(nc.vector.tensor_copy(base_row[0:1, :], ps6[0:1, 0:NG]))
                link(nc.vector.tensor_tensor(base_run[0:1, :], ps7[0:1, 0:NG], base_row[0:1, :], ALU.subtract))
                link(nc.vector.tensor_reduce(small[0:1, 2:3], base_run[0:1, :], AX.X, ALU.max))
                link(nc.vector.tensor_copy(kcnt[0:1, :], small[0:1, 2:3]))
                link(nc.vector.tensor_scalar(kcnt[0:1, :], kcnt[0:1, :], P.bit_length() - 1, None, ALU.logical_shift_right))
                link(nc.vector.tensor_scalar(kcnt[0:1, :], kcnt[0:1, :], 1.0, None, ALU.add))
                eng.wait_ge(s_pe0, 3)
                link(nc.vector.tensor_tensor(dstrel[:, :, :], dstrel[:, :, :],
                                             ps6[:, 0:NG].unsqueeze(2).to_broadcast([P, NG, U]), ALU.subtract))
                link.done()

            @block.scalar
            def _(eng):
                eng.sem_inc(eaT_sb, 1)
                eng.sem_inc(er_stat, 1)

            @block.tensor
            def _(eng):
                eng.sem_inc(summed, 2)
                eng.sem_inc(eaT_ps, 2)
                eng.wait_ge(s_dv0, 6)
                nc.tensor.transpose(ps01[0:NG, 0, 0:P], gmm[:, 0:NG], ident[:, :])
                nc.tensor.transpose(ps01[0:NG, 4, 0:P], gmm[:, NG:2 * NG], ident[:, :]).then_inc(s_pe0, 1)
                eng.wait_ge(s_dv0, 8)
                nc.tensor.transpose(ps6[0:1, 0:NG], small[0:NG, 0:1], ident[0:NG, 0:NG])
                nc.tensor.transpose(ps7[0:1, 0:NG], small[0:NG, 1:2], ident[0:NG, 0:NG]).then_inc(s_pe0, 1)
                eng.wait_ge(s_dv0, 14)
                nc.tensor.matmul(ps6[:, 0:NG], ones_row[0:1, :], base_row[0:1, :], start=True, stop=True).then_inc(s_pe0, 1)

        def passes(eng):
            return eng.value_load(kcnt[0:1, 0:1], min_val=1, max_val=MAXK)

        def one_hot(eng, dest, g, offsets):
            return nc.vector.tensor_tensor(dest, offsets[:, :].unsqueeze(1).to_broadcast([P, U, P]),
                                           dstrel[:, bass.ds(g, 1), :].rearrange("p a u -> p (a u)").unsqueeze(2).to_broadcast([P, U, P]),
                                           ALU.is_equal)

        def start_pass(link):
            link(nc.vector.tensor_scalar(basek_i[0:1, :], base_run[0:1, :], float(NP), None, ALU.min))

        def end_pass(link):
            link(nc.vector.tensor_scalar(base_run[0:1, :], base_run[0:1, :], float(P), None, ALU.add))
            link(nc.vector.tensor_scalar(iotak[:, :], iotak[:, :], float(P), None, ALU.add))

        def start_phase(link, target):
            link(nc.vector.memset(target[:, :], 0.0))
            link(nc.vector.tensor_copy(iotak[:, :], iota0[:, :]))
            link(nc.vector.tensor_copy(base_run[0:1, :], base_row[0:1, :]))
            link.eng.sem_inc(dve_gate, 1)

        def accumulate(eng, target, g, ps):
            at = eng.value_load(basek_i[0:1, bass.ds(g, 1)], min_val=0, max_val=NP)
            return lambda: nc.vector.tensor_tensor(target[:, bass.ds(at, P)], target[:, bass.ds(at, P)], ps, ALU.add)

        d_oh, d_sum, d_acc, d_link, d_row = sem("d_oh"), sem("d_sum"), sem("d_acc"), sem("d_link"), sem("d_row")
        with nc.Block() as block:
            @block.vector
            def _(eng):
                K = passes(eng)
                eng.sem_inc(d_acc, 2)
                link = Chain(eng, d_link, 0, 3)
                start_phase(link, degT)
                link.done()
                with eng.Fori(0, K) as k:
                    link = Chain(eng, d_link, k * 3 + 3, 3)
                    start_pass(link)
                    eng.sem_inc(dve_gate, 1)
                    with eng.Fori(0, NG // 2) as i:
                        for r in range(2):
                            g = i * 2 + r
                            eng.wait_ge(d_sum, k * NG + g + 1)
                            one_hot(eng, oh[r][:, :, :].rearrange("p u n -> p (u n)").bitcast(bf16)[:, 0:GE].rearrange("p (u n) -> p u n", n=P), g, iotak).then_inc(d_oh, 1)
                        for r in range(2):
                            g = i * 2 + r
                            add = accumulate(eng, degT, g, (ps6, ps7)[r][0:F, 0:P])
                            eng.wait_ge(d_sum, k * NG + g + 3)
                            eng.wait_ge(d_acc, k * NG + g + 2)
                            add().then_inc(d_acc, 1)
                    eng.wait_ge(d_acc, k * NG + NG + 2)
                    end_pass(link)
                    link.done()

            @block.tensor
            def _(eng):
                K = passes(eng)
                eng.sem_inc(d_sum, 2)
                with eng.Fori(0, K) as k:
                    with eng.Fori(0, NG // 2) as i:
                        for r in range(2):
                            g = i * 2 + r
                            eng.wait_ge(d_oh, k * NG + g + 1)
                            eng.wait_ge(d_acc, k * NG + g + 1)
                            hot = oh[r][:, :, :].rearrange("p u n -> p (u n)").bitcast(bf16)
                            for u in range(U):
                                last = nc.tensor.matmul((ps6, ps7)[r][0:F, 0:P], ones_bf[:, :], hot[:, u * P:(u + 1) * P],
                                                        start=(u == 0), stop=(u == U - 1))
                            last.then_inc(d_sum, 1)

            @block.sync
            def _(eng):
                K = passes(eng)
                eng.wait_ge(d_acc, K * NG + 2)
                eng.dma_start(degrow[0:1, :], degT[0:1, 0:NP]).then_inc(d_row, 16)
                eng.wait_ge(d_row, 16)
                eng.dma_start(small[:, 0:NB], degrow.rearrange("a (b p) -> p (a b)", p=P), allow_slow_non_contiguous=True).then_inc(d_row, 16)
                eng.wait_ge(d_row, 32)

        nd_staged, nd_T, nd_xT, nd_mm, nd_evac = sem("nd_staged"), sem("nd_T"), sem("nd_xT"), sem("nd_mm"), sem("nd_evac")
        nd_out, nd_dma, nd_link, nd_var, nd_sd = sem("nd_out"), sem("nd_dma"), sem("nd_link"), sem("nd_var"), sem("nd_sd")
        t_sd, t_tab, t_link, t_dma = sem("t_sd"), sem("t_tab"), sem("t_link"), sem("t_dma")
        with nc.Block() as block:
            @block.scalar
            def _(eng):
                eng.activation(dinv[:, :], small[:, 0:NB], ACT.Sqrt, bias=one_col[:, 0:1]).then_inc(t_sd, 1)

            @block.vector
            def _(eng):
                link = Chain(eng, t_link, 0, 3)
                eng.wait_ge(t_sd, 1)
                link(nc.vector.reciprocal(dinv[:, :], dinv[:, :]))
                link(nc.vector.tensor_scalar(rdeg[:, :], small[:, 0:NB], 1.0, None, ALU.max))
                link(nc.vector.reciprocal(rdeg[:, :], rdeg[:, :]))
                link.done()
                nc.vector.tensor_tensor(TAB[:, :, :], X[:, :, :], dinv[:, :].unsqueeze(2).to_broadcast([P, NB, F]), ALU.mult).then_inc(t_tab, 1)

            @block.sync
            def _(eng):
                eng.wait_ge(t_tab, 1)
                eng.dma_start(table.rearrange("(b p) f -> p b f", p=P), TAB[:, :, :]).then_inc(t_dma, 16)
                eng.wait_ge(t_dma, 16)

        def aggregate(ph, weighted=False, edge_stats=False):
            def at(k, K, g):
                return (k + K * ph) * NG + g

            with nc.Block() as block:
                @block.gpsimd
                def _(eng):
                    K = passes(eng)
                    with eng.Fori(0, K) as k:
                        with eng.Fori(0, NG // 2) as i:
                            for r in range(2):
                                eng.wait_ge(idx_staged, at(k, K, i * 2 + r) + 1)
                                eng.sem_inc(pool_gate, 1)
                                for u in range(U):
                                    eng.indirect_dma_start(
                                        out=rows[r][:, u, :], out_offset=None, in_=table[:, :],
                                        in_offset=bass.IndirectOffsetOnAxis(ap=idx_st[r][:, u:u + 1], axis=0)).then_inc(gathered[r], 16)

                @block.scalar
                def _(eng):
                    K = passes(eng)
                    with eng.Fori(0, K) as k:
                        with eng.Fori(0, NG // 2) as i:
                            for r in range(2):
                                g = i * 2 + r
                                eng.wait_ge(summed, at(k, K, g) + 1)
                                eng.sem_inc(act_gate, 1)
                                nc.scalar.activation(idx_st[r][:, :], idx_all[:, bass.ds(g, 1), :].rearrange("p a u -> p (a u)"),
                                                     ACT.Copy).then_inc(idx_staged, 1)
                                if edge_stats:
                                    n = k * NG + g
                                    eng.wait_ge(eaT_ps, n + 3)
                                    nc.scalar.activation(eaT[r][:, :], ps01[0:U * FE, 0, :], ACT.Copy).then_inc(eaT_sb, 1)
                                    eng.wait_ge(er_ps, n + 1)
                                    eng.wait_ge(est_done, n + 1)
                                    nc.scalar.activation(big[0:F, :], ps23[0:F, :, :].rearrange("p u e -> p (u e)"), ACT.Relu,
                                                         bias=cvec("b_edge"), accum_out=erst[r][:, 0:1]).then_inc(er_relu, 1)
                                    eng.wait_ge(er_relu, n + 1)
                                    nc.scalar.activation(big2[0:F, :], big[0:F, :], ACT.Square,
                                                         accum_out=erst[r][:, 1:2]).then_inc(er_stat, 1)

                @block.vector
                def _(eng):
                    K = passes(eng)
                    link = Chain(eng, k_link, K * (ph * 4) + ph * 3, 3)
                    start_phase(link, aggT)
                    link.done()
                    with eng.Fori(0, K) as k:
                        link = Chain(eng, k_link, (k + K * ph) * 4 + (ph * 3 + 3), 4)
                        start_pass(link)
                        link(nc.vector.memset(est[:, :], 0.0)) if edge_stats else link(nc.vector.memset(msq[:, :], 0.0))
                        eng.sem_inc(dve_gate, 1)
                        with eng.Fori(0, NG // 2) as i:
                            for r in range(2):
                                g = i * 2 + r
                                eng.wait_ge(summed, at(k, K, g) + 1)
                                if weighted:
                                    for u in range(U):
                                        last = nc.vector.tensor_scalar(
                                            oh[r][:, u, :], iotak[:, :],
                                            dstrel[:, bass.ds(g, 1), u:u + 1].rearrange("p a b -> p (a b)"),
                                            w_all[:, bass.ds(g, 1), u:u + 1].rearrange("p a b -> p (a b)"), ALU.is_equal, ALU.mult)
                                    last.then_inc(oh_ready, 1)
                                else:
                                    one_hot(eng, oh[r][:, :, :], g, iotak).then_inc(oh_ready, 1)
                                if edge_stats:
                                    eng.wait_ge(eaT_ps, k * NG + g + 1)
                                    nc.vector.tensor_scalar(ea_st[r][:, :], ea_all[:, bass.ds(g, 1), :].rearrange("p a c -> p (a c)"),
                                                            1.0, None, ALU.mult).then_inc(ea_ready, 1)
                            for r in range(2):
                                g = i * 2 + r
                                add = accumulate(eng, aggT, g, (ps6, ps7)[r][0:F, 0:P])
                                eng.wait_ge(summed, at(k, K, g) + 3)
                                eng.wait_ge(acc_done, at(k, K, g) + 2)
                                add().then_inc(acc_done, 1)
                                if edge_stats:
                                    eng.wait_ge(er_stat, k * NG + g + 2)
                                    eng.wait_ge(est_done, k * NG + g + 2)
                                    nc.vector.tensor_tensor(est[:, :], est[:, :], erst[r][:, :], ALU.add).then_inc(est_done, 1)
                        eng.wait_ge(acc_done, at(k, K, NG) + 2)
                        if edge_stats:
                            eng.wait_ge(est_done, k * NG + NG + 2)
                        end_pass(link)
                        link.done()

                @block.tensor
                def _(eng):
                    K = passes(eng)
                    with eng.Fori(0, K) as k:
                        with eng.Fori(0, NG // 2) as i:
                            for r in range(2):
                                g = i * 2 + r
                                if edge_stats:
                                    n = k * NG + g
                                    eng.wait_ge(ea_ready, n + 1)
                                    eng.wait_ge(eaT_sb, n + 1)
                                    nc.tensor.transpose(ps01[0:U * FE, 0, :], ea_st[r][:, :], ident[:, :]).then_inc(eaT_ps, 1)
                                    eng.wait_ge(eaT_sb, n + 2)
                                    eng.wait_ge(er_stat, n + 1)
                                    for u in range(U):
                                        last = nc.tensor.matmul(ps23[0:F, u, :], wblk[:, u, :], eaT[r][:, :], start=True, stop=True)
                                    last.then_inc(er_ps, 1)
                                eng.wait_ge(oh_ready, at(k, K, g) + 1)
                                eng.wait_ge(acc_done, at(k, K, g) + 1)
                                eng.wait_ge(gathered[r], ((k + K * ph) * (NG // 2) + i) * (16 * U) + 16 * U)
                                for u in range(U):
                                    last = nc.tensor.matmul((ps6, ps7)[r][0:F, 0:P], rows[r][:, u, :], oh[r][:, u, :],
                                                            start=(u == 0), stop=(u == U - 1))
                                last.then_inc(summed, 1)

        stA, stN, xT, tt = work[0], work[1], work[2], work[3]
        tt3 = tt[:, 0:CB * F].rearrange("p (b f) -> p b f", f=F)
        sq3 = big3[:, 0:CB * F].rearrange("p (b f) -> p b f", f=F)
        stN3 = stN[:, 0:CB * F].rearrange("p (b f) -> p b f", f=F)
        s1, v1 = small[:, 0:CB], small[:, 8:8 + CB]

        def bc(ap):
            return ap.unsqueeze(2).to_broadcast([P, CB, F])

        def layernorm(eng, link, result, n):
            link(nc.vector.tensor_reduce(s1, tt3, AX.X, ALU.add))
            link(nc.vector.tensor_scalar(s1, s1, 1.0 / F, None, ALU.mult))
            link(nc.vector.tensor_tensor(tt3, tt3, bc(s1), ALU.subtract))
            link(nc.vector.tensor_tensor(sq3, tt3, tt3, ALU.mult))
            link(nc.vector.tensor_reduce(v1, sq3, AX.X, ALU.add))
            eng.sem_inc(nd_var, 1)
            eng.wait_ge(nd_sd, n + 1)
            link(nc.vector.reciprocal(v1, v1))
            return nc.vector.tensor_tensor(result, tt3, bc(v1), ALU.mult)

        def stddev(eng, n):
            eng.wait_ge(nd_var, n + 1)
            nc.scalar.activation(v1, v1, ACT.Sqrt, bias=eps_col[:, 0:1], scale=1.0 / F).then_inc(nd_sd, 1)

        LINKS = 24
        ln_count = [0]

        def dense(q, node, WA, WB, brow_name, scale, relu, residual):
            ln0 = ln_count[0]
            if residual:
                ln_count[0] += NCH
            nlinks = 2 + (7 if residual else 1 if relu else 0)
            lbase = link_base[0]
            link_base[0] += nlinks * NCH
            with nc.Block() as block:
                @block.scalar
                def _(eng):
                    with eng.Fori(0, NCH) as c:
                        n = c + q * NCH
                        eng.wait_ge(nd_mm, n + 1)
                        eng.sem_inc(act_gate, 1)
                        nc.scalar.activation(stA[0:F, :], aggT[:, bass.ds(c * CW, CW)], ACT.Copy)
                        nc.scalar.activation(stN3, node[:, bass.ds(c * CB, CB), :], ACT.Copy).then_inc(nd_staged, 1)
                        eng.wait_ge(nd_T, n + 1)
                        nc.scalar.activation(xT[0:F, :], ps01[0:F, 0:CB, :].rearrange("p b n -> p (b n)"), ACT.Copy).then_inc(nd_xT, 1)
                        if residual:
                            stddev(eng, c + ln0)

                @block.tensor
                def _(eng):
                    with eng.Fori(0, NCH) as c:
                        n = c + q * NCH
                        eng.wait_ge(nd_staged, n + 1)
                        for j in range(CB):
                            last = nc.tensor.transpose(ps01[0:F, j, :], stN3[:, j, :], ident[:, :])
                        last.then_inc(nd_T, 1)
                        eng.wait_ge(nd_xT, n + 1)
                        eng.wait_ge(nd_evac, n + 1)
                        for j in range(CB):
                            a, b = stA[0:F, j * P:(j + 1) * P], xT[0:F, j * P:(j + 1) * P]
                            nc.tensor.matmul(ps23[:, j, 0:F], a, mat(WA), start=True, stop=WB is not None)
                            if WB is None:
                                nc.tensor.matmul(ps23[:, j, 0:F], b, mat(WA), start=False, stop=True)
                            else:
                                nc.tensor.matmul(ps45[:, j, 0:F], b, mat(WB), start=True, stop=False)
                            last = nc.tensor.matmul(ps45[:, j, 0:F], ones_row[0:1, :], bias(brow_name), start=WB is None, stop=True)
                        last.then_inc(nd_mm, 1)

                @block.vector
                def _(eng):
                    with eng.Fori(0, NCH) as c:
                        n = c + q * NCH
                        eng.wait_ge(nd_mm, n + 2)
                        eng.wait_ge(nd_out, n + 1)
                        link = Chain(eng, nd_link, c * nlinks + lbase, nlinks)
                        if scale is None:
                            link(nc.vector.tensor_copy(tt3, ps23[:, 0:CB, 0:F]))
                        else:
                            link(nc.vector.tensor_tensor(tt3, ps23[:, 0:CB, 0:F], bc(scale[:, bass.ds(c * CB, CB)]), ALU.mult))
                        link(nc.vector.tensor_tensor(tt3, tt3, ps45[:, 0:CB, 0:F], ALU.add))
                        eng.sem_inc(nd_evac, 1)
                        xc, tc = X[:, bass.ds(c * CB, CB), :], TAB[:, bass.ds(c * CB, CB), :]
                        if relu and residual:
                            link(nc.vector.scalar_tensor_tensor(out=tt3, in0=tt3, scalar=0.0, in1=xc, op0=ALU.max, op1=ALU.add))
                        elif residual:
                            link(nc.vector.tensor_tensor(tt3, tt3, xc, ALU.add))
                        elif relu:
                            link(nc.vector.tensor_scalar(tt3, tt3, 0.0, None, ALU.max))
                        if residual:
                            layernorm(eng, link, xc, c + ln0).then_inc(nd_out, 1)
                        elif q == 0:
                            nc.vector.tensor_tensor(tc, tt3, bc(dinv[:, bass.ds(c * CB, CB)]), ALU.mult).then_inc(nd_out, 1)
                        else:
                            nc.vector.tensor_scalar(tc, tt3, 1.0, None, ALU.mult).then_inc(nd_out, 1)
                        link.done()

                @block.sync
                def _(eng):
                    new = X if residual else TAB
                    with eng.Fori(0, NCH) as c:
                        eng.wait_ge(nd_out, c + (q * NCH + 2))
                        eng.dma_start(table[bass.ds(c * CW, CW), :].rearrange("(b p) f -> p b f", p=P),
                                      new[:, bass.ds(c * CB, CB), :]).then_inc(nd_dma, 16)
                    eng.wait_ge(nd_dma, 16 * NCH * (q + 1))

        link_base = [0]
        er_relu = sem("er_relu")
        with nc.Block() as block:
            @block.tensor
            def _(eng):
                eng.sem_inc(nd_mm, 1)
            @block.vector
            def _(eng):
                eng.sem_inc(nd_evac, 1)
                eng.sem_inc(nd_out, 1)

        aggregate(0, edge_stats=True)
        dense(0, TAB, "L0W1", None, "L0b1", dinv, True, False)
        aggregate(1)
        dense(1, TAB, "L0W2", None, "L0b2", dinv, True, True)
        aggregate(2)
        dense(2, X, "L1Wl1T", "L1Wr1T", "L1bl1", rdeg, True, False)
        aggregate(3)
        dense(3, TAB, "L1Wl2T", "L1Wr2T", "L1bl2", rdeg, False, True)
        aggregate(4, weighted=True)
        dense(4, X, "L2WbT", "L2WaT", "L2b", None, False, True)

        bn = sb("bn", [F, 24])
        bn_sd, bn_pe, bn_link = sem("bn_sd"), sem("bn_pe"), sem("bn_link")
        BN_LINKS = 9

        def bcol(i):
            return bn[:, i:i + 1]

        def batchnorm(eng, link, total, square, count, gamma, beta, at, n):
            mean, var, tmp, scale, shift = bcol(at + 2), bcol(at + 3), bcol(at + 4), bcol(at), bcol(at + 1)
            link(nc.vector.tensor_scalar(mean, total, 1.0 / count, None, ALU.mult))
            link(nc.vector.tensor_scalar(var, square, 1.0 / count, None, ALU.mult))
            link(nc.vector.tensor_tensor(tmp, mean, mean, ALU.mult))
            link(nc.vector.tensor_tensor(var, var, tmp, ALU.subtract))
            link(nc.vector.tensor_scalar(var, var, 0.0, None, ALU.max))
            eng.sem_inc(bn_var, 1)
            eng.wait_ge(bn_sd, n + 1)
            link(nc.vector.reciprocal(var, var))
            link(nc.vector.tensor_tensor(scale, var, cvec(gamma), ALU.mult))
            link(nc.vector.tensor_tensor(tmp, mean, scale, ALU.mult))
            link(nc.vector.tensor_tensor(shift, cvec(beta), tmp, ALU.subtract))

        def batch_stddev(eng, at, n):
            eng.wait_ge(bn_var, n + 1)
            nc.scalar.activation(bcol(at + 3), bcol(at + 3), ACT.Sqrt, bias=eps_col[0:F, 0:1]).then_inc(bn_sd, 1)

        bn_var = sem("bn_var")

        Q5 = 5
        qst3 = big[:, 0:CB * F].rearrange("p (b f) -> p b f", f=F)
        m_sc, m_q, m_pad, m_r = sem("m_sc"), sem("m_q"), sem("m_pad"), sem("m_r")
        with nc.Block() as block:
            @block.scalar
            def _(eng):
                batch_stddev(eng, 0, 0)
                with eng.Fori(0, NCH) as c:
                    n = c + Q5 * NCH
                    eng.wait_ge(nd_mm, n + 1)
                    eng.sem_inc(act_gate, 1)
                    nc.scalar.activation(stN3, X[:, bass.ds(c * CB, CB), :], ACT.Copy).then_inc(nd_staged, 1)
                    eng.wait_ge(nd_T, n + 1)
                    nc.scalar.activation(xT[0:F, :], ps01[0:F, 0:CB, :].rearrange("p b n -> p (b n)"), ACT.Copy).then_inc(nd_xT, 1)
                    eng.wait_ge(nd_mm, n + 2)
                    eng.sem_inc(act_gate, 1)
                    nc.scalar.activation(rT[:, bass.ds(c * CW, CW)], ps01[0:F, 0:CB, :].rearrange("p b n -> p (b n)"), ACT.Relu,
                                         bias=cvec("b_node")).then_inc(m_r, 1)

            @block.tensor
            def _(eng):
                eng.sem_inc(m_r, 1)
                eng.wait_ge(bn_link, BN_LINKS + 5)
                nc.tensor.matmul(ps6[0:1, 0:F], bcol(1), mat("Wfeat"), start=True, stop=True).then_inc(bn_pe, 1)
                eng.wait_ge(m_sc, 1)
                with eng.Fori(0, NCH) as c:
                    n = c + Q5 * NCH
                    eng.wait_ge(nd_staged, n + 1)
                    eng.wait_ge(m_r, c + 1)
                    for j in range(CB):
                        last = nc.tensor.transpose(ps01[0:F, j, :], stN3[:, j, :], ident[:, :])
                    last.then_inc(nd_T, 1)
                    eng.wait_ge(nd_xT, n + 1)
                    eng.wait_ge(nd_evac, n + 1)
                    for j in range(CB):
                        b = xT[0:F, j * P:(j + 1) * P]
                        nc.tensor.matmul(ps23[:, j, 0:F], b, mat("Wsrc"), start=True, stop=True)
                        nc.tensor.matmul(ps45[:, j, 0:F], b, mat("Wdst"), start=True, stop=False)
                        nc.tensor.matmul(ps45[:, j, 0:F], ones_row[0:1, :], crow[0:1, :], start=False, stop=True)
                    nc.tensor.matmul(ps01[0:F, 0:4, :], mat("Wnode"), xT[0:F, 0:4 * P], start=True, stop=True)
                    nc.tensor.matmul(ps01[0:F, 4:CB, :], mat("Wnode"), xT[0:F, 4 * P:CW], start=True, stop=True).then_inc(nd_mm, 1)

            @block.vector
            def _(eng):
                link = Chain(eng, bn_link, 0, BN_LINKS + 7)
                link(nc.vector.tensor_scalar(bcol(6), cvec("b_edge"), 0.0, None, ALU.max))
                link(nc.vector.tensor_tensor(bcol(7), bcol(6), bcol(6), ALU.mult))
                link(nc.vector.scalar_tensor_tensor(out=est[:, 0:1], in0=bcol(6), scalar=-float(NPAD_E), in1=est[:, 0:1],
                                                    op0=ALU.mult, op1=ALU.add))
                link(nc.vector.scalar_tensor_tensor(out=est[:, 1:2], in0=bcol(7), scalar=-float(NPAD_E), in1=est[:, 1:2],
                                                    op0=ALU.mult, op1=ALU.add))
                link(nc.vector.memset(big2[:, 0:F], 0.0))
                batchnorm(eng, link, est[:, 0:1], est[:, 1:2], E, "g_edge", "beta_edge", 0, 0)
                eng.wait_ge(bn_pe, 1)
                link(nc.vector.tensor_tensor(crow[0:1, :], ps6[0:1, 0:F], bias("b_msg"), ALU.add))
                link(nc.vector.tensor_scalar(mat("Wfeat"), mat("Wfeat"), bcol(0), None, ALU.mult))
                link.done()
                eng.sem_inc(m_sc, 1)
                with eng.Fori(0, NCH) as c:
                    n = c + Q5 * NCH
                    eng.wait_ge(nd_mm, n + 2)
                    eng.wait_ge(m_q, c * 16 + 16)
                    nc.vector.tensor_scalar(TAB[:, bass.ds(c * CB, CB), :], ps23[:, 0:CB, 0:F], 1.0, None, ALU.mult).then_inc(nd_out, 1)
                    nc.vector.tensor_copy(qst3, ps45[:, 0:CB, 0:F]).then_inc(nd_evac, 1)

            @block.sync
            def _(eng):
                eng.wait_ge(bn_link, 5)
                eng.dma_start(qtable[NP:AW, :], big2[:, 0:F]).then_inc(m_q, 16)
                with eng.Fori(0, NCH) as c:
                    eng.wait_ge(nd_out, c + (Q5 * NCH + 2))
                    eng.dma_start(table[bass.ds(c * CW, CW), :].rearrange("(b p) f -> p b f", p=P),
                                  TAB[:, bass.ds(c * CB, CB), :]).then_inc(nd_dma, 16)
                    eng.wait_ge(nd_evac, c + (Q5 * NCH + 2))
                    eng.dma_start(qtable[bass.ds(c * CW, CW), :].rearrange("(b p) f -> p b f", p=P), qst3).then_inc(m_q, 16)
                eng.wait_ge(nd_dma, 16 * NCH * (Q5 + 1))
                eng.wait_ge(m_q, 16 * NCH + 16)

        PH = 5
        v_link, sp_gate = sem("v_link"), sem("sp_gate")
        names = "oh ohb ea eaT eaTs ohT ohTs er ers pre hs relu h msq".split()
        q = {name: sem(f"q_{name}") for name in names}
        q_win = [sem("q_win0"), sem("q_win1")]
        q_pass = sem("q_pass")
        tabf = TAB[:, :, :].rearrange("p b f -> p (b f)")
        UF = U * F
        hbuf = [tabf[:, r * UF:(r + 1) * UF].rearrange("p (u f) -> p u f", f=F) for r in range(2)]
        sqbuf = [tabf[:, (2 + r) * UF:(3 + r) * UF].rearrange("p (u f) -> p u f", f=F) for r in range(2)]
        ohT_sb = big2[:, :].rearrange("p (u e) -> p u e", e=P)
        hsum = big3[:, 0:UF].rearrange("p (u f) -> p u f", f=F)
        ohT_ps = ps45[:, 0:4, :].rearrange("p b n -> p (b n)").bitcast(bf16).rearrange("p (u e) -> p u e", e=P)
        ea_ps = ps45[0:U * FE, 4, :]
        with nc.Block() as block:
            def flat(ap):
                return ap.rearrange("p u e -> p (u e)")

            @block.gpsimd
            def _(eng):
                K = passes(eng)
                with eng.Fori(0, K) as k:
                    with eng.Fori(0, NG // 2) as i:
                        for r in range(2):
                            eng.wait_ge(idx_staged, (k + K * PH) * NG + i * 2 + r + 1)
                            eng.sem_inc(pool_gate, 1)
                            for u in range(U):
                                eng.indirect_dma_start(
                                    out=rows[r][:, u, :], out_offset=None, in_=table[:, :],
                                    in_offset=bass.IndirectOffsetOnAxis(ap=idx_st[r][:, u:u + 1], axis=0)).then_inc(gathered[r], 16)

            @block.sync
            def _(eng):
                K = passes(eng)
                with eng.Fori(0, K) as k:
                    eng.wait_ge(q_pass, k + 1)
                    eng.sem_inc(sp_gate, 1)
                    with eng.Fori(0, NG // 2) as i:
                        for r in range(2):
                            g = i * 2 + r
                            at = eng.value_load(basek_i[0:1, bass.ds(g, 1)], min_val=0, max_val=NP)
                            eng.wait_ge(q["pre"], k * NG + g + 1)
                            eng.dma_start(qwin[r][:, :], qtable[bass.ds(at, P), :]).then_inc(q_win[r], 16)

            @block.scalar
            def _(eng):
                K = passes(eng)
                with eng.Fori(0, K) as k:
                    def wait(name, g):
                        eng.wait_ge(q[name], k * NG + g + 3)

                    def stage(g, r):
                        wait("hs", g - 2)
                        eng.sem_inc(act_gate, 1)
                        nc.scalar.activation(idx_st[r][:, :], idx_all[:, bass.ds(g, 1), :].rearrange("p a u -> p (a u)"),
                                             ACT.Copy).then_inc(idx_staged, 1)

                    def operands(g, r):
                        wait("oh", g)
                        wait("ohT", g - 1)
                        nc.scalar.activation(flat(ohb[:, :, :]), flat(oh[r][:, :, :]), ACT.Copy).then_inc(q["ohb"], 1)
                        wait("eaT", g)
                        nc.scalar.activation(eaT[r][:, :], ea_ps, ACT.Copy).then_inc(q["eaTs"], 1)

                    def features(g, r):
                        wait("er", g)
                        wait("pre", g - 1)
                        nc.scalar.activation(big[0:F, :], flat(ps01[0:F, :, :]), ACT.Relu, bias=cvec("b_edge")).then_inc(q["ers"], 1)

                    def messages(g, r):
                        wait("hs", g)
                        eng.wait_ge(summed, (k + K * PH) * NG + g + 1)
                        nc.scalar.activation(flat(hbuf[r]), flat(hsum), ACT.Relu).then_inc(q["relu"], 1)
                        wait("relu", g)
                        nc.scalar.activation(flat(sqbuf[r]), flat(hbuf[r]), ACT.Square).then_inc(q["h"], 1)

                    stage(0, 0)
                    operands(0, 0)
                    features(0, 0)
                    stage(1, 1)
                    operands(1, 1)
                    messages(0, 0)
                    features(1, 1)
                    with eng.Fori(0, NG // 2 - 1) as i:
                        for d in range(2):
                            g, r = i * 2 + (1 + d), (1 + d) % 2
                            stage(g + 1, 1 - r)
                            operands(g + 1, 1 - r)
                            messages(g, r)
                            features(g + 1, 1 - r)
                    messages(NG - 1, 1)

            @block.vector
            def _(eng):
                K = passes(eng)
                eng.sem_inc(q["ea"], 2)
                for name in names:
                    if name != "ea":
                        eng.sem_inc(q[name], 2)
                link = Chain(eng, k_link, K * (PH * 4) + PH * 3, 3)
                start_phase(link, aggT)
                link.done()
                vlink = Chain(eng, v_link, 0, 0)
                with eng.Fori(0, K) as k:
                    link = Chain(eng, k_link, (k + K * PH) * 4 + (PH * 3 + 3), 4)
                    start_pass(link)
                    link(nc.vector.memset(msq[:, :], 0.0))
                    vlink = Chain(eng, v_link, k * 3, 3)
                    vlink(nc.vector.tensor_scalar(flat(w_all[:, :, :]), flat(dstrel[:, :, :]), iotak[:, 0:1], 0.0, ALU.subtract, ALU.is_ge))
                    vlink(nc.vector.tensor_scalar(work[0][:, 0:NG * U], flat(dstrel[:, :, :]), iotak[:, 0:1], float(P), ALU.subtract, ALU.is_lt))
                    vlink(nc.vector.tensor_tensor(flat(w_all[:, :, :]), flat(w_all[:, :, :]), work[0][:, 0:NG * U], ALU.mult))
                    vlink.done()
                    eng.sem_inc(q_pass, 1)

                    def wait(name, g):
                        eng.wait_ge(q[name], k * NG + g + 3)

                    def hots(g, r):
                        eng.wait_ge(summed, (k + K * PH) * NG + g + 1)
                        one_hot(eng, oh[r][:, :, :], g, iotak).then_inc(q["oh"], 1)
                        nc.vector.tensor_scalar(valid[r][:, :], w_all[:, bass.ds(g, 1), :].rearrange("p a u -> p (a u)"), 1.0, None, ALU.mult)
                        nc.vector.tensor_scalar(ea_st[r][:, :], ea_all[:, bass.ds(g, 1), :].rearrange("p a c -> p (a c)"),
                                                1.0, None, ALU.mult).then_inc(q["ea"], 1)

                    def transposed(g, r):
                        wait("ohT", g)
                        wait("pre", g - 1)
                        nc.vector.tensor_copy(flat(ohT_sb), flat(ohT_ps)).then_inc(q["ohTs"], 1)

                    def add_rows(g, r, half):
                        wait("pre", g)
                        wait("h", g - 1)
                        eng.wait_ge(gathered[r], ((k + K * PH) * (NG // 2) + half) * (16 * U) + 16 * U)
                        nc.vector.tensor_tensor(hsum, ps23[:, :, 0:F], rows[r][:, :, :], ALU.add).then_inc(q["hs"], 1)

                    def accumulate_sums(g, r):
                        add = accumulate(eng, aggT, g, (ps6, ps7)[r][0:F, 0:P])
                        eng.wait_ge(summed, (k + K * PH) * NG + g + 3)
                        eng.wait_ge(acc_done, (k + K * PH) * NG + g + 2)
                        add().then_inc(acc_done, 1)
                        wait("msq", g - 1)
                        nc.vector.tensor_tensor(msq[:, :], msq[:, :], (ps6, ps7)[r][0:F, P:P + 1], ALU.add).then_inc(q["msq"], 1)

                    hots(0, 0)
                    transposed(0, 0)
                    hots(1, 1)
                    add_rows(0, 0, 0)
                    transposed(1, 1)
                    with eng.Fori(0, NG // 2 - 1) as i:
                        for d in range(2):
                            g, r = i * 2 + (1 + d), (1 + d) % 2
                            hots(g + 1, 1 - r)
                            accumulate_sums(g - 1, 1 - r)
                            add_rows(g, r, i + d)
                            transposed(g + 1, 1 - r)
                    accumulate_sums(NG - 2, 0)
                    add_rows(NG - 1, 1, NG // 2 - 1)
                    accumulate_sums(NG - 1, 1)
                    eng.wait_ge(acc_done, (k + K * PH) * NG + (NG + 2))
                    wait("msq", NG - 1)
                    end_pass(link)
                    link.done()

            @block.tensor
            def _(eng):
                K = passes(eng)
                with eng.Fori(0, K) as k:
                    def wait(name, g):
                        eng.wait_ge(q[name], k * NG + g + 3)

                    def operands(g, r):
                        wait("ea", g)
                        wait("eaTs", g - 1)
                        nc.tensor.transpose(ea_ps, ea_st[r][:, :], ident[:, :]).then_inc(q["eaT"], 1)
                        wait("ohb", g)
                        wait("ohTs", g - 1)
                        for u in range(U):
                            last = nc.tensor.transpose(ohT_ps[:, u, :], ohb[:, u, :], identb[:, :])
                        last.then_inc(q["ohT"], 1)
                        wait("eaTs", g)
                        wait("ers", g - 1)
                        for u in range(U):
                            last = nc.tensor.matmul(ps01[0:F, u, :], wblk[:, u, :], eaT[r][:, :], start=True, stop=True)
                        last.then_inc(q["er"], 1)

                    def preact(g, r, half):
                        wait("ers", g)
                        wait("ohTs", g)
                        wait("hs", g - 1)
                        eng.wait_ge(q_win[r], (k * (NG // 2) + half) * 16 + 16)
                        for u in range(U):
                            nc.tensor.matmul(ps23[:, u, 0:F], big[0:F, u * P:(u + 1) * P], mat("Wfeat"), start=True, stop=False)
                            last = nc.tensor.matmul(ps23[:, u, 0:F], ohT_sb[:, u, :], qwin[r][:, :], start=False, stop=True)
                        last.then_inc(q["pre"], 1)

                    def sums(g, r):
                        wait("h", g)
                        wait("msq", g - 2)
                        eng.wait_ge(acc_done, (k + K * PH) * NG + g + 1)
                        ps = (ps6, ps7)[r]
                        for u in range(U):
                            nc.tensor.matmul(ps[0:F, 0:P], hbuf[r][:, u, :], oh[r][:, u, :], start=(u == 0), stop=(u == U - 1))
                        for u in range(U):
                            last = nc.tensor.matmul(ps[0:F, P:P + 1], sqbuf[r][:, u, :], valid[r][:, u:u + 1],
                                                    start=(u == 0), stop=(u == U - 1))
                        last.then_inc(summed, 1)

                    operands(0, 0)
                    preact(0, 0, 0)
                    operands(1, 1)
                    with eng.Fori(0, NG // 2 - 1) as i:
                        for d in range(2):
                            g, r = i * 2 + (1 + d), (1 + d) % 2
                            sums(g - 1, 1 - r)
                            preact(g, r, i + d)
                            operands(g + 1, 1 - r)
                    sums(NG - 2, 0)
                    preact(NG - 1, 1, NG // 2 - 1)
                    sums(NG - 1, 1)

        f_stat, f_link, f_in, f_T, f_out, f_dma, f_free = sem("f_stat"), sem("f_link"), sem("f_in"), sem("f_T"), sem("f_out"), sem("f_dma"), sem("f_free")
        ln0 = ln_count[0]
        FL = 11
        ot3 = big2[:, 0:CB * F].rearrange("p (b f) -> p b f", f=F)
        with nc.Block() as block:
            @block.scalar
            def _(eng):
                for c in range(NCH):
                    w = min(CW, N - c * CW)
                    nc.scalar.activation(big[0:F, 0:w], rT[:, c * CW:c * CW + w], ACT.Square, accum_out=bn[:, 16 + c:17 + c]).then_inc(f_stat, 1)
                    eng.wait_ge(f_stat, c + 1)
                batch_stddev(eng, 0, 1)
                batch_stddev(eng, 8, 2)
                with eng.Fori(0, NCH) as c:
                    stddev(eng, c + ln0)

            @block.vector
            def _(eng):
                eng.sem_inc(f_out, 1)
                base = BN_LINKS + 7
                link = Chain(eng, bn_link, base, 2 * BN_LINKS + 3)
                link(nc.vector.tensor_reduce(bcol(14), aggT[:, 0:N], AX.X, ALU.add))
                link(nc.vector.tensor_reduce(bcol(15), rT[:, 0:N], AX.X, ALU.add))
                batchnorm(eng, link, bcol(14), msq[:, :], E, "g_msg", "beta_msg", 0, 1)
                eng.wait_ge(f_stat, NCH)
                link(nc.vector.tensor_reduce(bcol(23), bn[:, 16:16 + NCH], AX.X, ALU.add))
                batchnorm(eng, link, bcol(15), bcol(23), N, "g_node", "beta_node", 8, 2)
                link.done()
                with eng.Fori(0, NCH) as c:
                    link = Chain(eng, f_link, c * FL, FL)
                    cols_c = bass.ds(c * CW, CW)
                    link(nc.vector.tensor_scalar(stA[0:F, :], rT[:, cols_c], bcol(8), bcol(9), ALU.mult, ALU.add))
                    link(nc.vector.scalar_tensor_tensor(out=stA[0:F, :], in0=aggT[:, cols_c], scalar=bcol(0), in1=stA[0:F, :],
                                                        op0=ALU.mult, op1=ALU.add))
                    link(nc.vector.scalar_tensor_tensor(out=xT[0:F, :], in0=degT[:, cols_c], scalar=bcol(1), in1=stA[0:F, :],
                                                        op0=ALU.mult, op1=ALU.add))
                    eng.sem_inc(f_in, 1)
                    eng.wait_ge(f_T, c + 1)
                    link(nc.vector.tensor_tensor(tt3, ps23[:, 0:CB, 0:F], X[:, bass.ds(c * CB, CB), :], ALU.add))
                    done = layernorm(eng, link, sq3, c + ln0)
                    link(done)
                    eng.wait_ge(f_free, c + 1)
                    nc.vector.tensor_copy(ot3, sq3).then_inc(f_out, 1)
                    link.done()

            @block.tensor
            def _(eng):
                with eng.Fori(0, NCH) as c:
                    eng.wait_ge(f_in, c + 1)
                    for j in range(CB):
                        last = nc.tensor.transpose(ps23[:, j, 0:F], xT[0:F, j * P:(j + 1) * P], ident[0:F, 0:F])
                    last.then_inc(f_T, 1)

            @block.sync
            def _(eng):
                eng.sem_inc(f_free, 1)
                with eng.Fori(0, NCH - 1) as c:
                    eng.wait_ge(f_out, c + 2)
                    eng.dma_start(out[bass.ds(c * CW, CW), :].rearrange("(b p) f -> p b f", p=P), ot3).then_inc(f_dma, 16)
                    eng.wait_ge(f_dma, c * 16 + 16)
                    eng.sem_inc(f_free, 1)
                eng.wait_ge(f_out, NCH + 1)
                o = (NCH - 1) * CW
                eng.dma_start(out[o:(NB - 1) * P, :].rearrange("(b p) f -> p b f", p=P), ot3[:, 0:CB - 1, :]).then_inc(f_dma, 16)
                eng.dma_start(out[(NB - 1) * P:N, :], ot3[0:N - (NB - 1) * P, CB - 1, :]).then_inc(f_dma, 16)
                eng.wait_ge(f_dma, 16 * (NCH + 1))


MATS = ["L0W1", "L0W2", "L1Wl1T", "L1Wr1T", "L1Wl2T", "L1Wr2T", "L2WaT", "L2WbT", "Wnode", "Wsrc", "Wdst", "Wfeat"]
ROWS = ["L0b1", "L0b2", "L1bl1", "L1bl2", "L2b", "b_msg"]
COLS = ["b_edge", "g_edge", "beta_edge", "b_node", "g_node", "beta_node", "g_msg", "beta_msg"]


def kernel(**inputs):
    import numpy as np
    import concourse.bacc as bacc
    from concourse.bass_utils import run_bass_kernel_spmd as run

    a = {k: np.asarray(v) for k, v in inputs.items()}
    N, F = a["x"].shape
    E, FE = a["edge_attr_4"].shape
    W_msg = a["L3_gnn_W_msg"]
    mats = dict(zip(MATS, [
        a["L0_gnn_W1"], a["L0_gnn_W2"], a["L1_gnn_Wl1"].T, a["L1_gnn_Wr1"].T, a["L1_gnn_Wl2"].T, a["L1_gnn_Wr2"].T,
        a["L2_gnn_mlp_w"][:, :F].T, a["L2_gnn_mlp_w"][:, F:].T, a["L3_gnn_W_node"],
        W_msg[:F], W_msg[F:2 * F], W_msg[2 * F:]]))
    rows = {"L0b1": a["L0_gnn_b1"], "L0b2": a["L0_gnn_b2"], "L1bl1": a["L1_gnn_bl1"], "L1bl2": a["L1_gnn_bl2"],
            "L2b": a["L2_gnn_mlp_b"]}
    for part in ("edge", "node", "msg"):
        for kind in ("b", "g", "beta"):
            rows[f"{kind}_{part}"] = a[f"L3_gnn_{kind}_{part}"]

    nc = bacc.Bacc("TRN2", target_bir_lowering=False, num_devices=1)
    arrays = {}

    def given(name, array):
        array = np.ascontiguousarray(array)
        arrays[f"in_{name}"] = array
        return nc.dram_tensor(f"in_{name}", array.shape, mybir.dt.from_np(array.dtype), kind="ExternalInput").ap()

    x, src, dst = given("x", a["x"]), given("src", a["src"]), given("dst", a["dst"])
    ea, ew = given("edge_attr", a["edge_attr_4"]), given("edge_weight", a["edge_weight"])
    mats_dram = {k: given(k, v) for k, v in mats.items()}
    rows_dram = {k: given(k, v) for k, v in rows.items()}
    w_edge = given("w_edge", a["L3_gnn_W_edge"])
    out = nc.dram_tensor("out_x", (N, F), mybir.dt.float32, kind="ExternalOutput").ap()
    build(nc, x, src, dst, ea, ew, mats_dram, rows_dram, ROWS, COLS, w_edge, out, N, E, F, FE)
    return run(nc, [arrays], core_ids=[0]).results[0]["out_x"]
```

```python
import concourse.bass as bass
from concourse import mybir
from contextlib import ExitStack


def build(nc, x, src, dst, ea, ew, mats_dram, rows_dram, bias_rows, cols, w_edge, out, N, E, F, FE):
    mats = list(mats_dram)
    fp32, bf16, i32 = mybir.dt.float32, mybir.dt.bfloat16, mybir.dt.int32
    ALU, ACT, AX = mybir.AluOpType, mybir.ActivationFunctionType, mybir.AxisListType
    P, U = 128, 8
    GE = P * U
    NG = -(-E // GE)
    NG += NG % 2
    FULL = E // GE
    REST = E - FULL * GE
    NPAD_E = NG * GE - E
    NB = -(-N // P)
    CB = 7
    assert NB % CB == 0 and F % 32 == 0 and F < P
    NCH = NB // CB
    CW = CB * P
    NP = NB * P
    AW = NP + P
    MAXK = -(-N // P) + 1
    EPS = 1e-5
    FAR = 1.0e6

    ctx = ExitStack()
    with ctx:
        def sb(name, shape, dt=fp32):
            return ctx.enter_context(nc.sbuf_tensor(name, shape, dt))

        def pb(name, shape, dt=fp32):
            return ctx.enter_context(nc.psum_tensor(name, shape, dt))

        def sem(name):
            return ctx.enter_context(nc.semaphore(name))

        table = nc.dram_tensor("table", (NP, F), fp32, kind="Internal").ap()
        qtable = nc.dram_tensor("qtable", (AW, F), fp32, kind="Internal").ap()
        degrow = nc.dram_tensor("degrow", (NB, P), fp32, kind="Internal").ap()

        idx_all = sb("idx_all", [P, NG, U], i32)
        dstrel = sb("dstrel", [P, NG, U])
        w_all = sb("w_all", [P, NG, U])
        UH, PARTS = U // 2, 6
        KE = PARTS * UH * FE
        ea6 = sb("ea6", [P, NG, 2 * KE], bf16)
        X = sb("X", [P, NB, F])
        TAB = sb("TAB", [P, NB, F])
        aggT = sb("aggT", [F, AW])
        spare = sb("spare", [P, NP])
        rT = spare[0:F, :]
        RB = spare[:, 0:NB * F].rearrange("p (b f) -> p b f", f=F)
        ea_all = spare[:, 0:NG * U * FE].rearrange("p (g c) -> p g c", c=U * FE)
        M = sb("M", [F, len(mats), F])
        brow = sb("brow", [1, len(bias_rows), F])
        col = sb("col", [F, len(cols)])
        w6 = sb("w6", [KE, UH, F], bf16)
        bias_bc = sb("bias_bc", [P, F])
        ident = sb("ident", [P, P])
        identb = sb("identb", [P, P], bf16)
        iota_bf = sb("iota_bf", [P, P], bf16)
        iota_i = sb("iota_i", [P, P], i32)
        iota0 = sb("iota0", [P, P])
        iotak = sb("iotak", [P, P])
        ones_row = sb("ones_row", [1, P])
        ones_fp = sb("ones_fp", [F, P])
        eps_col = sb("eps_col", [P, 1])
        one_col = sb("one_col", [P, 1])
        base_row = sb("base_row", [1, NG])
        base_run = sb("base_run", [1, NG])
        basek_i = sb("basek_i", [1, NG], i32)
        kcnt = sb("kcnt", [1, 1], i32)
        deg = sb("deg", [P, NB])
        dinv = sb("dinv", [P, NB])
        rdeg = sb("rdeg", [P, NB])
        est = sb("est", [F, 2])
        msq = sb("msq", [F, 1])
        crow = sb("crow", [1, F])
        idx_st = [sb(f"idx_st{i}", [P, U], i32) for i in range(2)]
        rows = [sb(f"rows{i}", [P, U, F]) for i in range(2)]
        oh = [sb(f"oh{i}", [P, U, P]) for i in range(2)]
        work = [sb(f"work{i}", [P, CB * P]) for i in range(4)]
        big = sb("big", [P, GE])
        big2 = sb("big2", [P, GE])
        big3 = sb("big3", [P, GE])
        work4 = TAB[:, :, :].rearrange("p b f -> p (b f)")
        ohb = sb("ohb", [P, U, P], bf16)
        ea_st = [sb(f"ea_st{i}", [P, 2 * KE], bf16) for i in range(2)]
        eaT = [sb(f"eaT{i}", [KE, 2, P], bf16) for i in range(2)]
        erst = [sb(f"erst{i}", [F, 2]) for i in range(2)]
        small = sb("small", [P, 64])
        valid = [sb(f"valid{i}", [P, U]) for i in range(2)]
        vtmp = sb("vtmp", [P, U])
        qwin = [sb(f"qwin{i}", [P, F]) for i in range(2)]

        ps01 = pb("ps01", [P, 8, P])
        ps23 = pb("ps23", [P, 8, P])
        ps45 = pb("ps45", [P, 8, P])
        ps6 = pb("ps6", [P, 512])
        ps7 = pb("ps7", [P, 512])

        def mat(name):
            return M[:, mats.index(name), :]

        def bias(name):
            return brow[0:1, bias_rows.index(name), :]

        def cvec(name):
            return col[:, cols.index(name):cols.index(name) + 1]

        class Chain:

            def __init__(self, eng, semaphore, base, length):
                self.eng, self.sem, self.base, self.length, self.n = eng, semaphore, base, length, 0

            def __call__(self, ins):
                self.n += 1
                ins.then_inc(self.sem, 1)
                self.eng.wait_ge(self.sem, self.base + self.n)

            def done(self):
                assert self.n == self.length, (self.n, self.length)

        act_gate, pool_gate, dve_gate = sem("act_gate"), sem("pool_gate"), sem("dve_gate")

        s_pad, s_load, s_w, s_const, s_min = sem("s_pad"), sem("s_load"), sem("s_w"), sem("s_const"), sem("s_min")
        s_pe0, s_dv0 = sem("s_pe0"), sem("s_dv0")
        idx_staged, oh_ready, summed, acc_done = sem("idx_staged"), sem("oh_ready"), sem("summed"), sem("acc_done")
        gathered = [sem("gathered0"), sem("gathered1")]
        k_link, oh_cmp = sem("k_link"), sem("oh_cmp")
        ea_ready, eaT_ps, eaT_sb, er_ps = sem("ea_ready"), sem("eaT_ps"), sem("eaT_sb"), sem("er_ps")
        er_stat, est_done = sem("er_stat"), sem("est_done")
        dst_i = TAB[:, :, :].rearrange("p b f -> p (b f)").bitcast(i32)[:, 0:NG * U].rearrange("p (g u) -> p g u", u=U)
        gmm = work[0]
        wf = big[0:KE, 0:UH * F].rearrange("p (u f) -> p u f", f=F)
        wm = big2[0:KE, 0:UH * F].rearrange("p (u f) -> p u f", f=F)
        wpart = big3[0:KE, 0:UH * F].rearrange("p (u f) -> p u f", f=F)
        rowsel = small[0:KE, 8:11]
        s_wf, s_ea, s_ea_act, s_w6 = sem("s_wf"), sem("s_ea"), sem("s_ea_act"), sem("s_w6")
        ea_rest = work4[:, NG * U:NG * U * (FE + 1)].rearrange("p (g c) -> p g c", c=U * FE)
        ea_h = [ea6[:, :, h * KE:(h + 1) * KE].rearrange("p g (c u f) -> p g c (u f)", c=PARTS, f=FE) for h in range(2)]
        FP, FR = REST // U, REST % U

        def edge_dmas(eng, d3, s1, width, s_done):
            n = 0
            if FULL:
                eng.dma_start(d3[:, 0:FULL, :], s1[0:FULL * GE * width].rearrange("(g p u) -> p g u", p=P, u=U * width)).then_inc(s_done, 16)
                n += 16
            if FP:
                o = FULL * GE * width
                eng.dma_start(d3[0:FP, FULL, :], s1[o:o + FP * U * width].rearrange("(p u) -> p u", p=FP)).then_inc(s_done, 16)
                n += 16
            if FR:
                o = (FULL * GE + FP * U) * width
                eng.dma_start(d3[FP:FP + 1, FULL, 0:FR * width], s1[o:o + FR * width].rearrange("(p u) -> p u", p=1)).then_inc(s_done, 16)
                n += 16
            return n

        s_dst, s_hl, d_hi, d_lo, d_sum, d_acc = sem("s_dst"), sem("s_hl"), sem("d_hi"), sem("d_lo"), sem("d_sum"), sem("d_acc")
        hl_i = work[2][:, 0:NG * U].bitcast(i32)
        lo_f = work[3][:, 0:NG * U].rearrange("p (g u) -> p g u", u=U)
        hi_b = ohb[:, :, :].rearrange("p u n -> p (u n)")[:, 0:NG * U].rearrange("p (g u) -> p g u", u=U)
        iota_b = iota_bf[:, :]
        oh_lo = [oh[r][:, :, :].rearrange("p u n -> p (u n)").bitcast(bf16)[:, 0:GE].rearrange("p (u n) -> p u n", n=P) for r in range(2)]
        oh_hi = [oh[r][:, :, :].rearrange("p u n -> p (u n)").bitcast(bf16)[:, GE:GE + U * NB].rearrange("p (u n) -> p u n", n=NB) for r in range(2)]
        DL = 5

        with nc.Block() as block:
            @block.gpsimd
            def _(eng):
                eng.memset(idx_all[:, FULL:NG, :], 0).then_inc(s_pad, 1)
                eng.memset(dst_i[:, FULL:NG, :], int(FAR)).then_inc(s_pad, 1)
                eng.memset(w_all[:, FULL:NG, :], 0.0).then_inc(s_pad, 1)
                eng.memset(ea_all[:, FULL:NG, :], 0.0).then_inc(s_pad, 1)
                eng.memset(X[:, NB - 1:NB, :], 0.0).then_inc(s_pad, 1)
                eng.memset(wf, 0.0).then_inc(s_pad, 1)
                eng.memset(ident[:, :], 0.0).then_inc(s_const, 1)
                eng.memset(ones_row[:, :], 1.0).then_inc(s_const, 1)
                eng.memset(eps_col[:, :], EPS).then_inc(s_const, 1)
                eng.memset(one_col[:, :], 1.0).then_inc(s_const, 1)
                eng.iota(iota_i[:, :], pattern=[[1, P]], base=0, channel_multiplier=0).then_inc(s_const, 1)
                eng.memset(rowsel, 1.0).then_inc(s_const, 1)
                eng.wait_ge(s_const, 6)
                CU = UH * FE
                for sel, lo, hi in ((0, 0, 3 * CU), (1, 3 * CU, 5 * CU), (2, 5 * CU, 6 * CU)):
                    eng.affine_select(out=rowsel[:, sel:sel + 1], in_=rowsel[:, sel:sel + 1], compare_op=ALU.is_ge, fill=0.0,
                                      base=-lo, pattern=[[0, 1]], channel_multiplier=1).then_inc(s_w6, 1)
                    eng.wait_ge(s_w6, 2 * sel + 1)
                    eng.affine_select(out=rowsel[:, sel:sel + 1], in_=rowsel[:, sel:sel + 1], compare_op=ALU.is_ge, fill=0.0,
                                      base=hi - 1, pattern=[[0, 1]], channel_multiplier=-1).then_inc(s_w6, 1)
                    eng.wait_ge(s_w6, 2 * sel + 2)
                eng.affine_select(out=ident[:, :], in_=ident[:, :], compare_op=ALU.not_equal, fill=1.0,
                                  base=0, pattern=[[-1, P]], channel_multiplier=1).then_inc(s_const, 1)

            @block.sync
            def _(eng):
                eng.wait_ge(s_pad, 6)
                d = edge_dmas(eng, dst_i, dst, 1, s_dst)
                eng.wait_ge(s_dst, d)
                eng.sem_inc(s_min, 1)
                n = edge_dmas(eng, idx_all, src, 1, s_load)
                eng.dma_start(X[:, 0:NB - 1, :], x[0:(NB - 1) * P, :].rearrange("(b p) f -> p b f", p=P)).then_inc(s_w, 16)
                eng.dma_start(X[0:N - (NB - 1) * P, NB - 1, :], x[(NB - 1) * P:N, :]).then_inc(s_w, 16)
                m = edge_dmas(eng, w_all, ew, 1, s_w) + 32
                m += edge_dmas(eng, ea_all, ea.rearrange("e c -> (e c)"), FE, s_w)
                for i, name in enumerate(mats):
                    eng.dma_start(M[:, i, :], mats_dram[name]).then_inc(s_w, 16)
                for i, name in enumerate(bias_rows):
                    eng.dma_start(brow[0:1, i, :], rows_dram[name].rearrange("(a f) -> a f", a=1)).then_inc(s_w, 16)
                for i, name in enumerate(cols):
                    eng.dma_start(col[:, i:i + 1], rows_dram[name].rearrange("(f a) -> f a", a=1)).then_inc(s_w, 16)
                for c in range(PARTS):
                    for u in range(UH):
                        o = (c * UH + u) * FE
                        eng.dma_start(wf[o:o + FE, u, :], w_edge).then_inc(s_w, 16)
                m += 16 * (len(mats) + len(bias_rows) + len(cols) + PARTS * UH)
                eng.wait_ge(s_load, n)
                eng.wait_ge(s_w, m)
                eng.sem_inc(s_min, 1)

            @block.vector
            def _(eng):
                eng.sem_inc(acc_done, 2)
                eng.sem_inc(est_done, 2)
                eng.wait_ge(s_min, 1)
                eng.wait_ge(s_const, 7)
                eng.sem_inc(d_acc, 2)
                hl = Chain(eng, s_hl, 0, DL)
                dflat = dst_i.rearrange("p g u -> p (g u)")
                hl(nc.vector.tensor_scalar(hl_i, dflat, P.bit_length() - 1, None, ALU.logical_shift_right))
                hl(nc.vector.tensor_copy(hi_b.rearrange("p g u -> p (g u)"), hl_i))
                hl(nc.vector.tensor_scalar(hl_i, dflat, P - 1, None, ALU.bitwise_and))
                hl(nc.vector.tensor_copy(lo_f.rearrange("p g u -> p (g u)"), hl_i))
                hl(nc.vector.tensor_copy(iota_b, iota_i[:, :]))
                hl.done()
                with eng.Fori(0, NG // 2) as i:
                    for r in range(2):
                        g = i * 2 + r
                        eng.wait_ge(d_sum, g + 1)
                        for u in range(U):
                            last = nc.vector.tensor_scalar(oh_lo[r][:, u, :], iota_b,
                                                           lo_f[:, bass.ds(g, 1), u:u + 1].rearrange("p a b -> p (a b)"), None, ALU.is_equal)
                        last.then_inc(d_lo, 1)
                        nc.vector.tensor_tensor(oh_hi[r], iota_b[:, 0:NB].unsqueeze(1).to_broadcast([P, U, NB]),
                                                hi_b[:, bass.ds(g, 1), :].rearrange("p a u -> p (a u)").unsqueeze(2).to_broadcast([P, U, NB]),
                                                ALU.is_equal).then_inc(d_hi, 1)
                eng.wait_ge(d_sum, NG + 2)
                nc.vector.tensor_copy(deg[:, :], ps45[:, 0, 0:NB]).then_inc(d_acc, 1)
                eng.wait_ge(s_min, 2)
                link = Chain(eng, s_dv0, 0, 15 + 4 + 9)
                link(nc.vector.tensor_copy(iota0[:, :], iota_i[:, :]))
                link(nc.vector.tensor_copy(identb[:, :], ident[:, :]))
                link(nc.vector.tensor_copy(dstrel[:, :, :], dst_i[:, :, :]))
                link(nc.vector.tensor_reduce(gmm[:, 0:NG], dstrel[:, :, :], AX.X, ALU.min))
                m3 = work[1][:, 0:NG * U].rearrange("p (g u) -> p g u", u=U)
                link(nc.vector.scalar_tensor_tensor(out=m3, in0=dstrel[:, :, :], scalar=FAR, in1=dstrel[:, :, :],
                                                    op0=ALU.is_lt, op1=ALU.mult))
                link(nc.vector.tensor_reduce(gmm[:, NG:2 * NG], m3, AX.X, ALU.max))
                eng.wait_ge(s_pe0, 1)
                link(nc.vector.tensor_reduce(small[0:NG, 0:1], ps01[0:NG, 0, 0:P], AX.X, ALU.min))
                link(nc.vector.tensor_reduce(small[0:NG, 1:2], ps01[0:NG, 4, 0:P], AX.X, ALU.max))
                eng.wait_ge(s_pe0, 2)
                link(nc.vector.tensor_copy(base_row[0:1, :], ps6[0:1, 0:NG]))
                link(nc.vector.tensor_tensor(base_run[0:1, :], ps7[0:1, 0:NG], base_row[0:1, :], ALU.subtract))
                link(nc.vector.tensor_reduce(small[0:1, 2:3], base_run[0:1, :], AX.X, ALU.max))
                link(nc.vector.tensor_copy(kcnt[0:1, :], small[0:1, 2:3]))
                link(nc.vector.tensor_scalar(kcnt[0:1, :], kcnt[0:1, :], P.bit_length() - 1, None, ALU.logical_shift_right))
                link(nc.vector.tensor_scalar(kcnt[0:1, :], kcnt[0:1, :], 1.0, None, ALU.add))
                eng.wait_ge(s_pe0, 3)
                link(nc.vector.tensor_tensor(dstrel[:, :, :], dstrel[:, :, :],
                                             ps6[:, 0:NG].unsqueeze(2).to_broadcast([P, NG, U]), ALU.subtract))
                def less(part, n, out, full):
                    eng.wait_ge(s_ea_act, n)
                    for h in range(2):
                        f4 = full.rearrange("p g (h c) -> p g h c", h=2)[:, :, h, :]
                        o4 = out.rearrange("p g (h c) -> p g h c", h=2)[:, :, h, :]
                        link(nc.vector.tensor_tensor(o4, f4, ea_h[h][:, :, part, :], ALU.subtract))
                    eng.sem_inc(s_ea, 1)
                less(0, 2, ea_rest, ea_all)
                less(1, 4, ea_rest, ea_rest)
                eng.wait_ge(s_w6, 6)
                link(nc.vector.tensor_copy(w6[:, :, :], wf))
                link(nc.vector.tensor_tensor(wm, wf, w6[:, :, :], ALU.subtract))
                link(nc.vector.tensor_scalar(wpart, w6[:, :, :], rowsel[:, 0:1], None, ALU.mult))
                link(nc.vector.tensor_copy(w6[:, :, :], wm))
                link(nc.vector.tensor_tensor(wf, wm, w6[:, :, :], ALU.subtract))
                link(nc.vector.scalar_tensor_tensor(out=wpart, in0=w6[:, :, :], scalar=rowsel[:, 1:2], in1=wpart, op0=ALU.mult, op1=ALU.add))
                link(nc.vector.tensor_copy(w6[:, :, :], wf))
                link(nc.vector.scalar_tensor_tensor(out=wpart, in0=w6[:, :, :], scalar=rowsel[:, 2:3], in1=wpart, op0=ALU.mult, op1=ALU.add))
                link(nc.vector.tensor_copy(w6[:, :, :], wpart))
                link.done()

            @block.scalar
            def _(eng):
                eng.sem_inc(eaT_sb, 1)
                eng.sem_inc(er_stat, 1)
                eng.wait_ge(s_min, 2)
                for part, src4, after in ((0, ea_all, 0), (1, ea_rest, 1), (2, ea_rest, 2)):
                    if after:
                        eng.wait_ge(s_ea, after)
                    for h in range(2):
                        nc.scalar.activation(ea_h[h][:, :, part, :], src4.rearrange("p g (h c) -> p g h c", h=2)[:, :, h, :],
                                             ACT.Copy).then_inc(s_ea_act, 1)
                eng.wait_ge(s_ea_act, 6)
                for dest, part in ((3, 0), (4, 1), (5, 0)):
                    for h in range(2):
                        nc.scalar.activation(ea_h[h][:, :, dest, :], ea_h[h][:, :, part, :], ACT.Copy).then_inc(s_ea_act, 1)
                eng.wait_ge(s_ea_act, 12)

            @block.tensor
            def _(eng):
                eng.sem_inc(summed, 2)
                eng.sem_inc(eaT_ps, 2)
                eng.sem_inc(d_sum, 2)
                def count(r, first=False, end=False):
                    for u in range(U):
                        last = nc.tensor.matmul(ps45[:, 0, 0:NB], oh_lo[r][:, u, :], oh_hi[r][:, u, :],
                                                start=first and u == 0, stop=end and u == U - 1, skip_group_check=True)
                    last.then_inc(d_sum, 1)
                for g in range(2):
                    eng.wait_ge(d_lo, g + 1)
                    eng.wait_ge(d_hi, g + 1)
                    count(g, first=g == 0)
                with eng.Fori(1, NG // 2 - 1) as i:
                    for r in range(2):
                        eng.wait_ge(d_lo, i * 2 + (r + 1))
                        eng.wait_ge(d_hi, i * 2 + (r + 1))
                        count(r)
                for r in range(2):
                    eng.wait_ge(d_lo, NG - 1 + r)
                    eng.wait_ge(d_hi, NG - 1 + r)
                    count(r, end=r == 1)
                eng.wait_ge(s_dv0, 6)
                nc.tensor.transpose(ps01[0:NG, 0, 0:P], gmm[:, 0:NG], ident[:, :])
                nc.tensor.transpose(ps01[0:NG, 4, 0:P], gmm[:, NG:2 * NG], ident[:, :]).then_inc(s_pe0, 1)
                eng.wait_ge(s_dv0, 8)
                nc.tensor.transpose(ps6[0:1, 0:NG], small[0:NG, 0:1], ident[0:NG, 0:NG])
                nc.tensor.transpose(ps7[0:1, 0:NG], small[0:NG, 1:2], ident[0:NG, 0:NG]).then_inc(s_pe0, 1)
                eng.wait_ge(s_dv0, 14)
                nc.tensor.matmul(ps6[:, 0:NG], ones_row[0:1, :], base_row[0:1, :], start=True, stop=True).then_inc(s_pe0, 1)

        def passes(eng):
            return eng.value_load(kcnt[0:1, 0:1], min_val=1, max_val=MAXK)

        def one_hot(eng, dest, g, offsets):
            return nc.vector.tensor_tensor(dest, offsets[:, :].unsqueeze(1).to_broadcast([P, U, P]),
                                           dstrel[:, bass.ds(g, 1), :].rearrange("p a u -> p (a u)").unsqueeze(2).to_broadcast([P, U, P]),
                                           ALU.is_equal)

        def start_pass(link):
            link(nc.vector.tensor_scalar(basek_i[0:1, :], base_run[0:1, :], float(NP), None, ALU.min))

        def end_pass(link):
            link(nc.vector.tensor_scalar(base_run[0:1, :], base_run[0:1, :], float(P), None, ALU.add))
            link(nc.vector.tensor_scalar(iotak[:, :], iotak[:, :], float(P), None, ALU.add))

        def start_phase(link, target):
            link(nc.vector.memset(target[:, :], 0.0))
            link(nc.vector.tensor_copy(iotak[:, :], iota0[:, :]))
            link(nc.vector.tensor_copy(base_run[0:1, :], base_row[0:1, :]))
            link.eng.sem_inc(dve_gate, 1)

        def accumulate(eng, target, g, ps):
            at = eng.value_load(basek_i[0:1, bass.ds(g, 1)], min_val=0, max_val=NP)
            return lambda: nc.vector.tensor_tensor(target[:, bass.ds(at, P)], target[:, bass.ds(at, P)], ps, ALU.add)

        nd_staged, nd_T, nd_xT, nd_mm, nd_evac = sem("nd_staged"), sem("nd_T"), sem("nd_xT"), sem("nd_mm"), sem("nd_evac")
        nd_bias, nd_agg, nd_sum, nd_read, nd_out = sem("nd_bias"), sem("nd_agg"), sem("nd_sum"), sem("nd_read"), sem("nd_out")
        nd_dma, nd_link, nd_var, nd_sd, c_link = sem("nd_dma"), sem("nd_link"), sem("nd_var"), sem("nd_sd"), sem("c_link")
        t_sd, t_tab, t_link, t_dma, t_row = sem("t_sd"), sem("t_tab"), sem("t_link"), sem("t_dma"), sem("t_row")
        with nc.Block() as block:
            @block.scalar
            def _(eng):
                eng.activation(dinv[:, :], deg[:, :], ACT.Sqrt, bias=one_col[:, 0:1]).then_inc(t_sd, 1)

            @block.vector
            def _(eng):
                link = Chain(eng, t_link, 0, 3)
                eng.sem_inc(nd_read, 2)
                eng.sem_inc(nd_out, 2)
                eng.wait_ge(t_row, 1)
                nc.vector.tensor_copy(work[3][0:NB, 0:P], ps6[0:NB, 0:P]).then_inc(t_row, 1)
                eng.wait_ge(t_sd, 1)
                link(nc.vector.reciprocal(dinv[:, :], dinv[:, :]))
                link(nc.vector.tensor_scalar(rdeg[:, :], deg[:, :], 1.0, None, ALU.max))
                link(nc.vector.reciprocal(rdeg[:, :], rdeg[:, :]))
                link.done()
                nc.vector.tensor_tensor(TAB[:, :, :], X[:, :, :], dinv[:, :].unsqueeze(2).to_broadcast([P, NB, F]), ALU.mult).then_inc(t_tab, 1)

            @block.sync
            def _(eng):
                eng.wait_ge(t_row, 2)
                eng.dma_start(degrow[:, :], work[3][0:NB, 0:P]).then_inc(t_dma, 16)
                eng.wait_ge(t_tab, 1)
                eng.dma_start(table.rearrange("(b p) f -> p b f", p=P), TAB[:, :, :]).then_inc(t_dma, 16)
                eng.wait_ge(t_dma, 32)

            @block.tensor
            def _(eng):
                nc.tensor.transpose(ps6[0:NB, 0:P], deg[:, :], ident[:, :]).then_inc(t_row, 1)
                eng.sem_inc(nd_mm, 1)
                eng.sem_inc(nd_sum, 2)

        er_relu, deg_dma = sem("er_relu"), sem("deg_dma")

        stN, xT = work[1], work[2]
        stN3 = stN[:, 0:CB * F].rearrange("p (b f) -> p b f", f=F)
        sumT = [work[0], work[2]]
        sq3 = big3[:, 0:CB * F].rearrange("p (b f) -> p b f", f=F)
        ttr = [work[1][:, 0:CB * F].rearrange("p (b f) -> p b f", f=F), work[3][:, 0:CB * F].rearrange("p (b f) -> p b f", f=F)]
        s1r, v1r = [small[:, 0:CB], small[:, 8:8 + CB]], [small[:, 16:16 + CB], small[:, 24:24 + CB]]
        ea_ps2 = ps01[0:KE, 0, :].bitcast(bf16).rearrange("p (h e) -> p h e", h=2)
        psA = [ps01, ps23]

        def bc(ap):
            return ap.unsqueeze(2).to_broadcast([P, CB, F])

        LN_FIRST, LN_SECOND = 5, 1

        def ln_first(link, tt3, s1, v1):
            link(nc.vector.tensor_reduce(s1, tt3, AX.X, ALU.add))
            link(nc.vector.tensor_scalar(s1, s1, 1.0 / F, None, ALU.mult))
            link(nc.vector.tensor_tensor(tt3, tt3, bc(s1), ALU.subtract))
            link(nc.vector.tensor_tensor(sq3, tt3, tt3, ALU.mult))
            link(nc.vector.tensor_reduce(v1, sq3, AX.X, ALU.add))

        def ln_second(eng, link, result, tt3, v1, root):
            eng.wait_ge(nd_sd, root + 1)
            link(nc.vector.reciprocal(v1, v1))
            return nc.vector.tensor_tensor(result, tt3, bc(v1), ALU.mult)

        def stddev(eng, v1, root):
            eng.wait_ge(nd_var, root + 1)
            nc.scalar.activation(v1, v1, ACT.Sqrt, bias=eps_col[:, 0:1], scale=1.0 / F).then_inc(nd_sd, 1)

        roots, links = [0], [0]

        def layer(ph, node, W_agg, W_node, bias_name, scale, node_scale, relu, residual, weighted=False, edge_stats=False, prelude=None):
            early = residual and not relu
            first_n = (1 if scale is not None else 0) + 1 + (1 if relu and residual else 0) + (LN_FIRST if residual else 0)
            second_n = LN_SECOND if residual else 0
            per_chunk = first_n + second_n
            link0, root0 = links[0], roots[0]
            links[0] += NCH * per_chunk
            roots[0] += NCH if residual else 0

            def at(k, K, g):
                return (k + K * ph) * NG + g

            def chunk_no(k, K, i):
                return (k + K * ph) * NCH + i

            with nc.Block() as block:
                @block.gpsimd
                def _(eng):
                    K = passes(eng)
                    with eng.Fori(0, K) as k:
                        with eng.Fori(0, NG // 2) as i:
                            for r in range(2):
                                eng.wait_ge(idx_staged, at(k, K, i * 2 + r) + 1)
                                eng.sem_inc(pool_gate, 1)
                                for u in range(U):
                                    eng.indirect_dma_start(
                                        out=rows[r][:, u, :], out_offset=None, in_=table[:, :],
                                        in_offset=bass.IndirectOffsetOnAxis(ap=idx_st[r][:, u:u + 1], axis=0)).then_inc(gathered[r], 16)

                @block.scalar
                def _(eng):
                    K = passes(eng)
                    if prelude:
                        prelude("scalar", eng)

                    def pair(k, i, with_chunk):
                        for r in range(2):
                            g = i * 2 + r
                            eng.wait_ge(summed, at(k, K, g) + 1)
                            eng.sem_inc(act_gate, 1)
                            nc.scalar.activation(idx_st[r][:, :], idx_all[:, bass.ds(g, 1), :].rearrange("p a u -> p (a u)"),
                                                 ACT.Copy).then_inc(idx_staged, 1)
                        if with_chunk:
                            n = chunk_no(k, K, i)
                            eng.wait_ge(nd_mm, n + 1)
                            eng.sem_inc(act_gate, 1)
                            nc.scalar.activation(stN3, node[:, bass.ds(i * CB, CB), :], ACT.Copy).then_inc(nd_staged, 1)
                            eng.wait_ge(nd_T, n + 1)
                            nc.scalar.activation(xT[0:F, :], ps45[0:F, 0:CB, :].rearrange("p b n -> p (b n)"), ACT.Copy).then_inc(nd_xT, 1)
                        for r in range(2 * edge_stats):
                            n = k * NG + i * 2 + r
                            eng.wait_ge(eaT_ps, n + 3)
                            nc.scalar.activation(eaT[r][:, :, :], ea_ps2, ACT.Copy).then_inc(eaT_sb, 1)
                            eng.wait_ge(er_ps, n + 1)
                            eng.wait_ge(est_done, n + 1)
                            nc.scalar.activation(big[0:F, :], ps23[0:F, :, :].rearrange("p u e -> p (u e)"), ACT.Relu,
                                                 bias=cvec("b_edge"), accum_out=erst[r][:, 0:1]).then_inc(er_relu, 1)
                            eng.wait_ge(er_relu, n + 1)
                            nc.scalar.activation(big2[0:F, :], big[0:F, :], ACT.Square,
                                                 accum_out=erst[r][:, 1:2]).then_inc(er_stat, 1)

                    with eng.Fori(0, K) as k:
                        with eng.Fori(0, NCH) as i:
                            pair(k, i, True)
                        with eng.Fori(NCH, NG // 2) as i:
                            pair(k, i, False)

                    def stage(c, r):
                        eng.wait_ge(nd_sum, c + (ph * NCH + 1))
                        eng.sem_inc(act_gate, 1)
                        nc.scalar.activation(sumT[r][0:F, :], aggT[:, bass.ds(c * CW, CW)], ACT.Copy).then_inc(nd_agg, 1)

                    eng.wait_ge(acc_done, K * ((ph + 1) * NG) + 2)
                    eng.sem_inc(act_gate, 1)
                    stage(0, 0)
                    with eng.Fori(0, NCH // 2) as i:
                        for d in range(2):
                            c, r = i * 2 + (1 + d), (1 + d) % 2
                            stage(c, r)
                            if residual:
                                stddev(eng, v1r[1 - r], c + (root0 - 1))
                    if residual:
                        stddev(eng, v1r[0], NCH - 1 + root0)

                @block.vector
                def _(eng):
                    K = passes(eng)
                    link = Chain(eng, k_link, K * (ph * 4) + ph * 4, 4)
                    start_phase(link, aggT)
                    eng.wait_ge(nd_bias, ph + 1)
                    link(nc.vector.tensor_copy(bias_bc[:, :], ps45[:, 0, 0:F]))
                    link.done()
                    eng.sem_inc(nd_evac, 1)
                    if prelude:
                        prelude("vector", eng)

                    def pair(k, i, with_chunk):
                        for r in range(2):
                            g = i * 2 + r
                            eng.wait_ge(summed, at(k, K, g) + 1)
                            if weighted:
                                for u in range(U):
                                    last = nc.vector.tensor_scalar(
                                        oh[r][:, u, :], iotak[:, :],
                                        dstrel[:, bass.ds(g, 1), u:u + 1].rearrange("p a b -> p (a b)"),
                                        w_all[:, bass.ds(g, 1), u:u + 1].rearrange("p a b -> p (a b)"), ALU.is_equal, ALU.mult)
                                last.then_inc(oh_ready, 1)
                            else:
                                one_hot(eng, oh[r][:, :, :], g, iotak).then_inc(oh_ready, 1)
                            if edge_stats:
                                eng.wait_ge(eaT_ps, k * NG + g + 1)
                                nc.vector.tensor_scalar(ea_st[r][:, :], ea6[:, bass.ds(g, 1), :].rearrange("p a c -> p (a c)"),
                                                        1.0, None, ALU.mult).then_inc(ea_ready, 1)
                        if with_chunk:
                            rb, cb = RB[:, bass.ds(i * CB, CB), :], bass.ds(i * CB, CB)
                            n = chunk_no(k, K, i)
                            bbc = bias_bc[:, :].unsqueeze(1).to_broadcast([P, CB, F])
                            eng.wait_ge(nd_mm, n + 2)
                            clink = Chain(eng, c_link, n * 3, 3)
                            if node_scale is None:
                                clink(nc.vector.tensor_tensor(rb, ps45[:, 0:CB, 0:F], bbc, ALU.add))
                            else:
                                clink(nc.vector.tensor_tensor(rb, ps45[:, 0:CB, 0:F], bc(node_scale[:, cb]), ALU.mult))
                            eng.sem_inc(nd_evac, 1)
                            if node_scale is not None:
                                clink(nc.vector.tensor_tensor(rb, rb, bbc, ALU.add))
                            if early:
                                clink(nc.vector.tensor_tensor(rb, rb, X[:, cb, :], ALU.add))
                            eng.sem_inc(c_link, clink.length - clink.n)
                        for r in range(2):
                            g = i * 2 + r
                            add = accumulate(eng, aggT, g, (ps6, ps7)[r][0:F, 0:P])
                            eng.wait_ge(summed, at(k, K, g) + 3)
                            eng.wait_ge(acc_done, at(k, K, g) + 2)
                            add().then_inc(acc_done, 1)
                            if edge_stats:
                                eng.wait_ge(er_stat, k * NG + g + 2)
                                eng.wait_ge(est_done, k * NG + g + 2)
                                nc.vector.tensor_tensor(est[:, :], est[:, :], erst[r][:, :], ALU.add).then_inc(est_done, 1)

                    with eng.Fori(0, K) as k:
                        link = Chain(eng, k_link, (k + K * ph) * 4 + (ph * 4 + 4), 4)
                        start_pass(link)
                        link(nc.vector.memset(est[:, :], 0.0)) if edge_stats else link(nc.vector.memset(msq[:, :], 0.0))
                        eng.sem_inc(dve_gate, 1)
                        with eng.Fori(0, NCH) as i:
                            pair(k, i, True)
                        with eng.Fori(NCH, NG // 2) as i:
                            pair(k, i, False)
                        eng.wait_ge(acc_done, at(k, K, NG) + 2)
                        if edge_stats:
                            eng.wait_ge(est_done, k * NG + NG + 2)
                        end_pass(link)
                        link.done()

                    def first(c, r, base):
                        n = c + ph * NCH
                        link = Chain(eng, nd_link, base, first_n)
                        tt3, cb = ttr[r], bass.ds(c * CB, CB)
                        eng.wait_ge(nd_sum, n + 3)
                        eng.wait_ge(nd_out, n + 1)
                        if scale is not None:
                            link(nc.vector.tensor_tensor(tt3, psA[r][:, 0:CB, 0:F], bc(scale[:, cb]), ALU.mult))
                            link(nc.vector.tensor_tensor(tt3, tt3, RB[:, cb, :], ALU.add))
                        else:
                            link(nc.vector.tensor_tensor(tt3, psA[r][:, 0:CB, 0:F], RB[:, cb, :], ALU.add))
                        eng.sem_inc(nd_read, 1)
                        if relu and residual:
                            link(nc.vector.scalar_tensor_tensor(out=tt3, in0=tt3, scalar=0.0, in1=X[:, cb, :], op0=ALU.max, op1=ALU.add))
                        if residual:
                            ln_first(link, tt3, s1r[r], v1r[r])
                            eng.sem_inc(nd_var, 1)
                        link.done()

                    def second(c, r, base):
                        n = c + ph * NCH
                        tt3, cb = ttr[r], bass.ds(c * CB, CB)
                        if residual:
                            link = Chain(eng, nd_link, base, 1)
                            ln_second(eng, link, X[:, cb, :], tt3, v1r[r], c + root0).then_inc(nd_out, 1)
                        elif node_scale is not None:
                            nc.vector.scalar_tensor_tensor(out=TAB[:, cb, :], in0=tt3, scalar=0.0, in1=bc(dinv[:, cb]),
                                                           op0=ALU.max, op1=ALU.mult).then_inc(nd_out, 1)
                        else:
                            nc.vector.tensor_scalar(TAB[:, cb, :], tt3, 0.0, None, ALU.max).then_inc(nd_out, 1)

                    if residual:
                        first(0, 0, link0)
                        with eng.Fori(0, NCH // 2) as i:
                            for d in range(2):
                                c, r = i * 2 + (1 + d), (1 + d) % 2
                                first(c, r, c * per_chunk + (link0 - 1))
                                second(c - 1, 1 - r, c * per_chunk + (link0 + 2 * first_n - per_chunk))
                        second(NCH - 1, 0, link0 + (NCH - 1) * per_chunk + first_n)
                    else:
                        first(0, 0, link0)
                        second(0, 0, None)
                        with eng.Fori(0, NCH // 2) as i:
                            for d in range(2):
                                c, r = i * 2 + (1 + d), (1 + d) % 2
                                first(c, r, c * per_chunk + link0)
                                second(c, r, None)

                @block.tensor
                def _(eng):
                    K = passes(eng)
                    nc.tensor.matmul(ps45[:, 0, 0:F], ones_row[0:1, :], bias(bias_name), start=True, stop=True).then_inc(nd_bias, 1)
                    if prelude:
                        prelude("tensor", eng)

                    def pair(k, i, with_chunk):
                        if with_chunk:
                            n = chunk_no(k, K, i)
                            eng.wait_ge(nd_staged, n + 1)
                            eng.wait_ge(nd_evac, n + (ph + 1))
                            for j in range(CB):
                                last = nc.tensor.transpose(ps45[0:F, j, :], stN3[:, j, :], ident[:, :])
                            last.then_inc(nd_T, 1)
                            eng.wait_ge(nd_xT, n + 1)
                            for j in range(CB):
                                last = nc.tensor.matmul(ps45[:, j, 0:F], xT[0:F, j * P:(j + 1) * P], mat(W_node), start=True, stop=True)
                            last.then_inc(nd_mm, 1)
                        for r in range(2):
                            g = i * 2 + r
                            if edge_stats:
                                n = k * NG + g
                                eng.wait_ge(ea_ready, n + 1)
                                eng.wait_ge(eaT_sb, n + 1)
                                nc.tensor.transpose(ea_ps2[:, 0, :], ea_st[r][:, 0:KE], identb[:, :])
                                nc.tensor.transpose(ea_ps2[:, 1, :], ea_st[r][:, KE:2 * KE], identb[:, :]).then_inc(eaT_ps, 1)
                                eng.wait_ge(eaT_sb, n + 2)
                                eng.wait_ge(er_stat, n + 1)
                                for u in range(U):
                                    last = nc.tensor.matmul(ps23[0:F, u, :], w6[:, u % UH, :], eaT[r][:, u // UH, :], start=True, stop=True)
                                last.then_inc(er_ps, 1)
                            eng.wait_ge(oh_ready, at(k, K, g) + 1)
                            eng.wait_ge(acc_done, at(k, K, g) + 1)
                            eng.wait_ge(gathered[r], ((k + K * ph) * (NG // 2) + i) * (16 * U) + 16 * U)
                            for u in range(U):
                                last = nc.tensor.matmul((ps6, ps7)[r][0:F, 0:P], rows[r][:, u, :], oh[r][:, u, :],
                                                        start=(u == 0), stop=(u == U - 1))
                            last.then_inc(summed, 1)

                    with eng.Fori(0, K) as k:
                        with eng.Fori(0, NCH) as i:
                            pair(k, i, True)
                        with eng.Fori(NCH, NG // 2) as i:
                            pair(k, i, False)

                    def product(c, r):
                        n = c + ph * NCH
                        eng.wait_ge(nd_agg, n + 1)
                        eng.wait_ge(nd_read, n + 1)
                        for j in range(CB):
                            last = nc.tensor.matmul(psA[r][:, j, 0:F], sumT[r][0:F, j * P:(j + 1) * P], mat(W_agg), start=True, stop=True)
                        last.then_inc(nd_sum, 1)

                    product(0, 0)
                    with eng.Fori(0, NCH // 2) as i:
                        for d in range(2):
                            product(i * 2 + (1 + d), (1 + d) % 2)

                @block.sync
                def _(eng):
                    new = X if residual else TAB
                    if prelude:
                        prelude("sync", eng)
                    with eng.Fori(0, NCH) as c:
                        eng.wait_ge(nd_out, c + (ph * NCH + 3))
                        eng.dma_start(table[bass.ds(c * CW, CW), :].rearrange("(b p) f -> p b f", p=P),
                                      new[:, bass.ds(c * CB, CB), :]).then_inc(nd_dma, 16)
                    eng.wait_ge(nd_dma, 16 * NCH * (ph + 1))

        bn = sb("bn", [F, 24])
        bn_sd, bn_pe, bn_link = sem("bn_sd"), sem("bn_pe"), sem("bn_link")
        BN_LINKS = 9

        def bcol(i):
            return bn[:, i:i + 1]

        def batchnorm(eng, link, total, square, count, gamma, beta, at, n):
            mean, var, tmp, scale, shift = bcol(at + 2), bcol(at + 3), bcol(at + 4), bcol(at), bcol(at + 1)
            link(nc.vector.tensor_scalar(mean, total, 1.0 / count, None, ALU.mult))
            link(nc.vector.tensor_scalar(var, square, 1.0 / count, None, ALU.mult))
            link(nc.vector.tensor_tensor(tmp, mean, mean, ALU.mult))
            link(nc.vector.tensor_tensor(var, var, tmp, ALU.subtract))
            link(nc.vector.tensor_scalar(var, var, 0.0, None, ALU.max))
            eng.sem_inc(bn_var, 1)
            eng.wait_ge(bn_sd, n + 1)
            link(nc.vector.reciprocal(var, var))
            link(nc.vector.tensor_tensor(scale, var, cvec(gamma), ALU.mult))
            link(nc.vector.tensor_tensor(tmp, mean, scale, ALU.mult))
            link(nc.vector.tensor_tensor(shift, cvec(beta), tmp, ALU.subtract))

        def batch_stddev(eng, at, n):
            eng.wait_ge(bn_var, n + 1)
            nc.scalar.activation(bcol(at + 3), bcol(at + 3), ACT.Sqrt, bias=eps_col[0:F, 0:1]).then_inc(bn_sd, 1)

        bn_var = sem("bn_var")


        def edge_constants(engine, eng):
            if engine == "scalar":
                batch_stddev(eng, 0, 0)
            if engine == "tensor":
                eng.wait_ge(bn_link, BN_LINKS + 4)
                nc.tensor.matmul(ps23[0:1, 0, 0:F], bcol(1), mat("Wfeat"), start=True, stop=True).then_inc(bn_pe, 1)
            if engine == "vector":
                link = Chain(eng, bn_link, 0, EDGE_LINKS)
                link(nc.vector.tensor_scalar(bcol(6), cvec("b_edge"), 0.0, None, ALU.max))
                link(nc.vector.tensor_tensor(bcol(7), bcol(6), bcol(6), ALU.mult))
                link(nc.vector.scalar_tensor_tensor(out=est[:, 0:1], in0=bcol(6), scalar=-float(NPAD_E), in1=est[:, 0:1],
                                                    op0=ALU.mult, op1=ALU.add))
                link(nc.vector.scalar_tensor_tensor(out=est[:, 1:2], in0=bcol(7), scalar=-float(NPAD_E), in1=est[:, 1:2],
                                                    op0=ALU.mult, op1=ALU.add))
                batchnorm(eng, link, est[:, 0:1], est[:, 1:2], E, "g_edge", "beta_edge", 0, 0)
                eng.wait_ge(bn_pe, 1)
                link(nc.vector.tensor_tensor(crow[0:1, :], ps23[0:1, 0, 0:F], bias("b_msg"), ALU.add))
                link(nc.vector.tensor_scalar(mat("Wfeat"), mat("Wfeat"), bcol(0), None, ALU.mult))
                link.done()

        EDGE_LINKS = BN_LINKS + 6

        layer(0, TAB, "L0W1", "L0W1", "L0b1", dinv, dinv, True, False, edge_stats=True)
        layer(1, TAB, "L0W2", "L0W2", "L0b2", dinv, dinv, True, True)
        layer(2, X, "L1Wl1T", "L1Wr1T", "L1bl1", rdeg, None, True, False)
        layer(3, TAB, "L1Wl2T", "L1Wr2T", "L1bl2", rdeg, None, False, True)
        layer(4, X, "L2WbT", "L2WaT", "L2b", None, None, False, True, weighted=True, prelude=edge_constants)
        qst3 = big[:, 0:CB * F].rearrange("p (b f) -> p b f", f=F)
        nodes = [work[0][:, 0:CB * F].rearrange("p (b f) -> p b f", f=F), work[1][:, 0:CB * F].rearrange("p (b f) -> p b f", f=F)]
        nodesT = [work[2], work[3]]
        p_in, p_T, p_xT, p_mm, p_p, p_q = sem("p_in"), sem("p_T"), sem("p_xT"), sem("p_mm"), sem("p_p"), sem("p_q")
        p_r, p_tab, p_pad, m_q = sem("p_r"), sem("p_tab"), sem("p_pad"), sem("m_q")
        with nc.Block() as block:
            @block.scalar
            def _(eng):
                def load(c, r):
                    eng.wait_ge(p_T, c + 1)
                    eng.sem_inc(act_gate, 1)
                    nc.scalar.activation(nodes[r], X[:, bass.ds(c * CB, CB), :], ACT.Copy).then_inc(p_in, 1)

                def copy_back(c, r):
                    eng.wait_ge(p_T, c + 3)
                    nc.scalar.activation(nodesT[r][0:F, :], ps01[0:F, 0:CB, :].rearrange("p b n -> p (b n)"), ACT.Copy).then_inc(p_xT, 1)

                def node_features(c):
                    eng.wait_ge(p_mm, c + 3)
                    eng.sem_inc(act_gate, 1)
                    nc.scalar.activation(rT[:, bass.ds(c * CW, 4 * P)], ps6[0:F, :], ACT.Relu, bias=cvec("b_node"))
                    nc.scalar.activation(rT[:, bass.ds(c * CW + 4 * P, CW - 4 * P)], ps7[0:F, 0:CW - 4 * P], ACT.Relu,
                                         bias=cvec("b_node")).then_inc(p_r, 1)

                load(0, 0)
                copy_back(0, 0)
                with eng.Fori(0, NCH // 2) as i:
                    for d in range(2):
                        c, r = i * 2 + (1 + d), (1 + d) % 2
                        load(c, r)
                        copy_back(c, r)
                        node_features(c - 1)
                node_features(NCH - 1)

            @block.tensor
            def _(eng):
                eng.sem_inc(p_T, 2)
                eng.sem_inc(p_mm, 2)

                def transposes(c, r):
                    eng.wait_ge(p_in, c + 1)
                    eng.wait_ge(p_xT, c + 1)
                    for j in range(CB):
                        last = nc.tensor.transpose(ps01[0:F, j, :], nodes[r][:, j, :], ident[:, :])
                    last.then_inc(p_T, 1)

                def products(c, r):
                    eng.wait_ge(p_xT, c + 2)
                    eng.wait_ge(p_p, c + 1)
                    eng.wait_ge(p_q, c + 1)
                    eng.wait_ge(p_r, c + 1)
                    for j in range(CB):
                        b = nodesT[r][0:F, j * P:(j + 1) * P]
                        nc.tensor.matmul(ps23[:, j, 0:F], b, mat("Wsrc"), start=True, stop=True)
                        nc.tensor.matmul(ps45[:, j, 0:F], b, mat("Wdst"), start=True, stop=False)
                        nc.tensor.matmul(ps45[:, j, 0:F], ones_row[0:1, :], crow[0:1, :], start=False, stop=True)
                    nc.tensor.matmul(ps6[0:F, :], mat("Wnode"), nodesT[r][0:F, 0:4 * P], start=True, stop=True)
                    nc.tensor.matmul(ps7[0:F, 0:CW - 4 * P], mat("Wnode"), nodesT[r][0:F, 4 * P:CW], start=True, stop=True).then_inc(p_mm, 1)

                eng.sem_inc(p_xT, 1)
                eng.sem_inc(p_r, 1)
                transposes(0, 0)
                with eng.Fori(0, NCH // 2) as i:
                    for d in range(2):
                        c, r = i * 2 + (1 + d), (1 + d) % 2
                        transposes(c, r)
                        products(c - 1, 1 - r)
                products(NCH - 1, 0)

            @block.vector
            def _(eng):
                eng.sem_inc(p_p, 1)
                eng.sem_inc(p_q, 1)
                nc.vector.memset(big2[:, 0:F], 0.0).then_inc(p_pad, 1)
                with eng.Fori(0, NCH) as c:
                    eng.wait_ge(p_mm, c + 3)
                    nc.vector.tensor_scalar(TAB[:, bass.ds(c * CB, CB), :], ps23[:, 0:CB, 0:F], 1.0, None, ALU.mult).then_inc(p_p, 1)
                    eng.wait_ge(m_q, c * 16 + 16)
                    nc.vector.tensor_copy(qst3, ps45[:, 0:CB, 0:F]).then_inc(p_q, 1)

            @block.sync
            def _(eng):
                eng.wait_ge(p_pad, 1)
                eng.dma_start(qtable[NP:AW, :], big2[:, 0:F]).then_inc(m_q, 16)
                with eng.Fori(0, NCH) as c:
                    eng.wait_ge(p_p, c + 2)
                    eng.dma_start(table[bass.ds(c * CW, CW), :].rearrange("(b p) f -> p b f", p=P),
                                  TAB[:, bass.ds(c * CB, CB), :]).then_inc(p_tab, 16)
                    eng.wait_ge(p_q, c + 2)
                    eng.dma_start(qtable[bass.ds(c * CW, CW), :].rearrange("(b p) f -> p b f", p=P), qst3).then_inc(m_q, 16)
                eng.wait_ge(p_tab, 16 * NCH)
                eng.wait_ge(m_q, 16 * NCH + 16)

        PH = 5
        v_link, sp_gate = sem("v_link"), sem("sp_gate")
        names = "oh ohb ea eaT eaTs ohT ohTs er ers pre hs relu h msq".split()
        q = {name: sem(f"q_{name}") for name in names}
        q_win = [sem("q_win0"), sem("q_win1")]
        q_pass, f_stat = sem("q_pass"), sem("f_stat")
        tabf = TAB[:, :, :].rearrange("p b f -> p (b f)")
        UF = U * F
        hbuf = [tabf[:, r * UF:(r + 1) * UF].rearrange("p (u f) -> p u f", f=F) for r in range(2)]
        sqbuf = [tabf[:, (2 + r) * UF:(3 + r) * UF].rearrange("p (u f) -> p u f", f=F) for r in range(2)]
        ohT_sb = big2[:, :].rearrange("p (u e) -> p u e", e=P)
        hsum = big3[:, 0:UF].rearrange("p (u f) -> p u f", f=F)
        ohT_ps = ps45[:, 0:4, :].rearrange("p b n -> p (b n)").bitcast(bf16).rearrange("p (u e) -> p u e", e=P)
        ea_ps = ps45[0:KE, 4, :].bitcast(bf16).rearrange("p (h e) -> p h e", h=2)
        with nc.Block() as block:
            def flat(ap):
                return ap.rearrange("p u e -> p (u e)")

            @block.gpsimd
            def _(eng):
                K = passes(eng)
                with eng.Fori(0, K) as k:
                    with eng.Fori(0, NG // 2) as i:
                        for r in range(2):
                            eng.wait_ge(idx_staged, (k + K * PH) * NG + i * 2 + r + 1)
                            eng.sem_inc(pool_gate, 1)
                            for u in range(U):
                                eng.indirect_dma_start(
                                    out=rows[r][:, u, :], out_offset=None, in_=table[:, :],
                                    in_offset=bass.IndirectOffsetOnAxis(ap=idx_st[r][:, u:u + 1], axis=0)).then_inc(gathered[r], 16)

            @block.sync
            def _(eng):
                K = passes(eng)
                with eng.Fori(0, K) as k:
                    eng.wait_ge(q_pass, k + 1)
                    eng.sem_inc(sp_gate, 1)
                    with eng.Fori(0, NG // 2) as i:
                        for r in range(2):
                            g = i * 2 + r
                            at = eng.value_load(basek_i[0:1, bass.ds(g, 1)], min_val=0, max_val=NP)
                            eng.wait_ge(q["pre"], k * NG + g + 1)
                            eng.dma_start(qwin[r][:, :], qtable[bass.ds(at, P), :]).then_inc(q_win[r], 16)

            @block.scalar
            def _(eng):
                K = passes(eng)
                for c in range(NCH):
                    w = min(CW, N - c * CW)
                    nc.scalar.activation(work[1][0:F, 0:w], rT[:, c * CW:c * CW + w], ACT.Square, accum_out=bn[:, 16 + c:17 + c]).then_inc(f_stat, 1)
                    eng.wait_ge(f_stat, c + 1)
                batch_stddev(eng, 8, 1)
                eng.sem_inc(act_gate, 1)
                with eng.Fori(0, K) as k:
                    def wait(name, g):
                        eng.wait_ge(q[name], k * NG + g + 3)

                    def stage(g, r):
                        wait("hs", g - 2)
                        eng.sem_inc(act_gate, 1)
                        nc.scalar.activation(idx_st[r][:, :], idx_all[:, bass.ds(g, 1), :].rearrange("p a u -> p (a u)"),
                                             ACT.Copy).then_inc(idx_staged, 1)

                    def operands(g, r):
                        wait("oh", g)
                        wait("ohT", g - 1)
                        nc.scalar.activation(flat(ohb[:, :, :]), flat(oh[r][:, :, :]), ACT.Copy).then_inc(q["ohb"], 1)
                        wait("eaT", g)
                        nc.scalar.activation(eaT[r][:, :, :], ea_ps, ACT.Copy).then_inc(q["eaTs"], 1)

                    def features(g, r):
                        wait("er", g)
                        wait("pre", g - 1)
                        nc.scalar.activation(big[0:F, :], flat(ps01[0:F, :, :]), ACT.Relu, bias=cvec("b_edge")).then_inc(q["ers"], 1)

                    def messages(g, r):
                        wait("hs", g)
                        eng.wait_ge(summed, (k + K * PH) * NG + g + 1)
                        nc.scalar.activation(flat(hbuf[r]), flat(hsum), ACT.Relu).then_inc(q["relu"], 1)
                        wait("relu", g)
                        nc.scalar.activation(flat(sqbuf[r]), flat(hbuf[r]), ACT.Square).then_inc(q["h"], 1)

                    stage(0, 0)
                    operands(0, 0)
                    features(0, 0)
                    stage(1, 1)
                    operands(1, 1)
                    messages(0, 0)
                    features(1, 1)
                    with eng.Fori(0, NG // 2 - 1) as i:
                        for d in range(2):
                            g, r = i * 2 + (1 + d), (1 + d) % 2
                            stage(g + 1, 1 - r)
                            operands(g + 1, 1 - r)
                            messages(g, r)
                            features(g + 1, 1 - r)
                    messages(NG - 1, 1)

            @block.vector
            def _(eng):
                K = passes(eng)
                eng.sem_inc(q["ea"], 2)
                for name in names:
                    if name != "ea":
                        eng.sem_inc(q[name], 2)
                link = Chain(eng, k_link, K * (PH * 4) + PH * 4, 3)
                start_phase(link, aggT)
                link.done()
                link = Chain(eng, bn_link, EDGE_LINKS, BN_LINKS + 3)
                link(nc.vector.memset(ones_fp[:, :], 1.0))
                link(nc.vector.tensor_reduce(bcol(15), rT[:, 0:N], AX.X, ALU.add))
                eng.wait_ge(f_stat, NCH)
                link(nc.vector.tensor_reduce(bcol(23), bn[:, 16:16 + NCH], AX.X, ALU.add))
                batchnorm(eng, link, bcol(15), bcol(23), N, "g_node", "beta_node", 8, 1)
                link.done()
                with eng.Fori(0, K) as k:
                    link = Chain(eng, k_link, (k + K * PH) * 4 + (PH * 4 + 3), 4)
                    start_pass(link)
                    link(nc.vector.memset(msq[:, :], 0.0))
                    vlink = Chain(eng, v_link, k * 3, 3)
                    vlink(nc.vector.tensor_scalar(flat(w_all[:, :, :]), flat(dstrel[:, :, :]), iotak[:, 0:1], 0.0, ALU.subtract, ALU.is_ge))
                    vlink(nc.vector.tensor_scalar(work[0][:, 0:NG * U], flat(dstrel[:, :, :]), iotak[:, 0:1], float(P), ALU.subtract, ALU.is_lt))
                    vlink(nc.vector.tensor_tensor(flat(w_all[:, :, :]), flat(w_all[:, :, :]), work[0][:, 0:NG * U], ALU.mult))
                    vlink.done()
                    eng.sem_inc(q_pass, 1)

                    def wait(name, g):
                        eng.wait_ge(q[name], k * NG + g + 3)

                    def hots(g, r):
                        eng.wait_ge(summed, (k + K * PH) * NG + g + 1)
                        one_hot(eng, oh[r][:, :, :], g, iotak).then_inc(q["oh"], 1)
                        nc.vector.tensor_scalar(valid[r][:, :], w_all[:, bass.ds(g, 1), :].rearrange("p a u -> p (a u)"), 1.0, None, ALU.mult)
                        nc.vector.tensor_scalar(ea_st[r][:, :], ea6[:, bass.ds(g, 1), :].rearrange("p a c -> p (a c)"),
                                                1.0, None, ALU.mult).then_inc(q["ea"], 1)

                    def transposed(g, r):
                        wait("ohT", g)
                        wait("pre", g - 1)
                        nc.vector.tensor_copy(flat(ohT_sb), flat(ohT_ps)).then_inc(q["ohTs"], 1)

                    def add_rows(g, r, half):
                        wait("pre", g)
                        wait("h", g - 1)
                        eng.wait_ge(gathered[r], ((k + K * PH) * (NG // 2) + half) * (16 * U) + 16 * U)
                        nc.vector.tensor_tensor(hsum, ps23[:, :, 0:F], rows[r][:, :, :], ALU.add).then_inc(q["hs"], 1)

                    def accumulate_sums(g, r):
                        add = accumulate(eng, aggT, g, (ps6, ps7)[r][0:F, 0:P])
                        eng.wait_ge(summed, (k + K * PH) * NG + g + 3)
                        eng.wait_ge(acc_done, (k + K * PH) * NG + g + 2)
                        add().then_inc(acc_done, 1)
                        wait("msq", g - 1)
                        nc.vector.tensor_tensor(msq[:, :], msq[:, :], (ps6, ps7)[r][0:F, P:P + 1], ALU.add).then_inc(q["msq"], 1)

                    hots(0, 0)
                    transposed(0, 0)
                    hots(1, 1)
                    add_rows(0, 0, 0)
                    transposed(1, 1)
                    with eng.Fori(0, NG // 2 - 1) as i:
                        for d in range(2):
                            g, r = i * 2 + (1 + d), (1 + d) % 2
                            hots(g + 1, 1 - r)
                            accumulate_sums(g - 1, 1 - r)
                            add_rows(g, r, i + d)
                            transposed(g + 1, 1 - r)
                    accumulate_sums(NG - 2, 0)
                    add_rows(NG - 1, 1, NG // 2 - 1)
                    accumulate_sums(NG - 1, 1)
                    eng.wait_ge(acc_done, (k + K * PH) * NG + (NG + 2))
                    wait("msq", NG - 1)
                    end_pass(link)
                    link.done()

            @block.tensor
            def _(eng):
                K = passes(eng)
                with eng.Fori(0, K) as k:
                    def wait(name, g):
                        eng.wait_ge(q[name], k * NG + g + 3)

                    def operands(g, r):
                        wait("ea", g)
                        wait("eaTs", g - 1)
                        nc.tensor.transpose(ea_ps[:, 0, :], ea_st[r][:, 0:KE], identb[:, :])
                        nc.tensor.transpose(ea_ps[:, 1, :], ea_st[r][:, KE:2 * KE], identb[:, :]).then_inc(q["eaT"], 1)
                        wait("ohb", g)
                        wait("ohTs", g - 1)
                        for u in range(U):
                            last = nc.tensor.transpose(ohT_ps[:, u, :], ohb[:, u, :], identb[:, :])
                        last.then_inc(q["ohT"], 1)
                        wait("eaTs", g)
                        wait("ers", g - 1)
                        for u in range(U):
                            last = nc.tensor.matmul(ps01[0:F, u, :], w6[:, u % UH, :], eaT[r][:, u // UH, :], start=True, stop=True)
                        last.then_inc(q["er"], 1)

                    def preact(g, r, half):
                        wait("ers", g)
                        wait("ohTs", g)
                        wait("hs", g - 1)
                        eng.wait_ge(q_win[r], (k * (NG // 2) + half) * 16 + 16)
                        for u in range(U):
                            nc.tensor.matmul(ps23[:, u, 0:F], big[0:F, u * P:(u + 1) * P], mat("Wfeat"), start=True, stop=False)
                            last = nc.tensor.matmul(ps23[:, u, 0:F], ohT_sb[:, u, :], qwin[r][:, :], start=False, stop=True)
                        last.then_inc(q["pre"], 1)

                    def sums(g, r):
                        wait("h", g)
                        wait("msq", g - 2)
                        eng.wait_ge(acc_done, (k + K * PH) * NG + g + 1)
                        ps = (ps6, ps7)[r]
                        for u in range(U):
                            nc.tensor.matmul(ps[0:F, 0:P], hbuf[r][:, u, :], oh[r][:, u, :], start=(u == 0), stop=(u == U - 1))
                        for u in range(U):
                            last = nc.tensor.matmul(ps[0:F, P:P + 1], sqbuf[r][:, u, :], valid[r][:, u:u + 1],
                                                    start=(u == 0), stop=(u == U - 1))
                        last.then_inc(summed, 1)

                    operands(0, 0)
                    preact(0, 0, 0)
                    operands(1, 1)
                    with eng.Fori(0, NG // 2 - 1) as i:
                        for d in range(2):
                            g, r = i * 2 + (1 + d), (1 + d) % 2
                            sums(g - 1, 1 - r)
                            preact(g, r, i + d)
                            operands(g + 1, 1 - r)
                    sums(NG - 2, 0)
                    preact(NG - 1, 1, NG // 2 - 1)
                    sums(NG - 1, 1)

        f_link, f_in, f_T, f_out, f_dma, f_free, f_d = sem("f_link"), sem("f_in"), sem("f_T"), sem("f_out"), sem("f_dma"), sem("f_free"), sem("f_d")
        f_read, f_deg = sem("f_read"), sem("f_deg")
        root0, FIRST, LAST = roots[0], 1 + LN_FIRST, LN_SECOND
        PER = FIRST + LAST
        ot = [big[:, 0:CB * F].rearrange("p (b f) -> p b f", f=F), big2[:, 0:CB * F].rearrange("p (b f) -> p b f", f=F)]
        tabw = TAB[:, :, :].rearrange("p b f -> p (b f)")
        part = [[tabw[0:F, (3 * r + n) * CW:(3 * r + n) * CW + CW] if 3 * r + n < 5 else work[0][0:F, :] for n in range(3)] for r in range(2)]
        ttf = [work[1][:, 0:CB * F].rearrange("p (b f) -> p b f", f=F), work[2][:, 0:CB * F].rearrange("p (b f) -> p b f", f=F)]
        diag = [work[3][0:F, n * F:(n + 1) * F] for n in range(4)]
        with nc.Block() as block:
            @block.scalar
            def _(eng):
                batch_stddev(eng, 0, 2)

                def load(c, r):
                    eng.wait_ge(f_T, c + 1)
                    eng.sem_inc(act_gate, 1)
                    nc.scalar.activation(part[r][0], aggT[:, bass.ds(c * CW, CW)], ACT.Copy)
                    nc.scalar.activation(part[r][2], rT[:, bass.ds(c * CW, CW)], ACT.Copy).then_inc(f_in, 1)

                load(0, 0)
                with eng.Fori(0, NCH // 2) as i:
                    for d in range(2):
                        c, r = i * 2 + (1 + d), (1 + d) % 2
                        load(c, r)
                        stddev(eng, v1r[1 - r], c + (root0 - 1))
                stddev(eng, v1r[0], NCH - 1 + root0)

            @block.vector
            def _(eng):
                eng.sem_inc(f_out, 2)
                link = Chain(eng, bn_link, EDGE_LINKS + BN_LINKS + 3, BN_LINKS + 5)
                link(nc.vector.tensor_reduce(bcol(14), aggT[:, 0:N], AX.X, ALU.add))
                batchnorm(eng, link, bcol(14), msq[:, :], E, "g_msg", "beta_msg", 0, 2)
                for n, at in enumerate((0, 1, 8, 9)):
                    link(nc.vector.tensor_scalar(diag[n], ident[0:F, 0:F], bcol(at), None, ALU.mult))
                link.done()
                eng.sem_inc(f_d, 1)
                eng.sem_inc(f_read, 2)

                def first(c, r, base):
                    link = Chain(eng, f_link, base, FIRST)
                    eng.wait_ge(f_T, c + 3)
                    eng.wait_ge(f_out, c + 1)
                    link(nc.vector.tensor_tensor(ttf[r], psA[r][:, 0:CB, 0:F], X[:, bass.ds(c * CB, CB), :], ALU.add))
                    eng.sem_inc(f_read, 1)
                    ln_first(link, ttf[r], s1r[r], v1r[r])
                    eng.sem_inc(nd_var, 1)
                    link.done()

                def second(c, r, base):
                    link = Chain(eng, f_link, base, LAST)
                    eng.wait_ge(f_free, c + 1)
                    ln_second(eng, link, ot[r], ttf[r], v1r[r], c + root0).then_inc(f_out, 1)
                    link.done()

                first(0, 0, 0)
                with eng.Fori(0, NCH // 2) as i:
                    for d in range(2):
                        c, r = i * 2 + (1 + d), (1 + d) % 2
                        first(c, r, c * PER - LAST)
                        second(c - 1, 1 - r, c * PER + (FIRST - LAST))
                second(NCH - 1, 0, (NCH - 1) * PER + FIRST)

            @block.tensor
            def _(eng):
                eng.sem_inc(f_T, 2)
                eng.wait_ge(f_d, 1)

                def product(c, r):
                    eng.wait_ge(f_in, c + 1)
                    eng.wait_ge(f_deg, c * 16 + 16)
                    eng.wait_ge(f_read, c + 1)
                    for j in range(CB):
                        a, b, f = (x[:, j * P:(j + 1) * P] for x in part[r])
                        nc.tensor.matmul(psA[r][:, j, 0:F], a, diag[0], start=True, stop=False)
                        nc.tensor.matmul(psA[r][:, j, 0:F], b, diag[1], start=False, stop=False)
                        nc.tensor.matmul(psA[r][:, j, 0:F], f, diag[2], start=False, stop=False)
                        last = nc.tensor.matmul(psA[r][:, j, 0:F], ones_fp[:, :], diag[3], start=False, stop=True)
                    last.then_inc(f_T, 1)

                product(0, 0)
                with eng.Fori(0, NCH // 2) as i:
                    for d in range(2):
                        product(i * 2 + (1 + d), (1 + d) % 2)

            @block.sync
            def _(eng):
                eng.sem_inc(f_free, 2)

                def degrees(c, r):
                    eng.wait_ge(f_T, c + 1)
                    eng.sem_inc(sp_gate, 1)
                    eng.dma_start(part[r][1], degrow.rearrange("b p -> (b p)")[bass.ds(c * CW, CW)].partition_broadcast(F)).then_inc(f_deg, 16)
                    eng.wait_ge(f_deg, c * 16 + 16)
                    eng.sem_inc(sp_gate, 1)

                def store(c, r):
                    eng.wait_ge(f_out, c + 3)
                    eng.dma_start(out[bass.ds(c * CW, CW), :].rearrange("(b p) f -> p b f", p=P), ot[r]).then_inc(f_dma, 16)
                    eng.wait_ge(f_dma, c * 16 + 16)
                    eng.sem_inc(f_free, 1)

                degrees(0, 0)
                with eng.Fori(0, NCH // 2) as i:
                    for r in range(2):
                        degrees(i * 2 + (r + 1), 1 - r)
                        store(i * 2 + r, r)
                eng.wait_ge(f_out, NCH + 2)
                o = (NCH - 1) * CW
                eng.dma_start(out[o:(NB - 1) * P, :].rearrange("(b p) f -> p b f", p=P), ot[0][:, 0:CB - 1, :]).then_inc(f_dma, 16)
                eng.dma_start(out[(NB - 1) * P:N, :], ot[0][0:N - (NB - 1) * P, CB - 1, :]).then_inc(f_dma, 16)
                eng.wait_ge(f_dma, 16 * (NCH + 1))


MATS = ["L0W1", "L0W2", "L1Wl1T", "L1Wr1T", "L1Wl2T", "L1Wr2T", "L2WaT", "L2WbT", "Wnode", "Wsrc", "Wdst", "Wfeat"]
ROWS = ["L0b1", "L0b2", "L1bl1", "L1bl2", "L2b", "b_msg"]
COLS = ["b_edge", "g_edge", "beta_edge", "b_node", "g_node", "beta_node", "g_msg", "beta_msg"]


def kernel(**inputs):
    import numpy as np
    import concourse.bacc as bacc
    from concourse.bass_utils import run_bass_kernel_spmd as run

    a = {k: np.asarray(v) for k, v in inputs.items()}
    N, F = a["x"].shape
    E, FE = a["edge_attr_4"].shape
    W_msg = a["L3_gnn_W_msg"]
    mats = dict(zip(MATS, [
        a["L0_gnn_W1"], a["L0_gnn_W2"], a["L1_gnn_Wl1"].T, a["L1_gnn_Wr1"].T, a["L1_gnn_Wl2"].T, a["L1_gnn_Wr2"].T,
        a["L2_gnn_mlp_w"][:, :F].T, a["L2_gnn_mlp_w"][:, F:].T, a["L3_gnn_W_node"],
        W_msg[:F], W_msg[F:2 * F], W_msg[2 * F:]]))
    rows = {"L0b1": a["L0_gnn_b1"], "L0b2": a["L0_gnn_b2"], "L1bl1": a["L1_gnn_bl1"], "L1bl2": a["L1_gnn_bl2"],
            "L2b": a["L2_gnn_mlp_b"]}
    for part in ("edge", "node", "msg"):
        for kind in ("b", "g", "beta"):
            rows[f"{kind}_{part}"] = a[f"L3_gnn_{kind}_{part}"]

    nc = bacc.Bacc("TRN2", target_bir_lowering=False, num_devices=1)
    arrays = {}

    def given(name, array):
        array = np.ascontiguousarray(array)
        arrays[f"in_{name}"] = array
        return nc.dram_tensor(f"in_{name}", array.shape, mybir.dt.from_np(array.dtype), kind="ExternalInput").ap()

    x, src, dst = given("x", a["x"]), given("src", a["src"]), given("dst", a["dst"])
    ea, ew = given("edge_attr", a["edge_attr_4"]), given("edge_weight", a["edge_weight"])
    mats_dram = {k: given(k, v) for k, v in mats.items()}
    rows_dram = {k: given(k, v) for k, v in rows.items()}
    w_edge = given("w_edge", a["L3_gnn_W_edge"])
    out = nc.dram_tensor("out_x", (N, F), mybir.dt.float32, kind="ExternalOutput").ap()
    build(nc, x, src, dst, ea, ew, mats_dram, rows_dram, ROWS, COLS, w_edge, out, N, E, F, FE)
    return run(nc, [arrays], core_ids=[0]).results[0]["out_x"]
```

```python
import concourse.bass as bass
from concourse import mybir
from contextlib import ExitStack


def build(nc, x, src, dst, ea, ew, mats_dram, rows_dram, bias_rows, cols, w_edge, out, N, E, F, FE):
    mats = list(mats_dram)
    fp32, bf16, i32 = mybir.dt.float32, mybir.dt.bfloat16, mybir.dt.int32
    ALU, ACT, AX = mybir.AluOpType, mybir.ActivationFunctionType, mybir.AxisListType
    P, U = 128, 8
    GE = P * U
    NG = -(-E // GE)
    NG += -NG % 4
    FULL = E // GE
    REST = E - FULL * GE
    NPAD_E = NG * GE - E
    NB = -(-N // P)
    CB = 7
    assert NB % CB == 0 and F % 32 == 0 and F < P
    NCH = NB // CB
    CW = CB * P
    NP = NB * P
    AW = NP + P
    MAXK = -(-N // P) + 1
    EPS = 1e-5
    FAR = 1.0e6

    ctx = ExitStack()
    with ctx:
        def sb(name, shape, dt=fp32):
            return ctx.enter_context(nc.sbuf_tensor(name, shape, dt))

        def pb(name, shape, dt=fp32):
            return ctx.enter_context(nc.psum_tensor(name, shape, dt))

        def sem(name):
            return ctx.enter_context(nc.semaphore(name))

        table = nc.dram_tensor("table", (NP, F), fp32, kind="Internal").ap()
        qtable = nc.dram_tensor("qtable", (AW, 3 * F), bf16, kind="Internal").ap()
        degrow = nc.dram_tensor("degrow", (NB, P), fp32, kind="Internal").ap()

        idx_all = sb("idx_all", [P, NG, U], i32)
        dstrel = sb("dstrel", [P, NG, U])
        w_all = sb("w_all", [P, NG, U])
        UH, PARTS = U // 2, 6
        KE = PARTS * UH * FE
        ea6 = sb("ea6", [P, NG, 2 * KE], bf16)
        X = sb("X", [P, NB, F])
        TAB = sb("TAB", [P, NB, F])
        aggT = sb("aggT", [F, AW])
        spare = sb("spare", [P, NP])
        rT = spare[0:F, :]
        RB = spare[:, 0:NB * F].rearrange("p (b f) -> p b f", f=F)
        ea_all = spare[:, 0:NG * U * FE].rearrange("p (g c) -> p g c", c=U * FE)
        M = sb("M", [F, len(mats), F])
        brow = sb("brow", [1, len(bias_rows), F])
        col = sb("col", [F, len(cols)])
        w6 = sb("w6", [KE, UH, F], bf16)
        bias_bc = sb("bias_bc", [P, F])
        ident = sb("ident", [P, P])
        identb = sb("identb", [P, P], bf16)
        iota_bf = sb("iota_bf", [P, P], bf16)
        iota_i = sb("iota_i", [P, P], i32)
        iota0 = sb("iota0", [P, P])
        iotak = sb("iotak", [P, P])
        ones_row = sb("ones_row", [1, P])
        eps_col = sb("eps_col", [P, 1])
        one_col = sb("one_col", [P, 1])
        base_row = sb("base_row", [1, NG])
        base_run = sb("base_run", [1, NG])
        basek_i = sb("basek_i", [1, NG], i32)
        kcnt = sb("kcnt", [1, 1], i32)
        deg = sb("deg", [P, NB])
        dinv = sb("dinv", [P, NB])
        rdeg = sb("rdeg", [P, NB])
        est = sb("est", [F, 2])
        msq = sb("msq", [F, 1])
        crow = sb("crow", [1, F])
        idx_st = [sb(f"idx_st{i}", [P, U], i32) for i in range(2)]
        rows = [sb(f"rows{i}", [P, U, F]) for i in range(2)]
        oh = [sb(f"oh{i}", [P, U, P]) for i in range(2)]
        work = [sb(f"work{i}", [P, CB * P]) for i in range(4)]
        big = sb("big", [P, GE])
        big2 = sb("big2", [P, GE])
        big3 = sb("big3", [P, GE])
        work4 = TAB[:, :, :].rearrange("p b f -> p (b f)")
        ohb = sb("ohb", [P, U, P], bf16)
        ea_st = [sb(f"ea_st{i}", [P, 2 * KE], bf16) for i in range(2)]
        eaT = [sb(f"eaT{i}", [KE, 2, P], bf16) for i in range(2)]
        erst = [sb(f"erst{i}", [F, 2]) for i in range(2)]
        small = sb("small", [P, 64])
        valid = [sb(f"valid{i}", [P, U]) for i in range(4)]
        qwin = [sb(f"qwin{i}", [P, 3 * F], bf16) for i in range(2)]

        ps01 = pb("ps01", [P, 8, P])
        ps23 = pb("ps23", [P, 8, P])
        ps45 = pb("ps45", [P, 8, P])
        ps6 = pb("ps6", [P, 512])
        ps7 = pb("ps7", [P, 512])

        def mat(name):
            return M[:, mats.index(name), :]

        def bias(name):
            return brow[0:1, bias_rows.index(name), :]

        def cvec(name):
            return col[:, cols.index(name):cols.index(name) + 1]

        class Chain:

            def __init__(self, eng, semaphore, base, length):
                self.eng, self.sem, self.base, self.length, self.n = eng, semaphore, base, length, 0

            def __call__(self, ins):
                self.n += 1
                ins.then_inc(self.sem, 1)
                self.eng.wait_ge(self.sem, self.base + self.n)

            def done(self):
                assert self.n == self.length, (self.n, self.length)

        act_gate, pool_gate, dve_gate = sem("act_gate"), sem("pool_gate"), sem("dve_gate")

        s_pad, s_load, s_w, s_const, s_min = sem("s_pad"), sem("s_load"), sem("s_w"), sem("s_const"), sem("s_min")
        s_pe0, s_dv0 = sem("s_pe0"), sem("s_dv0")
        idx_staged, oh_ready, summed, acc_done = sem("idx_staged"), sem("oh_ready"), sem("summed"), sem("acc_done")
        gathers = [[sem(f"gathered{ph}_{r}") for r in range(2)] for ph in range(6)]
        k_link = sem("k_link")
        ea_ready, eaT_ps, eaT_sb, er_ps = sem("ea_ready"), sem("eaT_ps"), sem("eaT_sb"), sem("er_ps")
        er_stat, est_done = sem("er_stat"), sem("est_done")
        dst_i = TAB[:, :, :].rearrange("p b f -> p (b f)").bitcast(i32)[:, 0:NG * U].rearrange("p (g u) -> p g u", u=U)
        gmm = work[0]
        wf = big[0:KE, 0:UH * F].rearrange("p (u f) -> p u f", f=F)
        wm = big2[0:KE, 0:UH * F].rearrange("p (u f) -> p u f", f=F)
        wpart = big3[0:KE, 0:UH * F].rearrange("p (u f) -> p u f", f=F)
        rowsel = small[0:KE, 8:11]
        s_split = sem("s_split")
        s_ea, s_ea_act, s_w6 = sem("s_ea"), sem("s_ea_act"), sem("s_w6")
        ea_rest = work4[:, NG * U:NG * U * (FE + 1)].rearrange("p (g c) -> p g c", c=U * FE)
        ea_h = [ea6[:, :, h * KE:(h + 1) * KE].rearrange("p g (c u f) -> p g c (u f)", c=PARTS, f=FE) for h in range(2)]
        FP, FR = REST // U, REST % U

        def edge_dmas(eng, d3, s1, width, s_done):
            n = 0
            if FULL:
                eng.dma_start(d3[:, 0:FULL, :], s1[0:FULL * GE * width].rearrange("(g p u) -> p g u", p=P, u=U * width)).then_inc(s_done, 16)
                n += 16
            if FP:
                o = FULL * GE * width
                eng.dma_start(d3[0:FP, FULL, :], s1[o:o + FP * U * width].rearrange("(p u) -> p u", p=FP)).then_inc(s_done, 16)
                n += 16
            if FR:
                o = (FULL * GE + FP * U) * width
                eng.dma_start(d3[FP:FP + 1, FULL, 0:FR * width], s1[o:o + FR * width].rearrange("(p u) -> p u", p=1)).then_inc(s_done, 16)
                n += 16
            return n

        s_dst, s_hl, d_hi, d_lo, d_sum, d_acc = sem("s_dst"), sem("s_hl"), sem("d_hi"), sem("d_lo"), sem("d_sum"), sem("d_acc")
        hl_i = work[2][:, 0:NG * U].bitcast(i32)
        lo_b = work[3][:, :].bitcast(bf16)[:, 0:NG * U].rearrange("p (g u) -> p g u", u=U)
        hi_b = ohb[:, :, :].rearrange("p u n -> p (u n)")[:, 0:NG * U].rearrange("p (g u) -> p g u", u=U)
        iota_b = iota_bf[:, :]
        oh_lo = [oh[r][:, :, :].rearrange("p u n -> p (u n)").bitcast(bf16)[:, 0:GE].rearrange("p (u n) -> p u n", n=P) for r in range(2)]
        oh_hi = [oh[r][:, :, :].rearrange("p u n -> p (u n)").bitcast(bf16)[:, GE:GE + U * NB].rearrange("p (u n) -> p u n", n=NB) for r in range(2)]
        hi_diff, hi_square = [[work[2][:, :].bitcast(bf16)[:, (2 * n + r) * U * NB:(2 * n + r + 1) * U * NB].rearrange("p (u n) -> p u n", n=NB)
                               for r in range(2)] for n in range(2)]
        d_diff, d_sq = sem("d_diff"), sem("d_sq")
        DL = 5
        EARLY = NG // 8

        with nc.Block() as block:
            @block.gpsimd
            def _(eng):
                eng.memset(idx_all[:, FULL:NG, :], 0).then_inc(s_pad, 1)
                eng.memset(dst_i[:, FULL:NG, :], int(FAR)).then_inc(s_pad, 1)
                eng.memset(w_all[:, FULL:NG, :], 0.0).then_inc(s_pad, 1)
                eng.memset(ea_all[:, FULL:NG, :], 0.0).then_inc(s_pad, 1)
                eng.memset(X[:, NB - 1:NB, :], 0.0).then_inc(s_pad, 1)
                eng.memset(wf, 0.0).then_inc(s_pad, 1)
                eng.memset(ident[:, :], 0.0).then_inc(s_const, 1)
                eng.memset(ones_row[:, :], 1.0).then_inc(s_const, 1)
                eng.memset(eps_col[:, :], EPS).then_inc(s_const, 1)
                eng.memset(one_col[:, :], 1.0).then_inc(s_const, 1)
                eng.iota(iota_i[:, :], pattern=[[1, P]], base=0, channel_multiplier=0).then_inc(s_const, 1)
                eng.memset(rowsel, 1.0).then_inc(s_const, 1)
                eng.wait_ge(s_const, 6)
                CU = UH * FE
                for sel, lo, hi in ((0, 0, 3 * CU), (1, 3 * CU, 5 * CU), (2, 5 * CU, 6 * CU)):
                    eng.affine_select(out=rowsel[:, sel:sel + 1], in_=rowsel[:, sel:sel + 1], compare_op=ALU.is_ge, fill=0.0,
                                      base=-lo, pattern=[[0, 1]], channel_multiplier=1).then_inc(s_w6, 1)
                    eng.wait_ge(s_w6, 2 * sel + 1)
                    eng.affine_select(out=rowsel[:, sel:sel + 1], in_=rowsel[:, sel:sel + 1], compare_op=ALU.is_ge, fill=0.0,
                                      base=hi - 1, pattern=[[0, 1]], channel_multiplier=-1).then_inc(s_w6, 1)
                    eng.wait_ge(s_w6, 2 * sel + 2)
                eng.affine_select(out=ident[:, :], in_=ident[:, :], compare_op=ALU.not_equal, fill=1.0,
                                  base=0, pattern=[[-1, P]], channel_multiplier=1).then_inc(s_const, 1)

                eng.wait_ge(s_hl, DL)

                def hi_diffs(i):
                    for r in range(2):
                        g = i * 2 + r
                        eng.wait_ge(d_sq, g + 1)
                        nc.gpsimd.tensor_tensor(hi_diff[r], iota_b[:, 0:NB].unsqueeze(1).to_broadcast([P, U, NB]),
                                                hi_b[:, bass.ds(g, 1), :].rearrange("p a u -> p (a u)").unsqueeze(2).to_broadcast([P, U, NB]),
                                                ALU.subtract).then_inc(d_diff, 1)

                with eng.Fori(0, EARLY) as i:
                    hi_diffs(i)
                eng.wait_ge(s_min, 2)
                slink = Chain(eng, s_split, 0, 4)
                def less(part, n, out, full):
                    eng.wait_ge(s_ea_act, n)
                    for h in range(2):
                        f4 = full.rearrange("p g (h c) -> p g h c", h=2)[:, :, h, :]
                        o4 = out.rearrange("p g (h c) -> p g h c", h=2)[:, :, h, :]
                        slink(nc.gpsimd.tensor_tensor(o4, f4, ea_h[h][:, :, part, :], ALU.subtract))
                    eng.sem_inc(s_ea, 1)
                less(0, 2, ea_rest, ea_all)
                less(1, 4, ea_rest, ea_rest)
                slink.done()
                with eng.Fori(EARLY, NG // 2) as i:
                    hi_diffs(i)

            @block.sync
            def _(eng):
                eng.wait_ge(s_pad, 6)
                d = edge_dmas(eng, dst_i, dst, 1, s_dst)
                eng.wait_ge(s_dst, d)
                eng.sem_inc(s_min, 1)
                n = edge_dmas(eng, idx_all, src, 1, s_load)
                eng.dma_start(X[:, 0:NB - 1, :], x[0:(NB - 1) * P, :].rearrange("(b p) f -> p b f", p=P)).then_inc(s_w, 16)
                eng.dma_start(X[0:N - (NB - 1) * P, NB - 1, :], x[(NB - 1) * P:N, :]).then_inc(s_w, 16)
                m = edge_dmas(eng, w_all, ew, 1, s_w) + 32
                m += edge_dmas(eng, ea_all, ea.rearrange("e c -> (e c)"), FE, s_w)
                for i, name in enumerate(mats):
                    eng.dma_start(M[:, i, :], mats_dram[name]).then_inc(s_w, 16)
                for i, name in enumerate(bias_rows):
                    eng.dma_start(brow[0:1, i, :], rows_dram[name].rearrange("(a f) -> a f", a=1)).then_inc(s_w, 16)
                for i, name in enumerate(cols):
                    eng.dma_start(col[:, i:i + 1], rows_dram[name].rearrange("(f a) -> f a", a=1)).then_inc(s_w, 16)
                for c in range(PARTS):
                    for u in range(UH):
                        o = (c * UH + u) * FE
                        eng.dma_start(wf[o:o + FE, u, :], w_edge).then_inc(s_w, 16)
                m += 16 * (len(mats) + len(bias_rows) + len(cols) + PARTS * UH)
                eng.wait_ge(s_load, n)
                eng.wait_ge(s_w, m)
                eng.sem_inc(s_min, 1)

            @block.vector
            def _(eng):
                eng.sem_inc(acc_done, 2)
                eng.sem_inc(est_done, 2)
                eng.wait_ge(s_min, 1)
                eng.wait_ge(s_const, 7)
                hl = Chain(eng, s_hl, 0, DL)
                dflat = dst_i.rearrange("p g u -> p (g u)")
                hl(nc.vector.tensor_scalar(hl_i, dflat, P.bit_length() - 1, None, ALU.logical_shift_right))
                hl(nc.vector.tensor_copy(hi_b.rearrange("p g u -> p (g u)"), hl_i))
                hl(nc.vector.tensor_scalar(hl_i, dflat, P - 1, None, ALU.bitwise_and))
                hl(nc.vector.tensor_copy(lo_b.rearrange("p g u -> p (g u)"), hl_i))
                hl(nc.vector.tensor_copy(iota_b, iota_i[:, :]))
                hl.done()
                def lo_one_hots(i):
                    for r in range(2):
                        g = i * 2 + r
                        eng.wait_ge(d_sum, g + 1)
                        nc.vector.tensor_tensor(oh_lo[r], iota_b.unsqueeze(1).to_broadcast([P, U, P]),
                                                lo_b[:, bass.ds(g, 1), :].rearrange("p a u -> p (a u)").unsqueeze(2).to_broadcast([P, U, P]),
                                                ALU.is_equal).then_inc(d_lo, 1)

                with eng.Fori(0, EARLY) as i:
                    lo_one_hots(i)
                link = Chain(eng, s_dv0, 0, 15 + 9)
                link(nc.vector.tensor_copy(iota0[:, :], iota_i[:, :]))
                link(nc.vector.tensor_copy(identb[:, :], ident[:, :]))
                link(nc.vector.tensor_copy(dstrel[:, :, :], dst_i[:, :, :]))
                link(nc.vector.tensor_reduce(gmm[:, 0:NG], dstrel[:, :, :], AX.X, ALU.min))
                m3 = work[1][:, 0:NG * U].rearrange("p (g u) -> p g u", u=U)
                link(nc.vector.scalar_tensor_tensor(out=m3, in0=dstrel[:, :, :], scalar=FAR, in1=dstrel[:, :, :],
                                                    op0=ALU.is_lt, op1=ALU.mult))
                link(nc.vector.tensor_reduce(gmm[:, NG:2 * NG], m3, AX.X, ALU.max))
                eng.wait_ge(s_pe0, 1)
                link(nc.vector.tensor_reduce(small[0:NG, 0:1], ps01[0:NG, 0, 0:P], AX.X, ALU.min))
                link(nc.vector.tensor_reduce(small[0:NG, 1:2], ps01[0:NG, 4, 0:P], AX.X, ALU.max))
                eng.wait_ge(s_pe0, 2)
                link(nc.vector.tensor_copy(base_row[0:1, :], ps6[0:1, 0:NG]))
                link(nc.vector.tensor_tensor(base_run[0:1, :], ps7[0:1, 0:NG], base_row[0:1, :], ALU.subtract))
                link(nc.vector.tensor_reduce(small[0:1, 2:3], base_run[0:1, :], AX.X, ALU.max))
                link(nc.vector.tensor_copy(kcnt[0:1, :], small[0:1, 2:3]))
                link(nc.vector.tensor_scalar(kcnt[0:1, :], kcnt[0:1, :], P.bit_length() - 1, None, ALU.logical_shift_right))
                link(nc.vector.tensor_scalar(kcnt[0:1, :], kcnt[0:1, :], 1.0, None, ALU.add))
                eng.wait_ge(s_pe0, 3)
                link(nc.vector.tensor_tensor(dstrel[:, :, :], dstrel[:, :, :],
                                             ps6[:, 0:NG].unsqueeze(2).to_broadcast([P, NG, U]), ALU.subtract))
                eng.wait_ge(s_min, 2)
                eng.wait_ge(s_w6, 6)
                link(nc.vector.tensor_copy(w6[:, :, :], wf))
                link(nc.vector.tensor_tensor(wm, wf, w6[:, :, :], ALU.subtract))
                link(nc.vector.tensor_scalar(wpart, w6[:, :, :], rowsel[:, 0:1], None, ALU.mult))
                link(nc.vector.tensor_copy(w6[:, :, :], wm))
                link(nc.vector.tensor_tensor(wf, wm, w6[:, :, :], ALU.subtract))
                link(nc.vector.scalar_tensor_tensor(out=wpart, in0=w6[:, :, :], scalar=rowsel[:, 1:2], in1=wpart, op0=ALU.mult, op1=ALU.add))
                link(nc.vector.tensor_copy(w6[:, :, :], wf))
                link(nc.vector.scalar_tensor_tensor(out=wpart, in0=w6[:, :, :], scalar=rowsel[:, 2:3], in1=wpart, op0=ALU.mult, op1=ALU.add))
                link(nc.vector.tensor_copy(w6[:, :, :], wpart))
                link.done()
                with eng.Fori(EARLY, NG // 2) as i:
                    lo_one_hots(i)
                eng.wait_ge(d_sum, NG + 2)
                nc.vector.tensor_copy(deg[:, :], ps45[:, 0, 0:NB]).then_inc(d_acc, 1)

            @block.scalar
            def _(eng):
                eng.sem_inc(eaT_sb, 1)
                eng.sem_inc(er_stat, 1)
                eng.wait_ge(s_const, 7)
                eng.sem_inc(d_sq, 2)

                def hi_one_hots(i):
                    for r in range(2):
                        g = i * 2 + r
                        eng.wait_ge(d_diff, g + 1)
                        nc.scalar.activation(hi_square[r], hi_diff[r], ACT.Square).then_inc(d_sq, 1)
                        eng.wait_ge(d_sq, g + 3)
                        eng.wait_ge(d_sum, g + 1)
                        nc.scalar.activation(oh_hi[r], hi_square[r], ACT.Relu, bias=one_col[:, 0:1], scale=-1.0).then_inc(d_hi, 1)

                with eng.Fori(0, EARLY) as i:
                    hi_one_hots(i)
                eng.wait_ge(s_min, 2)
                for part, src4, after in ((0, ea_all, 0), (1, ea_rest, 1), (2, ea_rest, 2)):
                    if after:
                        eng.wait_ge(s_ea, after)
                    for h in range(2):
                        nc.scalar.activation(ea_h[h][:, :, part, :], src4.rearrange("p g (h c) -> p g h c", h=2)[:, :, h, :],
                                             ACT.Copy).then_inc(s_ea_act, 1)
                eng.wait_ge(s_ea_act, 6)
                for dest, part in ((3, 0), (4, 1), (5, 0)):
                    for h in range(2):
                        nc.scalar.activation(ea_h[h][:, :, dest, :], ea_h[h][:, :, part, :], ACT.Copy).then_inc(s_ea_act, 1)
                eng.wait_ge(s_ea_act, 12)
                with eng.Fori(EARLY, NG // 2) as i:
                    hi_one_hots(i)

            @block.tensor
            def _(eng):
                eng.sem_inc(summed, 2)
                eng.sem_inc(eaT_ps, 2)
                eng.sem_inc(d_sum, 2)
                def count(r, first=False, end=False):
                    for u in range(U):
                        last = nc.tensor.matmul(ps45[:, 0, 0:NB], oh_lo[r][:, u, :], oh_hi[r][:, u, :],
                                                start=first and u == 0, stop=end and u == U - 1, skip_group_check=True)
                    last.then_inc(d_sum, 1)
                for g in range(2):
                    eng.wait_ge(d_lo, g + 1)
                    eng.wait_ge(d_hi, g + 1)
                    count(g, first=g == 0)
                def counts(i):
                    for r in range(2):
                        eng.wait_ge(d_lo, i * 2 + (r + 1))
                        eng.wait_ge(d_hi, i * 2 + (r + 1))
                        count(r)

                with eng.Fori(1, EARLY) as i:
                    counts(i)
                eng.wait_ge(s_dv0, 6)
                nc.tensor.transpose(ps01[0:NG, 0, 0:P], gmm[:, 0:NG], ident[:, :])
                nc.tensor.transpose(ps01[0:NG, 4, 0:P], gmm[:, NG:2 * NG], ident[:, :]).then_inc(s_pe0, 1)
                eng.wait_ge(s_dv0, 8)
                nc.tensor.transpose(ps6[0:1, 0:NG], small[0:NG, 0:1], ident[0:NG, 0:NG])
                nc.tensor.transpose(ps7[0:1, 0:NG], small[0:NG, 1:2], ident[0:NG, 0:NG]).then_inc(s_pe0, 1)
                eng.wait_ge(s_dv0, 14)
                nc.tensor.matmul(ps6[:, 0:NG], ones_row[0:1, :], base_row[0:1, :], start=True, stop=True).then_inc(s_pe0, 1)
                with eng.Fori(EARLY, NG // 2 - 1) as i:
                    counts(i)
                for r in range(2):
                    eng.wait_ge(d_lo, NG - 1 + r)
                    eng.wait_ge(d_hi, NG - 1 + r)
                    count(r, end=r == 1)

        def passes(eng):
            return eng.value_load(kcnt[0:1, 0:1], min_val=1, max_val=MAXK)

        def one_hot(eng, dest, g, offsets):
            return nc.vector.tensor_tensor(dest, offsets[:, :].unsqueeze(1).to_broadcast([P, U, P]),
                                           dstrel[:, bass.ds(g, 1), :].rearrange("p a u -> p (a u)").unsqueeze(2).to_broadcast([P, U, P]),
                                           ALU.is_equal)

        def start_pass(link):
            link(nc.vector.tensor_scalar(basek_i[0:1, :], base_run[0:1, :], float(NP), None, ALU.min))

        def end_pass(link):
            link(nc.vector.tensor_scalar(base_run[0:1, :], base_run[0:1, :], float(P), None, ALU.add))
            link(nc.vector.tensor_scalar(iotak[:, :], iotak[:, :], float(P), None, ALU.add))

        def start_phase(link, target):
            link(nc.vector.memset(target[:, :], 0.0))
            link(nc.vector.tensor_copy(iotak[:, :], iota0[:, :]))
            link(nc.vector.tensor_copy(base_run[0:1, :], base_row[0:1, :]))
            link.eng.sem_inc(dve_gate, 1)

        def accumulate(eng, target, g, ps):
            at = eng.value_load(basek_i[0:1, bass.ds(g, 1)], min_val=0, max_val=NP)
            return lambda: nc.vector.tensor_tensor(target[:, bass.ds(at, P)], target[:, bass.ds(at, P)], ps, ALU.add)

        nd_staged, nd_T, nd_xT, nd_mm, nd_evac = sem("nd_staged"), sem("nd_T"), sem("nd_xT"), sem("nd_mm"), sem("nd_evac")
        nd_bias, nd_agg, nd_sum, nd_read, nd_out = sem("nd_bias"), sem("nd_agg"), sem("nd_sum"), sem("nd_read"), sem("nd_out")
        nd_sq = sem("nd_sq")
        nd_dma, nd_link, nd_var, nd_sd, c_link = sem("nd_dma"), sem("nd_link"), sem("nd_var"), sem("nd_sd"), sem("c_link")
        t_sd, t_tab, t_link, t_dma, t_row = sem("t_sd"), sem("t_tab"), sem("t_link"), sem("t_dma"), sem("t_row")
        with nc.Block() as block:
            @block.scalar
            def _(eng):
                eng.activation(dinv[:, :], deg[:, :], ACT.Sqrt, bias=one_col[:, 0:1]).then_inc(t_sd, 1)

            @block.vector
            def _(eng):
                link = Chain(eng, t_link, 0, 3)
                eng.sem_inc(nd_read, 2)
                eng.sem_inc(nd_out, 2)
                eng.wait_ge(t_row, 1)
                nc.vector.tensor_copy(work[3][0:NB, 0:P], ps6[0:NB, 0:P]).then_inc(t_row, 1)
                eng.wait_ge(t_sd, 1)
                link(nc.vector.reciprocal(dinv[:, :], dinv[:, :]))
                link(nc.vector.tensor_scalar(rdeg[:, :], deg[:, :], 1.0, None, ALU.max))
                link(nc.vector.reciprocal(rdeg[:, :], rdeg[:, :]))
                link.done()
                for c in range(NCH):
                    b = slice(c * CB, (c + 1) * CB)
                    nc.vector.tensor_tensor(TAB[:, b, :], X[:, b, :], dinv[:, b].unsqueeze(2).to_broadcast([P, CB, F]), ALU.mult).then_inc(t_tab, 1)

            @block.sync
            def _(eng):
                eng.wait_ge(t_row, 2)
                eng.dma_start(degrow[:, :], work[3][0:NB, 0:P]).then_inc(t_dma, 16)
                for c in range(NCH):
                    eng.wait_ge(t_tab, c + 1)
                    eng.dma_start(table[c * CW:(c + 1) * CW, :].rearrange("(b p) f -> p b f", p=P), TAB[:, c * CB:(c + 1) * CB, :]).then_inc(t_dma, 16)
                eng.wait_ge(t_dma, 16 * (NCH + 1))

            @block.tensor
            def _(eng):
                nc.tensor.transpose(ps6[0:NB, 0:P], deg[:, :], ident[:, :]).then_inc(t_row, 1)
                eng.sem_inc(nd_mm, 1)
                eng.sem_inc(nd_sum, 2)

        er_relu = sem("er_relu")

        stN, xT = work[1], work[2]
        stN3 = stN[:, 0:CB * F].rearrange("p (b f) -> p b f", f=F)
        sumT = [work[0], work[2]]
        sq3 = big3[:, 0:CB * F].rearrange("p (b f) -> p b f", f=F)
        ttr = [work[1][:, 0:CB * F].rearrange("p (b f) -> p b f", f=F), work[3][:, 0:CB * F].rearrange("p (b f) -> p b f", f=F)]
        s1r, v1r = [small[:, 0:CB], small[:, 8:8 + CB]], [small[:, 16:16 + CB], small[:, 24:24 + CB]]
        ea_ps2 = ps01[0:KE, 0, :].bitcast(bf16).rearrange("p (h e) -> p h e", h=2)
        psA = [ps01, ps23]

        def bc(ap):
            return ap.unsqueeze(2).to_broadcast([P, CB, F])

        LN_FIRST, LN_SECOND = 2, 1

        def ln_first(link, tt3, s1):
            link(nc.vector.tensor_reduce(s1, tt3, AX.X, ALU.add))
            link(nc.vector.tensor_scalar(s1, s1, -1.0 / F, None, ALU.mult))

        def stddev(eng, tt3, s1, v1, root):
            eng.wait_ge(nd_var, root + 1)
            for j in range(CB):
                last = nc.scalar.activation(sq3[:, j, :], tt3[:, j, :], ACT.Square, bias=s1[:, j:j + 1], accum_out=v1[:, j:j + 1])
            last.then_inc(nd_sq, 1)
            eng.wait_ge(nd_sq, root + 1)
            eng.sem_inc(act_gate, 1)
            nc.scalar.activation(v1, v1, ACT.Sqrt, bias=eps_col[:, 0:1], scale=1.0 / F).then_inc(nd_sd, 1)

        def ln_second(eng, link, result, tt3, s1, v1, root):
            eng.wait_ge(nd_sd, root + 1)
            link(nc.vector.reciprocal(v1, v1))
            for j in range(CB):
                last = nc.vector.tensor_scalar(result(j), tt3[:, j, :], s1[:, j:j + 1], v1[:, j:j + 1], ALU.add, ALU.mult)
            return last

        roots, links = [0], [0]

        def layer(ph, node, W_agg, W_node, bias_name, scale, node_scale, relu, residual, weighted=False, edge_stats=False, prelude=None):
            early = residual and not relu
            first_n = (1 if scale is not None else 0) + 1 + (1 if relu and residual else 0) + (LN_FIRST if residual else 0)
            second_n = LN_SECOND if residual else 0
            per_chunk = first_n + second_n
            link0, root0 = links[0], roots[0]
            links[0] += NCH * per_chunk
            roots[0] += NCH if residual else 0
            gathered = gathers[ph]

            def at(k, K, g):
                return (k + K * ph) * NG + g

            def chunk_no(k, K, i):
                return (k + K * ph) * NCH + i

            with nc.Block() as block:
                @block.gpsimd
                def _(eng):
                    K = passes(eng)
                    with eng.Fori(0, K) as k:
                        with eng.Fori(0, NG // 2) as i:
                            for r in range(2):
                                eng.wait_ge(idx_staged, at(k, K, i * 2 + r) + 1)
                                eng.sem_inc(pool_gate, 1)
                                for u in range(U):
                                    eng.indirect_dma_start(
                                        out=rows[r][:, u, :], out_offset=None, in_=table[:, :],
                                        in_offset=bass.IndirectOffsetOnAxis(ap=idx_st[r][:, u:u + 1], axis=0)).then_inc(gathered[r], 16)

                @block.scalar
                def _(eng):
                    K = passes(eng)
                    if prelude:
                        prelude("scalar", eng)

                    def pair(k, i, with_chunk):
                        for r in range(2):
                            g = i * 2 + r
                            eng.wait_ge(summed, at(k, K, g) + 1)
                            eng.sem_inc(act_gate, 1)
                            nc.scalar.activation(idx_st[r][:, :], idx_all[:, bass.ds(g, 1), :].rearrange("p a u -> p (a u)"),
                                                 ACT.Copy).then_inc(idx_staged, 1)
                        if with_chunk:
                            n = chunk_no(k, K, i)
                            eng.wait_ge(nd_mm, n + 1)
                            eng.sem_inc(act_gate, 1)
                            nc.scalar.activation(stN3, node[:, bass.ds(i * CB, CB), :], ACT.Copy).then_inc(nd_staged, 1)
                            eng.wait_ge(nd_T, n + 1)
                            nc.scalar.activation(xT[0:F, :], ps45[0:F, 0:CB, :].rearrange("p b n -> p (b n)"), ACT.Copy).then_inc(nd_xT, 1)
                        for r in range(2 * edge_stats):
                            n = k * NG + i * 2 + r
                            eng.wait_ge(eaT_ps, n + 3)
                            nc.scalar.activation(eaT[r][:, :, :], ea_ps2, ACT.Copy).then_inc(eaT_sb, 1)
                            eng.wait_ge(er_ps, n + 1)
                            eng.wait_ge(est_done, n + 1)
                            nc.scalar.activation(big[0:F, :], ps23[0:F, :, :].rearrange("p u e -> p (u e)"), ACT.Relu,
                                                 bias=cvec("b_edge"), accum_out=erst[r][:, 0:1]).then_inc(er_relu, 1)
                            eng.wait_ge(er_relu, n + 1)
                            nc.scalar.activation(big2[0:F, :], big[0:F, :], ACT.Square,
                                                 accum_out=erst[r][:, 1:2]).then_inc(er_stat, 1)

                    with eng.Fori(0, K) as k:
                        with eng.Fori(0, NCH) as i:
                            pair(k, i, True)
                        with eng.Fori(NCH, NG // 2) as i:
                            pair(k, i, False)

                    def stage(c, r):
                        eng.wait_ge(nd_sum, c + (ph * NCH + 1))
                        eng.sem_inc(act_gate, 1)
                        nc.scalar.activation(sumT[r][0:F, :], aggT[:, bass.ds(c * CW, CW)], ACT.Copy).then_inc(nd_agg, 1)

                    eng.wait_ge(acc_done, K * ((ph + 1) * NG) + 2)
                    eng.sem_inc(act_gate, 1)
                    stage(0, 0)
                    with eng.Fori(0, NCH // 2) as i:
                        for d in range(2):
                            c, r = i * 2 + (1 + d), (1 + d) % 2
                            stage(c, r)
                            if residual:
                                stddev(eng, ttr[1 - r], s1r[1 - r], v1r[1 - r], c + (root0 - 1))
                    if residual:
                        stddev(eng, ttr[0], s1r[0], v1r[0], NCH - 1 + root0)

                @block.vector
                def _(eng):
                    K = passes(eng)
                    link = Chain(eng, k_link, K * (ph * 4) + ph * 4, 4)
                    start_phase(link, aggT)
                    eng.wait_ge(nd_bias, ph + 1)
                    link(nc.vector.tensor_copy(bias_bc[:, :], ps45[:, 0, 0:F]))
                    link.done()
                    eng.sem_inc(nd_evac, 1)
                    if prelude:
                        prelude("vector", eng)

                    def pair(k, i, with_chunk):
                        for r in range(2):
                            g = i * 2 + r
                            eng.wait_ge(summed, at(k, K, g) + 1)
                            if weighted:
                                for u in range(U):
                                    last = nc.vector.tensor_scalar(
                                        oh[r][:, u, :], iotak[:, :],
                                        dstrel[:, bass.ds(g, 1), u:u + 1].rearrange("p a b -> p (a b)"),
                                        w_all[:, bass.ds(g, 1), u:u + 1].rearrange("p a b -> p (a b)"), ALU.is_equal, ALU.mult)
                                last.then_inc(oh_ready, 1)
                            else:
                                one_hot(eng, oh[r][:, :, :], g, iotak).then_inc(oh_ready, 1)
                            if edge_stats:
                                eng.wait_ge(eaT_ps, k * NG + g + 1)
                                nc.vector.tensor_scalar(ea_st[r][:, :], ea6[:, bass.ds(g, 1), :].rearrange("p a c -> p (a c)"),
                                                        1.0, None, ALU.mult).then_inc(ea_ready, 1)
                        if with_chunk:
                            rb, cb = RB[:, bass.ds(i * CB, CB), :], bass.ds(i * CB, CB)
                            n = chunk_no(k, K, i)
                            bbc = bias_bc[:, :].unsqueeze(1).to_broadcast([P, CB, F])
                            eng.wait_ge(nd_mm, n + 2)
                            clink = Chain(eng, c_link, n * 3, 3)
                            if node_scale is None:
                                clink(nc.vector.tensor_tensor(rb, ps45[:, 0:CB, 0:F], bbc, ALU.add))
                            else:
                                clink(nc.vector.tensor_tensor(rb, ps45[:, 0:CB, 0:F], bc(node_scale[:, cb]), ALU.mult))
                            eng.sem_inc(nd_evac, 1)
                            if node_scale is not None:
                                clink(nc.vector.tensor_tensor(rb, rb, bbc, ALU.add))
                            if early:
                                clink(nc.vector.tensor_tensor(rb, rb, X[:, cb, :], ALU.add))
                            eng.sem_inc(c_link, clink.length - clink.n)
                        for r in range(2):
                            g = i * 2 + r
                            add = accumulate(eng, aggT, g, (ps6, ps7)[r][0:F, 0:P])
                            eng.wait_ge(summed, at(k, K, g) + 3)
                            eng.wait_ge(acc_done, at(k, K, g) + 2)
                            add().then_inc(acc_done, 1)
                            if edge_stats:
                                eng.wait_ge(er_stat, k * NG + g + 2)
                                eng.wait_ge(est_done, k * NG + g + 2)
                                nc.vector.tensor_tensor(est[:, :], est[:, :], erst[r][:, :], ALU.add).then_inc(est_done, 1)

                    with eng.Fori(0, K) as k:
                        link = Chain(eng, k_link, (k + K * ph) * 4 + (ph * 4 + 4), 4)
                        start_pass(link)
                        link(nc.vector.memset((est if edge_stats else msq)[:, :], 0.0))
                        eng.sem_inc(dve_gate, 1)
                        with eng.Fori(0, NCH) as i:
                            pair(k, i, True)
                        with eng.Fori(NCH, NG // 2) as i:
                            pair(k, i, False)
                        eng.wait_ge(acc_done, at(k, K, NG) + 2)
                        if edge_stats:
                            eng.wait_ge(est_done, k * NG + NG + 2)
                        end_pass(link)
                        link.done()

                    def first(c, r, base):
                        n = c + ph * NCH
                        link = Chain(eng, nd_link, base, first_n)
                        tt3, cb = ttr[r], bass.ds(c * CB, CB)
                        eng.wait_ge(nd_sum, n + 3)
                        eng.wait_ge(nd_out, n + 1)
                        if scale is not None:
                            link(nc.vector.tensor_tensor(tt3, psA[r][:, 0:CB, 0:F], bc(scale[:, cb]), ALU.mult))
                            link(nc.vector.tensor_tensor(tt3, tt3, RB[:, cb, :], ALU.add))
                        else:
                            link(nc.vector.tensor_tensor(tt3, psA[r][:, 0:CB, 0:F], RB[:, cb, :], ALU.add))
                        eng.sem_inc(nd_read, 1)
                        if relu and residual:
                            link(nc.vector.scalar_tensor_tensor(out=tt3, in0=tt3, scalar=0.0, in1=X[:, cb, :], op0=ALU.max, op1=ALU.add))
                        if residual:
                            ln_first(link, tt3, s1r[r])
                            eng.sem_inc(nd_var, 1)
                        link.done()

                    def second(c, r, base):
                        n = c + ph * NCH
                        tt3, cb = ttr[r], bass.ds(c * CB, CB)
                        if residual:
                            link = Chain(eng, nd_link, base, 1)
                            ln_second(eng, link, lambda j: X[:, bass.ds(c * CB + j, 1), :].rearrange("p a f -> p (a f)"),
                                      tt3, s1r[r], v1r[r], c + root0).then_inc(nd_out, 1)
                        elif node_scale is not None:
                            nc.vector.scalar_tensor_tensor(out=TAB[:, cb, :], in0=tt3, scalar=0.0, in1=bc(dinv[:, cb]),
                                                           op0=ALU.max, op1=ALU.mult).then_inc(nd_out, 1)
                        else:
                            nc.vector.tensor_scalar(TAB[:, cb, :], tt3, 0.0, None, ALU.max).then_inc(nd_out, 1)

                    if residual:
                        first(0, 0, link0)
                        with eng.Fori(0, NCH // 2) as i:
                            for d in range(2):
                                c, r = i * 2 + (1 + d), (1 + d) % 2
                                first(c, r, c * per_chunk + (link0 - 1))
                                second(c - 1, 1 - r, c * per_chunk + (link0 + 2 * first_n - per_chunk))
                        second(NCH - 1, 0, link0 + (NCH - 1) * per_chunk + first_n)
                    else:
                        first(0, 0, link0)
                        second(0, 0, None)
                        with eng.Fori(0, NCH // 2) as i:
                            for d in range(2):
                                c, r = i * 2 + (1 + d), (1 + d) % 2
                                first(c, r, c * per_chunk + link0)
                                second(c, r, None)

                @block.tensor
                def _(eng):
                    K = passes(eng)
                    nc.tensor.matmul(ps45[:, 0, 0:F], ones_row[0:1, :], bias(bias_name), start=True, stop=True).then_inc(nd_bias, 1)
                    if prelude:
                        prelude("tensor", eng)

                    def pair(k, i, with_chunk):
                        if with_chunk:
                            n = chunk_no(k, K, i)
                            eng.wait_ge(nd_staged, n + 1)
                            eng.wait_ge(nd_evac, n + (ph + 1))
                            for j in range(CB):
                                last = nc.tensor.transpose(ps45[0:F, j, :], stN3[:, j, :], ident[:, :])
                            last.then_inc(nd_T, 1)
                            eng.wait_ge(nd_xT, n + 1)
                            for j in range(CB):
                                last = nc.tensor.matmul(ps45[:, j, 0:F], xT[0:F, j * P:(j + 1) * P], mat(W_node), start=True, stop=True)
                            last.then_inc(nd_mm, 1)
                        for r in range(2):
                            g = i * 2 + r
                            if edge_stats:
                                n = k * NG + g
                                eng.wait_ge(ea_ready, n + 1)
                                eng.wait_ge(eaT_sb, n + 1)
                                nc.tensor.transpose(ea_ps2[:, 0, :], ea_st[r][:, 0:KE], identb[:, :])
                                nc.tensor.transpose(ea_ps2[:, 1, :], ea_st[r][:, KE:2 * KE], identb[:, :]).then_inc(eaT_ps, 1)
                                eng.wait_ge(eaT_sb, n + 2)
                                eng.wait_ge(er_stat, n + 1)
                                for u in range(U):
                                    last = nc.tensor.matmul(ps23[0:F, u, :], w6[:, u % UH, :], eaT[r][:, u // UH, :], start=True, stop=True)
                                last.then_inc(er_ps, 1)
                        for r in range(2):
                            g = i * 2 + r
                            eng.wait_ge(oh_ready, at(k, K, g) + 1)
                            eng.wait_ge(acc_done, at(k, K, g) + 1)
                            eng.wait_ge(gathered[r], (k * (NG // 2) + i) * (16 * U) + 16 * U)
                            for u in range(U):
                                last = nc.tensor.matmul((ps6, ps7)[r][0:F, 0:P], rows[r][:, u, :], oh[r][:, u, :],
                                                        start=(u == 0), stop=(u == U - 1))
                            last.then_inc(summed, 1)

                    with eng.Fori(0, K) as k:
                        with eng.Fori(0, NCH) as i:
                            pair(k, i, True)
                        with eng.Fori(NCH, NG // 2) as i:
                            pair(k, i, False)

                    def product(c, r):
                        n = c + ph * NCH
                        eng.wait_ge(nd_agg, n + 1)
                        eng.wait_ge(nd_read, n + 1)
                        for j in range(CB):
                            last = nc.tensor.matmul(psA[r][:, j, 0:F], sumT[r][0:F, j * P:(j + 1) * P], mat(W_agg), start=True, stop=True)
                        last.then_inc(nd_sum, 1)

                    product(0, 0)
                    with eng.Fori(0, NCH // 2) as i:
                        for d in range(2):
                            product(i * 2 + (1 + d), (1 + d) % 2)

                @block.sync
                def _(eng):
                    new = X if residual else TAB
                    if prelude:
                        prelude("sync", eng)
                    with eng.Fori(0, NCH) as c:
                        eng.wait_ge(nd_out, c + (ph * NCH + 3))
                        eng.dma_start(table[bass.ds(c * CW, CW), :].rearrange("(b p) f -> p b f", p=P),
                                      new[:, bass.ds(c * CB, CB), :]).then_inc(nd_dma, 16)
                    eng.wait_ge(nd_dma, 16 * NCH * (ph + 1))

        bn = sb("bn", [F, 24])
        bn_sd, bn_pe, bn_link = sem("bn_sd"), sem("bn_pe"), sem("bn_link")
        BN_LINKS = 9

        def bcol(i):
            return bn[:, i:i + 1]

        def batchnorm(eng, link, total, square, count, gamma, beta, at, n):
            mean, var, tmp, scale, shift = bcol(at + 2), bcol(at + 3), bcol(at + 4), bcol(at), bcol(at + 1)
            link(nc.vector.tensor_scalar(mean, total, 1.0 / count, None, ALU.mult))
            link(nc.vector.tensor_scalar(var, square, 1.0 / count, None, ALU.mult))
            link(nc.vector.tensor_tensor(tmp, mean, mean, ALU.mult))
            link(nc.vector.tensor_tensor(var, var, tmp, ALU.subtract))
            link(nc.vector.tensor_scalar(var, var, 0.0, None, ALU.max))
            eng.sem_inc(bn_var, 1)
            eng.wait_ge(bn_sd, n + 1)
            link(nc.vector.reciprocal(var, var))
            link(nc.vector.tensor_tensor(scale, var, cvec(gamma), ALU.mult))
            link(nc.vector.tensor_tensor(tmp, mean, scale, ALU.mult))
            link(nc.vector.tensor_tensor(shift, cvec(beta), tmp, ALU.subtract))

        def batch_stddev(eng, at, n):
            eng.wait_ge(bn_var, n + 1)
            nc.scalar.activation(bcol(at + 3), bcol(at + 3), ACT.Sqrt, bias=eps_col[0:F, 0:1]).then_inc(bn_sd, 1)

        bn_var = sem("bn_var")


        def edge_constants(engine, eng):
            if engine == "scalar":
                batch_stddev(eng, 0, 0)
            if engine == "tensor":
                eng.wait_ge(bn_link, BN_LINKS + 4)
                nc.tensor.matmul(ps23[0:1, 0, 0:F], bcol(1), mat("Wfeat"), start=True, stop=True).then_inc(bn_pe, 1)
            if engine == "vector":
                link = Chain(eng, bn_link, 0, EDGE_LINKS)
                link(nc.vector.tensor_scalar(bcol(6), cvec("b_edge"), 0.0, None, ALU.max))
                link(nc.vector.tensor_tensor(bcol(7), bcol(6), bcol(6), ALU.mult))
                link(nc.vector.scalar_tensor_tensor(out=est[:, 0:1], in0=bcol(6), scalar=-float(NPAD_E), in1=est[:, 0:1],
                                                    op0=ALU.mult, op1=ALU.add))
                link(nc.vector.scalar_tensor_tensor(out=est[:, 1:2], in0=bcol(7), scalar=-float(NPAD_E), in1=est[:, 1:2],
                                                    op0=ALU.mult, op1=ALU.add))
                batchnorm(eng, link, est[:, 0:1], est[:, 1:2], E, "g_edge", "beta_edge", 0, 0)
                eng.wait_ge(bn_pe, 1)
                link(nc.vector.tensor_tensor(crow[0:1, :], ps23[0:1, 0, 0:F], bias("b_msg"), ALU.add))
                link(nc.vector.tensor_scalar(mat("Wfeat"), mat("Wfeat"), bcol(0), None, ALU.mult))
                link.done()

        EDGE_LINKS = BN_LINKS + 6

        layer(0, TAB, "L0W1", "L0W1", "L0b1", dinv, dinv, True, False, edge_stats=True)
        layer(1, TAB, "L0W2", "L0W2", "L0b2", dinv, dinv, True, True)
        layer(2, X, "L1Wl1T", "L1Wr1T", "L1bl1", rdeg, None, True, False)
        layer(3, TAB, "L1Wl2T", "L1Wr2T", "L1bl2", rdeg, None, False, True)
        layer(4, X, "L2WbT", "L2WaT", "L2b", None, None, False, True, weighted=True, prelude=edge_constants)
        qparts = [t[:, :].bitcast(bf16)[:, 0:CB * 3 * F].rearrange("p (b t f) -> p b t f", t=3, f=F) for t in (big, big3)]
        qst3 = [t[:, :].bitcast(bf16)[:, 0:CB * 3 * F].rearrange("p (b c) -> p b c", c=3 * F) for t in (big, big3)]
        qf = rows[0][:, :, :].rearrange("p u f -> p (u f)")[:, 0:CB * F].rearrange("p (b f) -> p b f", f=F)
        qpad = rows[1][:, :, :].rearrange("p u f -> p (u f)").bitcast(bf16)[:, 0:3 * F]
        nodes = [work[0][:, 0:CB * F].rearrange("p (b f) -> p b f", f=F), work[1][:, 0:CB * F].rearrange("p (b f) -> p b f", f=F)]
        nodesT = [work[2], work[3]]
        p_in, p_T, p_xT, p_mm, p_p, p_q = sem("p_in"), sem("p_T"), sem("p_xT"), sem("p_mm"), sem("p_p"), sem("p_q")
        p_r, p_tab, p_pad, p_crow, p_link = sem("p_r"), sem("p_tab"), sem("p_pad"), sem("p_crow"), sem("p_link")
        p_split, p_qmm, p_pmm = sem("p_split"), sem("p_qmm"), sem("p_pmm")
        m_q = [sem("m_q0"), sem("m_q1")]
        with nc.Block() as block:
            @block.scalar
            def _(eng):
                def load(c, r):
                    eng.wait_ge(p_T, c + 1)
                    eng.sem_inc(act_gate, 1)
                    nc.scalar.activation(nodes[r], X[:, bass.ds(c * CB, CB), :], ACT.Copy).then_inc(p_in, 1)

                def copy_back(c, r):
                    eng.wait_ge(p_T, c + 3)
                    nc.scalar.activation(nodesT[r][0:F, :], ps01[0:F, 0:CB, :].rearrange("p b n -> p (b n)"), ACT.Copy).then_inc(p_xT, 1)

                def source_operands(c):
                    eng.wait_ge(p_pmm, c + 1)
                    eng.sem_inc(act_gate, 1)
                    nc.scalar.activation(TAB[:, bass.ds(c * CB, CB), :], ps23[:, 0:CB, 0:F], ACT.Copy).then_inc(p_p, 1)

                def node_features(c):
                    eng.wait_ge(p_mm, c + 3)
                    eng.sem_inc(act_gate, 1)
                    nc.scalar.activation(rT[:, bass.ds(c * CW, 4 * P)], ps6[0:F, :], ACT.Relu, bias=cvec("b_node"))
                    nc.scalar.activation(rT[:, bass.ds(c * CW + 4 * P, CW - 4 * P)], ps7[0:F, 0:CW - 4 * P], ACT.Relu,
                                         bias=cvec("b_node")).then_inc(p_r, 1)

                def step(c, r, load_next=True):
                    copy_back(c, r)
                    if load_next:
                        load(c + 1, 1 - r)
                    source_operands(c - 1)
                    node_features(c - 1)

                eng.sem_inc(p_p, 1)
                load(0, 0)
                load(1, 1)
                copy_back(0, 0)
                with eng.Fori(0, NCH // 2 - 1) as i:
                    for d in range(2):
                        step(i * 2 + (1 + d), (1 + d) % 2)
                step(NCH - 2, 1)
                step(NCH - 1, 0, load_next=False)
                source_operands(NCH - 1)
                node_features(NCH - 1)

            @block.tensor
            def _(eng):
                eng.sem_inc(p_T, 2)
                eng.sem_inc(p_mm, 2)

                def transposes(c, r):
                    eng.wait_ge(p_in, c + 1)
                    eng.wait_ge(p_xT, c + 1)
                    for j in range(CB):
                        last = nc.tensor.transpose(ps01[0:F, j, :], nodes[r][:, j, :], ident[:, :])
                    last.then_inc(p_T, 1)

                def products(c, r):
                    eng.wait_ge(p_xT, c + 2)
                    eng.wait_ge(p_q, c + 1)
                    for j in range(CB):
                        last = nc.tensor.matmul(ps45[:, j, 0:F], nodesT[r][0:F, j * P:(j + 1) * P], mat("Wdst"), start=True, stop=True)
                    last.then_inc(p_qmm, 1)
                    eng.wait_ge(p_p, c + 1)
                    for j in range(CB):
                        last = nc.tensor.matmul(ps23[:, j, 0:F], nodesT[r][0:F, j * P:(j + 1) * P], mat("Wsrc"), start=True, stop=True)
                    last.then_inc(p_pmm, 1)
                    eng.wait_ge(p_r, c + 1)
                    nc.tensor.matmul(ps6[0:F, :], mat("Wnode"), nodesT[r][0:F, 0:4 * P], start=True, stop=True)
                    nc.tensor.matmul(ps7[0:F, 0:CW - 4 * P], mat("Wnode"), nodesT[r][0:F, 4 * P:CW], start=True, stop=True).then_inc(p_mm, 1)

                nc.tensor.matmul(ps45[:, 0, 0:F], ones_row[0:1, :], crow[0:1, :], start=True, stop=True).then_inc(p_crow, 1)
                eng.sem_inc(p_xT, 1)
                eng.sem_inc(p_r, 1)
                transposes(0, 0)
                with eng.Fori(0, NCH // 2) as i:
                    for d in range(2):
                        c, r = i * 2 + (1 + d), (1 + d) % 2
                        transposes(c, r)
                        products(c - 1, 1 - r)
                products(NCH - 1, 0)

            @block.vector
            def _(eng):
                nc.vector.memset(qpad, 0.0).then_inc(p_pad, 1)
                nc.vector.memset(spare[F:F + 2, :], 1.0).then_inc(p_pad, 1)
                eng.wait_ge(p_crow, 1)
                nc.vector.tensor_copy(bias_bc[:, :], ps45[:, 0, 0:F]).then_inc(p_q, 1)
                eng.wait_ge(p_q, 1)

                def chunk(c, r, stores):
                    hi, mid, lo = (qparts[r][:, :, part, :] for part in range(3))
                    link = Chain(eng, p_link, c * 4, 4)
                    eng.wait_ge(p_qmm, c + 1)
                    link(nc.vector.tensor_tensor(qf, ps45[:, 0:CB, 0:F], bias_bc[:, :].unsqueeze(1).to_broadcast([P, CB, F]), ALU.add))
                    eng.sem_inc(p_q, 1)
                    eng.wait_ge(m_q[r], stores * 16 + 16)
                    link(nc.vector.tensor_copy(hi, qf))
                    link(nc.vector.tensor_tensor(qf, qf, hi, ALU.subtract))
                    link(nc.vector.tensor_copy(mid, qf))
                    link.done()
                    nc.vector.tensor_tensor(lo, qf, mid, ALU.subtract).then_inc(p_split, 1)
                    eng.wait_ge(p_split, c + 1)

                chunk(0, 0, 0)
                with eng.Fori(0, NCH // 2) as i:
                    chunk(i * 2 + 1, 1, i)
                    chunk(i * 2 + 2, 0, i + 1)

            @block.sync
            def _(eng):
                eng.wait_ge(p_pad, 2)
                for r in range(2):
                    eng.dma_start(qtable[NP + r * (P // 2):NP + (r + 1) * (P // 2), :], qpad[r * (P // 2):(r + 1) * (P // 2), :]).then_inc(m_q[r], 16)

                def store(c, r):
                    eng.wait_ge(p_split, c + 1)
                    eng.dma_start(qtable[bass.ds(c * CW, CW), :].rearrange("(b p) f -> p b f", p=P), qst3[r]).then_inc(m_q[r], 16)
                    eng.wait_ge(p_p, c + 2)
                    eng.dma_start(table[bass.ds(c * CW, CW), :].rearrange("(b p) f -> p b f", p=P),
                                  TAB[:, bass.ds(c * CB, CB), :]).then_inc(p_tab, 16)

                store(0, 0)
                with eng.Fori(0, NCH // 2) as i:
                    store(i * 2 + 1, 1)
                    store(i * 2 + 2, 0)
                eng.wait_ge(p_tab, 16 * NCH)
                eng.wait_ge(m_q[0], 16 * (NCH // 2 + 1) + 16)
                eng.wait_ge(m_q[1], 16 * (NCH // 2) + 16)

        PH = 5
        gathered = gathers[PH]
        v_link, sp_gate = sem("v_link"), sem("sp_gate")
        names = "oh ea eaT eaTs ohT ohTs er ers pre hs relu hi sq rem mid lo msq".split()
        q = {name: sem(f"q_{name}") for name in names}
        q_win = [sem("q_win0"), sem("q_win1")]
        q_pass, f_stat, f_deg = sem("q_pass"), sem("f_stat"), sem("f_deg")
        tabf = TAB[:, :, :].rearrange("p b f -> p (b f)")
        UF = U * F
        h32, hrest, hsum = tabf[:, 0:UF], tabf[:, UF:2 * UF], big3[:, 0:UF]
        sqbuf = [work[1 + r][:, 0:UF].rearrange("p (u f) -> p u f", f=F) for r in range(2)]
        hp = [[tabf[:, 2 * UF:5 * UF].bitcast(bf16)[:, (3 * r + n) * UF:(3 * r + n + 1) * UF] for n in range(3)] for r in range(2)]
        ohb = [oh[s % 2][:, :, :].rearrange("p u n -> p (u n)").bitcast(bf16)[:, (s // 2) * GE:(s // 2 + 1) * GE].rearrange("p (u n) -> p u n", n=P)
               for s in range(4)]
        ohT_sb = big2[:, :].bitcast(bf16)[:, 0:GE].rearrange("p (u e) -> p u e", e=P)
        ohT_ps = ps45[:, 0:4, :].rearrange("p b n -> p (b n)").bitcast(bf16).rearrange("p (u e) -> p u e", e=P)
        ea_ps = ps45[0:KE, 4, :].bitcast(bf16).rearrange("p (h e) -> p h e", h=2)
        with nc.Block() as block:
            def flat(ap):
                return ap.rearrange("p u e -> p (u e)")

            @block.gpsimd
            def _(eng):
                K = passes(eng)
                with eng.Fori(0, K) as k:
                    with eng.Fori(0, NG // 2) as i:
                        for r in range(2):
                            eng.wait_ge(idx_staged, (k + K * PH) * NG + i * 2 + r + 1)
                            eng.sem_inc(pool_gate, 1)
                            for u in range(U):
                                eng.indirect_dma_start(
                                    out=rows[r][:, u, :], out_offset=None, in_=table[:, :],
                                    in_offset=bass.IndirectOffsetOnAxis(ap=idx_st[r][:, u:u + 1], axis=0)).then_inc(gathered[r], 16)

            @block.sync
            def _(eng):
                K = passes(eng)
                eng.dma_start(spare[F:F + 1, 0:NP], degrow.rearrange("(a b) p -> a (b p)", a=1)).then_inc(f_deg, 16)
                eng.wait_ge(f_deg, 16)
                with eng.Fori(0, K) as k:
                    eng.wait_ge(q_pass, k + 1)
                    eng.sem_inc(sp_gate, 1)
                    with eng.Fori(0, NG // 2) as i:
                        for r in range(2):
                            g = i * 2 + r
                            at = eng.value_load(basek_i[0:1, bass.ds(g, 1)], min_val=0, max_val=NP)
                            eng.wait_ge(q["pre"], k * NG + g + 1)
                            eng.dma_start(qwin[r][:, :], qtable[bass.ds(at, P), :]).then_inc(q_win[r], 16)

            @block.scalar
            def _(eng):
                K = passes(eng)
                for c in range(NCH):
                    w = min(CW, N - c * CW)
                    nc.scalar.activation(work[1][0:F, 0:w], rT[:, c * CW:c * CW + w], ACT.Square, accum_out=bn[:, 16 + c:17 + c]).then_inc(f_stat, 1)
                    eng.wait_ge(f_stat, c + 1)
                batch_stddev(eng, 8, 1)
                eng.sem_inc(act_gate, 1)
                with eng.Fori(0, K) as k:
                    def wait(name, g):
                        eng.wait_ge(q[name], k * NG + g + 3)

                    def stage(g, r):
                        wait("hs", g - 2)
                        eng.sem_inc(act_gate, 1)
                        nc.scalar.activation(idx_st[r][:, :], idx_all[:, bass.ds(g, 1), :].rearrange("p a u -> p (a u)"),
                                             ACT.Copy).then_inc(idx_staged, 1)

                    def operands(g, r):
                        wait("eaT", g)
                        nc.scalar.activation(eaT[r][:, :, :], ea_ps, ACT.Copy).then_inc(q["eaTs"], 1)

                    def features(g, r):
                        wait("er", g)
                        wait("pre", g - 1)
                        nc.scalar.activation(big[0:F, :], flat(ps01[0:F, :, :]), ACT.Relu, bias=cvec("b_edge")).then_inc(q["ers"], 1)

                    def messages(g, r):
                        wait("hs", g)
                        wait("rem", g - 1)
                        wait("sq", g - 1)
                        wait("hi", g - 1)
                        nc.scalar.activation(h32, hsum, ACT.Relu).then_inc(q["relu"], 1)
                        wait("relu", g)
                        eng.wait_ge(summed, (k + K * PH) * NG + g + 1)
                        nc.scalar.activation(hp[r][0], h32, ACT.Copy).then_inc(q["hi"], 1)
                        nc.scalar.activation(flat(sqbuf[r]), h32, ACT.Square).then_inc(q["sq"], 1)
                        wait("rem", g)
                        nc.scalar.activation(hp[r][1], hrest, ACT.Copy).then_inc(q["mid"], 1)

                    def step(g, d, ahead=2):
                        r = d % 2
                        if ahead == 2:
                            stage(g + 2, r)
                        messages(g, r)
                        if ahead == 2:
                            operands(g + 2, r)
                            features(g + 2, r)

                    for g in range(2):
                        stage(g, g)
                    for g in range(2):
                        operands(g, g)
                        features(g, g)
                    with eng.Fori(0, NG // 4 - 1) as i:
                        for d in range(4):
                            step(i * 4 + d, d)
                    for d in range(4):
                        step(NG - 4 + d, d, min(2, 3 - d))

            @block.vector
            def _(eng):
                K = passes(eng)
                eng.sem_inc(q["ea"], 2)
                for name in names:
                    if name != "ea":
                        eng.sem_inc(q[name], 2)
                link = Chain(eng, k_link, K * (PH * 4) + PH * 4, 3)
                start_phase(link, aggT)
                link.done()
                link = Chain(eng, bn_link, EDGE_LINKS, BN_LINKS + 2)
                link(nc.vector.tensor_reduce(bcol(15), rT[:, 0:N], AX.X, ALU.add))
                eng.wait_ge(f_stat, NCH)
                link(nc.vector.tensor_reduce(bcol(23), bn[:, 16:16 + NCH], AX.X, ALU.add))
                batchnorm(eng, link, bcol(15), bcol(23), N, "g_node", "beta_node", 8, 1)
                link.done()
                with eng.Fori(0, K) as k:
                    link = Chain(eng, k_link, (k + K * PH) * 4 + (PH * 4 + 3), 4)
                    start_pass(link)
                    link(nc.vector.memset(msq[:, :], 0.0))
                    vlink = Chain(eng, v_link, k * 3, 3)
                    vlink(nc.vector.tensor_scalar(flat(w_all[:, :, :]), flat(dstrel[:, :, :]), iotak[:, 0:1], 0.0, ALU.subtract, ALU.is_ge))
                    vlink(nc.vector.tensor_scalar(work[0][:, 0:NG * U], flat(dstrel[:, :, :]), iotak[:, 0:1], float(P), ALU.subtract, ALU.is_lt))
                    vlink(nc.vector.tensor_tensor(flat(w_all[:, :, :]), flat(w_all[:, :, :]), work[0][:, 0:NG * U], ALU.mult))
                    vlink.done()
                    eng.sem_inc(q_pass, 1)

                    def wait(name, g):
                        eng.wait_ge(q[name], k * NG + g + 3)

                    def hots(g, s, free=False):
                        r = s % 2
                        if not free:
                            eng.wait_ge(summed, (k + K * PH) * NG + (g - 1))
                        one_hot(eng, ohb[s], g, iotak).then_inc(q["oh"], 1)
                        nc.vector.tensor_scalar(valid[s][:, :], w_all[:, bass.ds(g, 1), :].rearrange("p a u -> p (a u)"), 1.0, None, ALU.mult)
                        nc.vector.tensor_scalar(ea_st[r][:, :], ea6[:, bass.ds(g, 1), :].rearrange("p a c -> p (a c)"),
                                                1.0, None, ALU.mult).then_inc(q["ea"], 1)

                    def transposed(g, r):
                        wait("ohT", g)
                        wait("pre", g - 1)
                        nc.vector.tensor_copy(flat(ohT_sb), flat(ohT_ps)).then_inc(q["ohTs"], 1)

                    def add_rows(g, r, half):
                        wait("pre", g)
                        wait("relu", g - 1)
                        eng.wait_ge(gathered[r], (k * (NG // 2) + half) * (16 * U) + 16 * U)
                        nc.vector.tensor_tensor(hsum.rearrange("p (u f) -> p u f", f=F), ps23[:, :, 0:F], rows[r][:, :, :], ALU.add).then_inc(q["hs"], 1)

                    def accumulate_sums(g, r):
                        add = accumulate(eng, aggT, g, (ps6, ps7)[r][0:F, 0:P])
                        eng.wait_ge(summed, (k + K * PH) * NG + g + 3)
                        eng.wait_ge(acc_done, (k + K * PH) * NG + g + 2)
                        add().then_inc(acc_done, 1)
                        wait("msq", g - 1)
                        nc.vector.tensor_tensor(msq[:, :], msq[:, :], (ps6, ps7)[r][0:F, P:P + 1], ALU.add).then_inc(q["msq"], 1)

                    def rest(g, r):
                        wait("hi", g)
                        wait("mid", g - 1)
                        wait("lo", g - 1)
                        nc.vector.tensor_tensor(hrest, h32, hp[r][0], ALU.subtract).then_inc(q["rem"], 1)

                    def low(g, r):
                        wait("mid", g)
                        nc.vector.tensor_tensor(hp[r][2], hrest, hp[r][1], ALU.subtract).then_inc(q["lo"], 1)

                    def step(g, d, half, first=False, ahead=2):
                        r = d % 2
                        add_rows(g, r, half)
                        if ahead == 2:
                            hots(g + 2, (d + 2) % 4, free=first and d < 2)
                        rest(g, r)
                        if not (first and d == 0):
                            accumulate_sums(g - 1, 1 - r)
                        low(g, r)
                        if ahead == 2:
                            transposed(g + 2, r)

                    hots(0, 0, free=True)
                    hots(1, 1, free=True)
                    transposed(0, 0)
                    transposed(1, 1)
                    for d in range(4):
                        step(d, d, d // 2, first=True)
                    with eng.Fori(1, NG // 4 - 1) as i:
                        for d in range(4):
                            step(i * 4 + d, d, i * 2 + d // 2)
                    for d in range(4):
                        step(NG - 4 + d, d, NG // 2 - 2 + d // 2, ahead=min(2, 3 - d))
                    accumulate_sums(NG - 1, 1)
                    eng.wait_ge(acc_done, (k + K * PH) * NG + (NG + 2))
                    wait("msq", NG - 1)
                    end_pass(link)
                    link.done()

            @block.tensor
            def _(eng):
                K = passes(eng)
                with eng.Fori(0, K) as k:
                    def wait(name, g):
                        eng.wait_ge(q[name], k * NG + g + 3)

                    def operands(g, s):
                        r = s % 2
                        wait("ea", g)
                        wait("eaTs", g - 1)
                        nc.tensor.transpose(ea_ps[:, 0, :], ea_st[r][:, 0:KE], identb[:, :])
                        nc.tensor.transpose(ea_ps[:, 1, :], ea_st[r][:, KE:2 * KE], identb[:, :]).then_inc(q["eaT"], 1)
                        wait("oh", g)
                        wait("ohTs", g - 1)
                        for u in range(U):
                            last = nc.tensor.transpose(ohT_ps[:, u, :], ohb[s][:, u, :], identb[:, :])
                        last.then_inc(q["ohT"], 1)
                        wait("eaTs", g)
                        wait("ers", g - 1)
                        for u in range(U):
                            last = nc.tensor.matmul(ps01[0:F, u, :], w6[:, u % UH, :], eaT[r][:, u // UH, :], start=True, stop=True)
                        last.then_inc(q["er"], 1)

                    def preact(g, r, half):
                        wait("ers", g)
                        wait("ohTs", g)
                        wait("hs", g - 1)
                        eng.wait_ge(q_win[r], (k * (NG // 2) + half) * 16 + 16)
                        for u in range(U):
                            nc.tensor.matmul(ps23[:, u, 0:F], big[0:F, u * P:(u + 1) * P], mat("Wfeat"), start=True, stop=False)
                            for part in range(3):
                                last = nc.tensor.matmul(ps23[:, u, 0:F], ohT_sb[:, u, :], qwin[r][:, part * F:(part + 1) * F],
                                                        start=False, stop=part == 2)
                        last.then_inc(q["pre"], 1)

                    def sums(g, s):
                        r = s % 2
                        wait("lo", g)
                        wait("sq", g)
                        wait("msq", g - 2)
                        eng.wait_ge(acc_done, (k + K * PH) * NG + g + 1)
                        ps = (ps6, ps7)[r]
                        for u in range(U):
                            for part in range(3):
                                nc.tensor.matmul(ps[0:F, 0:P], hp[r][part][:, u * F:(u + 1) * F], ohb[s][:, u, :],
                                                 start=(u == 0 and part == 0), stop=(u == U - 1 and part == 2))
                        for u in range(U):
                            last = nc.tensor.matmul(ps[0:F, P:P + 1], sqbuf[r][:, u, :], valid[s][:, u:u + 1],
                                                    start=(u == 0), stop=(u == U - 1))
                        last.then_inc(summed, 1)

                    def step(g, d, half, ahead=2):
                        if ahead:
                            preact(g + 1, (d + 1) % 2, half)
                        if ahead == 2:
                            operands(g + 2, (d + 2) % 4)
                        sums(g, d)

                    operands(0, 0)
                    preact(0, 0, 0)
                    operands(1, 1)
                    with eng.Fori(0, NG // 4 - 1) as i:
                        for d in range(4):
                            step(i * 4 + d, d, i * 2 + (d + 1) // 2)
                    for d in range(4):
                        step(NG - 4 + d, d, NG // 2 - 2 + (d + 1) // 2, min(2, 3 - d))

        f_link, f_in, f_T, f_out, f_dma, f_free, f_d = sem("f_link"), sem("f_in"), sem("f_T"), sem("f_out"), sem("f_dma"), sem("f_free"), sem("f_d")
        f_read, f_ext = sem("f_read"), sem("f_ext")
        root0, FIRST, LAST = roots[0], 1 + LN_FIRST, LN_SECOND
        PER = FIRST + LAST
        ot = [big[:, 0:CB * F].rearrange("p (b f) -> p b f", f=F), big2[:, 0:CB * F].rearrange("p (b f) -> p b f", f=F)]
        tabw = TAB[:, :, :].rearrange("p b f -> p (b f)")
        part = [[tabw[0:F + 2 * n, (2 * r + n) * CW:(2 * r + n + 1) * CW] for n in range(2)] for r in range(2)]
        ttf = [work[1][:, 0:CB * F].rearrange("p (b f) -> p b f", f=F), work[2][:, 0:CB * F].rearrange("p (b f) -> p b f", f=F)]
        sums_scale, nodes_scale = work[3][0:F, 0:F], work[3][0:F + 2, F:2 * F]
        scale_cols = work[3][0:F, 2 * F:3 * F + 2]
        with nc.Block() as block:
            @block.scalar
            def _(eng):
                batch_stddev(eng, 0, 2)

                def load(c, r):
                    eng.wait_ge(f_T, c + 1)
                    eng.sem_inc(act_gate, 1)
                    nc.scalar.activation(part[r][0], aggT[:, bass.ds(c * CW, CW)], ACT.Copy)
                    nc.scalar.activation(part[r][1], spare[0:F + 2, bass.ds(c * CW, CW)], ACT.Copy).then_inc(f_in, 1)

                load(0, 0)
                with eng.Fori(0, NCH // 2) as i:
                    for d in range(2):
                        c, r = i * 2 + (1 + d), (1 + d) % 2
                        load(c, r)
                        stddev(eng, ttf[1 - r], s1r[1 - r], v1r[1 - r], c + (root0 - 1))
                stddev(eng, ttf[0], s1r[0], v1r[0], NCH - 1 + root0)

            @block.vector
            def _(eng):
                eng.sem_inc(f_out, 2)
                link = Chain(eng, bn_link, EDGE_LINKS + BN_LINKS + 2, BN_LINKS + 6)
                link(nc.vector.tensor_reduce(bcol(14), aggT[:, 0:N], AX.X, ALU.add))
                batchnorm(eng, link, bcol(14), msq[:, :], E, "g_msg", "beta_msg", 0, 2)
                link(nc.vector.tensor_scalar(scale_cols[:, 0:F], ident[0:F, 0:F], bcol(8), None, ALU.mult))
                link(nc.vector.tensor_copy(scale_cols[:, F:F + 1], bcol(1)))
                link(nc.vector.tensor_copy(scale_cols[:, F + 1:F + 2], bcol(9)))
                eng.sem_inc(f_d, 1)
                link(nc.vector.tensor_scalar(sums_scale, ident[0:F, 0:F], bcol(0), None, ALU.mult))
                eng.wait_ge(f_ext, 1)
                link(nc.vector.tensor_copy(nodes_scale, ps6[0:F + 2, 0:F]))
                link.done()
                eng.sem_inc(f_d, 1)
                eng.sem_inc(f_read, 2)

                def first(c, r, base):
                    link = Chain(eng, f_link, base, FIRST)
                    eng.wait_ge(f_T, c + 3)
                    eng.wait_ge(f_out, c + 1)
                    link(nc.vector.tensor_tensor(ttf[r], psA[r][:, 0:CB, 0:F], X[:, bass.ds(c * CB, CB), :], ALU.add))
                    eng.sem_inc(f_read, 1)
                    ln_first(link, ttf[r], s1r[r])
                    eng.sem_inc(nd_var, 1)
                    link.done()

                def second(c, r, base):
                    link = Chain(eng, f_link, base, LAST)
                    eng.wait_ge(f_free, c + 1)
                    ln_second(eng, link, lambda j: ot[r][:, j, :], ttf[r], s1r[r], v1r[r], c + root0).then_inc(f_out, 1)
                    link.done()

                first(0, 0, 0)
                with eng.Fori(0, NCH // 2) as i:
                    for d in range(2):
                        c, r = i * 2 + (1 + d), (1 + d) % 2
                        first(c, r, c * PER - LAST)
                        second(c - 1, 1 - r, c * PER + (FIRST - LAST))
                second(NCH - 1, 0, (NCH - 1) * PER + FIRST)

            @block.tensor
            def _(eng):
                eng.sem_inc(f_T, 2)
                eng.wait_ge(f_d, 1)
                nc.tensor.transpose(ps6[0:F + 2, 0:F], scale_cols, ident[0:F, 0:F]).then_inc(f_ext, 1)
                eng.wait_ge(f_d, 2)

                def product(c, r):
                    eng.wait_ge(f_in, c + 1)
                    eng.wait_ge(f_read, c + 1)
                    for j in range(CB):
                        a, b = (x[:, j * P:(j + 1) * P] for x in part[r])
                        nc.tensor.matmul(psA[r][:, j, 0:F], a, sums_scale, start=True, stop=False)
                        last = nc.tensor.matmul(psA[r][:, j, 0:F], b, nodes_scale, start=False, stop=True)
                    last.then_inc(f_T, 1)

                product(0, 0)
                with eng.Fori(0, NCH // 2) as i:
                    for d in range(2):
                        product(i * 2 + (1 + d), (1 + d) % 2)

            @block.sync
            def _(eng):
                eng.sem_inc(f_free, 2)

                def store(c, r):
                    eng.wait_ge(f_out, c + 3)
                    eng.dma_start(out[bass.ds(c * CW, CW), :].rearrange("(b p) f -> p b f", p=P), ot[r]).then_inc(f_dma, 16)
                    eng.wait_ge(f_dma, c * 16 + 16)
                    eng.sem_inc(f_free, 1)

                with eng.Fori(0, NCH // 2) as i:
                    for r in range(2):
                        store(i * 2 + r, r)
                eng.wait_ge(f_out, NCH + 2)
                o = (NCH - 1) * CW
                eng.dma_start(out[o:(NB - 1) * P, :].rearrange("(b p) f -> p b f", p=P), ot[0][:, 0:CB - 1, :]).then_inc(f_dma, 16)
                eng.dma_start(out[(NB - 1) * P:N, :], ot[0][0:N - (NB - 1) * P, CB - 1, :]).then_inc(f_dma, 16)
                eng.wait_ge(f_dma, 16 * (NCH + 1))


MATS = ["L0W1", "L0W2", "L1Wl1T", "L1Wr1T", "L1Wl2T", "L1Wr2T", "L2WaT", "L2WbT", "Wnode", "Wsrc", "Wdst", "Wfeat"]
ROWS = ["L0b1", "L0b2", "L1bl1", "L1bl2", "L2b", "b_msg"]
COLS = ["b_edge", "g_edge", "beta_edge", "b_node", "g_node", "beta_node", "g_msg", "beta_msg"]


def kernel(**inputs):
    import numpy as np
    import concourse.bacc as bacc
    from concourse.bass_utils import run_bass_kernel_spmd as run

    a = {k: np.asarray(v) for k, v in inputs.items()}
    N, F = a["x"].shape
    E, FE = a["edge_attr_4"].shape
    W_msg = a["L3_gnn_W_msg"]
    mats = dict(zip(MATS, [
        a["L0_gnn_W1"], a["L0_gnn_W2"], a["L1_gnn_Wl1"].T, a["L1_gnn_Wr1"].T, a["L1_gnn_Wl2"].T, a["L1_gnn_Wr2"].T,
        a["L2_gnn_mlp_w"][:, :F].T, a["L2_gnn_mlp_w"][:, F:].T, a["L3_gnn_W_node"],
        W_msg[:F], W_msg[F:2 * F], W_msg[2 * F:]]))
    rows = {"L0b1": a["L0_gnn_b1"], "L0b2": a["L0_gnn_b2"], "L1bl1": a["L1_gnn_bl1"], "L1bl2": a["L1_gnn_bl2"],
            "L2b": a["L2_gnn_mlp_b"]}
    for part in ("edge", "node", "msg"):
        for kind in ("b", "g", "beta"):
            rows[f"{kind}_{part}"] = a[f"L3_gnn_{kind}_{part}"]

    nc = bacc.Bacc("TRN2", target_bir_lowering=False, num_devices=1)
    arrays = {}

    def given(name, array):
        array = np.ascontiguousarray(array)
        arrays[f"in_{name}"] = array
        return nc.dram_tensor(f"in_{name}", array.shape, mybir.dt.from_np(array.dtype), kind="ExternalInput").ap()

    x, src, dst = given("x", a["x"]), given("src", a["src"]), given("dst", a["dst"])
    ea, ew = given("edge_attr", a["edge_attr_4"]), given("edge_weight", a["edge_weight"])
    mats_dram = {k: given(k, v) for k, v in mats.items()}
    rows_dram = {k: given(k, v) for k, v in rows.items()}
    w_edge = given("w_edge", a["L3_gnn_W_edge"])
    out = nc.dram_tensor("out_x", (N, F), mybir.dt.float32, kind="ExternalOutput").ap()
    build(nc, x, src, dst, ea, ew, mats_dram, rows_dram, ROWS, COLS, w_edge, out, N, E, F, FE)
    return run(nc, [arrays], core_ids=[0]).results[0]["out_x"]
```
